# Optimizing a Trainium2 kernel written in Bass

```python
import numpy as np
import jax
import jax.numpy as jnp

def _softmax(x, axis=-1):
    return jax.nn.softmax(x, axis=axis)

def _gelu(x):
    return jax.nn.gelu(x, approximate=True)

def _silu(x):
    return jax.nn.silu(x)

def _sigmoid(x):
    return jax.nn.sigmoid(x)

def _layernorm(x, axis=-1, eps=1e-05):
    m = jnp.mean(x, axis=axis, keepdims=True)
    v = jnp.var(x, axis=axis, keepdims=True)
    return (x - m) / jnp.sqrt(v + eps)

def _scatter_add(tgt, idx, src, axis=0):
    return tgt.at[idx].add(src)

def _segment_sum(src, seg, n):
    return jax.ops.segment_sum(src, seg, n)
kernel_name = 'mk_prb_d2_jaxref_r4_b96cab'

def setup_inputs(seed: int=0):
    np.random.seed(seed)
    _w = jnp.asarray

    def _L0_attn_setup():
        import jax, jax.numpy as jnp
        import numpy as np
        N_HEAD = 16
        MIN_CTX = 64
        FULL_CTX = 256

        def _pruning_ratio(T):
            if T < MIN_CTX:
                return 1.0
            if T >= FULL_CTX:
                return 0.2
            progress = (T - MIN_CTX) / (FULL_CTX - MIN_CTX)
            return 0.5 - 0.3 * progress
        key = jax.random.key(seed)
        ks = jax.random.split(key, 3)
        B, T, C = (2, 512, 256)
        x = jax.random.normal(ks[0], (B, T, C), jnp.float32)
        w_attn = jax.random.normal(ks[1], (3 * C, C), jnp.float32) * 0.02
        b_attn = jnp.zeros((3 * C,), jnp.float32)
        w_proj = jax.random.normal(ks[2], (C, C), jnp.float32) * 0.02
        b_proj = jnp.zeros((C,), jnp.float32)
        return {'x': x, 'w_attn': w_attn, 'b_attn': b_attn, 'w_proj': w_proj, 'b_proj': b_proj}
    _L0_attn_in = _L0_attn_setup()

    def _L0_ffn_setup():
        import jax, jax.numpy as jnp
        import numpy as np
        E, D, F, GATE_DIM = (8, 256, 1024, 16)
        B, T = (2, 512)
        key = jax.random.key(seed)
        ks = jax.random.split(key, 7)
        s = 0.02
        return {'hidden_states': jax.random.normal(ks[0], (B, T, D), dtype=jnp.float32), 'w_red': jax.random.normal(ks[1], (D, GATE_DIM), dtype=jnp.float32) * s, 'wg': jax.random.normal(ks[2], (E, GATE_DIM), dtype=jnp.float32), 'w1': jax.random.normal(ks[3], (E, D, F), dtype=jnp.float32) * s, 'b1': jax.random.normal(ks[4], (E, F), dtype=jnp.float32) * s, 'w2': jax.random.normal(ks[5], (E, F, D), dtype=jnp.float32) * s, 'b2': jax.random.normal(ks[6], (E, D), dtype=jnp.float32) * s}
    _L0_ffn_in = _L0_ffn_setup()

    def _L1_attn_setup():
        import jax, jax.numpy as jnp
        import numpy as np
        DIM = 256
        HEADS = 8
        DIM_QK = 64
        MAX_POS = 10
        SCALE = DIM_QK ** (-0.5)
        key = jax.random.key(seed)
        ks = jax.random.split(key, 6)
        b, n = (4, 512)
        x = jax.random.normal(ks[0], (b, n, DIM), dtype=jnp.float32)
        mask = jnp.ones((b, n), dtype=bool)
        s = DIM ** (-0.5)
        W_qk = jax.random.normal(ks[1], (DIM, DIM_QK * HEADS * 2), dtype=jnp.float32) * s
        W_v = jax.random.normal(ks[2], (DIM, DIM), dtype=jnp.float32) * s
        W_out = jax.random.normal(ks[3], (DIM, DIM), dtype=jnp.float32) * s
        b_out = jnp.zeros((DIM,), dtype=jnp.float32)
        conv = jax.random.normal(ks[4], (HEADS, 2 * MAX_POS + 1), dtype=jnp.float32) * 0.02
        return {'x': x, 'mask': mask, 'W_qk': W_qk, 'W_v': W_v, 'W_out': W_out, 'b_out': b_out, 'conv': conv}
    _L1_attn_in = _L1_attn_setup()

    def _L1_ffn_setup():
        import jax, jax.numpy as jnp
        import numpy as np
        D_MODEL, D_FF, RANK = (256, 1024, 64)
        B, S = (4, 1024)
        key = jax.random.key(seed)
        ks = jax.random.split(key, 7)
        return {'x': jax.random.normal(ks[0], (B, S, D_MODEL), dtype=jnp.float32), 'U1': jax.random.normal(ks[1], (D_MODEL, RANK), dtype=jnp.float32) * 0.02, 'V1': jax.random.normal(ks[2], (RANK, D_FF), dtype=jnp.float32) * 0.02, 'b1': jnp.zeros((D_FF,), dtype=jnp.float32), 'U2': jax.random.normal(ks[3], (D_FF, RANK), dtype=jnp.float32) * 0.02, 'V2': jax.random.normal(ks[4], (RANK, D_MODEL), dtype=jnp.float32) * 0.02, 'b2': jnp.zeros((D_MODEL,), dtype=jnp.float32)}
    _L1_ffn_in = _L1_ffn_setup()
    _d = {'L0_attn_x': _L0_attn_in['x'], 'L0_attn_w_attn': _L0_attn_in['w_attn'], 'L0_attn_b_attn': _L0_attn_in['b_attn'], 'L0_attn_w_proj': _L0_attn_in['w_proj'], 'L0_attn_b_proj': _L0_attn_in['b_proj'], 'L0_ffn_w_red': _L0_ffn_in['w_red'], 'L0_ffn_wg': _L0_ffn_in['wg'], 'L0_ffn_w1': _L0_ffn_in['w1'], 'L0_ffn_b1': _L0_ffn_in['b1'], 'L0_ffn_w2': _L0_ffn_in['w2'], 'L0_ffn_b2': _L0_ffn_in['b2'], 'L1_attn_mask': _L1_attn_in['mask'], 'L1_attn_W_qk': _L1_attn_in['W_qk'], 'L1_attn_W_v': _L1_attn_in['W_v'], 'L1_attn_W_out': _L1_attn_in['W_out'], 'L1_attn_b_out': _L1_attn_in['b_out'], 'L1_attn_conv': _L1_attn_in['conv'], 'L1_ffn_U1': _L1_ffn_in['U1'], 'L1_ffn_V1': _L1_ffn_in['V1'], 'L1_ffn_b1': _L1_ffn_in['b1'], 'L1_ffn_U2': _L1_ffn_in['U2'], 'L1_ffn_V2': _L1_ffn_in['V2'], 'L1_ffn_b2': _L1_ffn_in['b2']}
    _x0 = _d['L0_attn_x']
    _d['L0_attn_x'] = jax.random.normal(jax.random.fold_in(jax.random.key(seed), 1), (2, 2048, 256), dtype=_x0.dtype)
    del _x0
    return _d

def reference(L0_attn_x, L0_attn_w_attn, L0_attn_b_attn, L0_attn_w_proj, L0_attn_b_proj, L0_ffn_w_red, L0_ffn_wg, L0_ffn_w1, L0_ffn_b1, L0_ffn_w2, L0_ffn_b2, L1_attn_mask, L1_attn_W_qk, L1_attn_W_v, L1_attn_W_out, L1_attn_b_out, L1_attn_conv, L1_ffn_U1, L1_ffn_V1, L1_ffn_b1, L1_ffn_U2, L1_ffn_V2, L1_ffn_b2):

    def _L0_attn_ref(x, w_attn, b_attn, w_proj, b_proj):
        import jax, jax.numpy as jnp
        import numpy as np
        N_HEAD = 16
        MIN_CTX = 64
        FULL_CTX = 256

        def _pruning_ratio(T):
            if T < MIN_CTX:
                return 1.0
            if T >= FULL_CTX:
                return 0.2
            progress = (T - MIN_CTX) / (FULL_CTX - MIN_CTX)
            return 0.5 - 0.3 * progress
        B, T, C = x.shape
        nh = N_HEAD
        hd = C // nh
        neg_inf = jnp.float32(-jnp.inf)
        qkv = x @ w_attn.T + b_attn
        q, k, v = jnp.split(qkv, 3, axis=2)
        to_heads = lambda t: t.reshape(B, T, nh, hd).transpose(0, 2, 1, 3)
        q, k, v = (to_heads(q), to_heads(k), to_heads(v))
        att = jnp.einsum('bhid,bhjd->bhij', q, k) / jnp.sqrt(jnp.float32(hd))
        i = jnp.arange(T)
        causal = i[None, :] <= i[:, None]
        att = jnp.where(causal[None, None], att, neg_inf)
        S = jax.nn.relu(att[:, 0])
        S = S.at[..., 0].set(0.0)
        S = S * (1.0 - jnp.eye(T, dtype=S.dtype))
        S_shifted = jnp.concatenate([jnp.zeros((B, 1, T), S.dtype), S[:, :-1]], axis=1)
        FF = jnp.cumsum(S_shifted, axis=1)
        att = att - FF[:, None]
        ratio = _pruning_ratio(T)
        memory_budget = max(1, int(T * ratio))
        if ratio < 1.0:
            FF_mod = jnp.where(causal[None], FF, jnp.inf)
            sorted_idx = jnp.argsort(FF_mod, axis=-1)
            rank = jnp.argsort(sorted_idx, axis=-1)
            eff_k = jnp.minimum(memory_budget - 1, i + 1)
            keep = rank < eff_k[None, :, None]
            keep = keep | jnp.eye(T, dtype=bool)[None]
            att = jnp.where(keep[:, None], att, neg_inf)
        y = jax.nn.softmax(att, axis=-1) @ v
        y = y.transpose(0, 2, 1, 3).reshape(B, T, C)
        return y @ w_proj.T + b_proj

    def _L0_ffn_ref(hidden_states, w_red, wg, w1, b1, w2, b2):
        import jax, jax.numpy as jnp
        import numpy as np
        E, D, F, GATE_DIM = (8, 256, 1024, 16)
        B, T = (2, 512)
        b, t, c = hidden_states.shape
        x = hidden_states.reshape(-1, c)
        red = x @ w_red
        wg_n = wg / jnp.maximum(jnp.linalg.norm(wg, axis=1, keepdims=True), 0.0001)
        logits = red @ wg_n.T
        gates = jax.nn.softmax(logits, axis=1)
        idx = jnp.argmax(gates, axis=1)
        scores = jnp.take_along_axis(gates, idx[:, None], axis=1)
        h = jax.nn.gelu(jnp.einsum('td,edf->etf', x, w1) + b1[:, None, :], approximate=False)
        y = jnp.einsum('etf,efd->etd', h, w2) + b2[:, None, :]
        out = jnp.take_along_axis(y, idx[None, :, None], axis=0)[0]
        out = out * scores
        return out.reshape(b, t, c)

    def _L1_attn_ref(x, mask, W_qk, W_v, W_out, b_out, conv):
        import jax, jax.numpy as jnp
        import numpy as np
        DIM = 256
        HEADS = 8
        DIM_QK = 64
        MAX_POS = 10
        SCALE = DIM_QK ** (-0.5)
        b, n, _ = x.shape
        h, dqk = (HEADS, DIM_QK)
        dv = DIM // h
        qk = x @ W_qk
        q, k = jnp.split(qk, 2, axis=-1)
        v = x @ W_v
        q = q.reshape(b, n, h, dqk).transpose(0, 2, 1, 3)
        k = k.reshape(b, n, h, dqk).transpose(0, 2, 1, 3)
        v = v.reshape(b, n, h, dv).transpose(0, 2, 1, 3)
        dots = jnp.einsum('bhid,bhjd->bhij', q, k) * SCALE
        seq = jnp.arange(n)
        dist = jnp.clip(seq[None, :] - seq[:, None], -MAX_POS, MAX_POS) + MAX_POS
        bias = conv[:, dist]
        attn = jax.nn.softmax(dots + bias[None], axis=-1)
        out = jnp.einsum('bhij,bhjd->bhid', attn, v)
        out = out.transpose(0, 2, 1, 3).reshape(b, n, h * dv)
        return out @ W_out + b_out

    def _L1_ffn_ref(x, U1, V1, b1, U2, V2, b2):
        import jax, jax.numpy as jnp
        import numpy as np
        D_MODEL, D_FF, RANK = (256, 1024, 64)
        B, S = (4, 1024)
        P = jnp.einsum('bsd,dr->bsr', x, U1)
        H = jax.nn.gelu(jnp.einsum('bsr,rf->bsf', P, V1) + b1)
        Q = jnp.einsum('bsf,fr->bsr', H, U2)
        return jnp.einsum('bsr,rd->bsd', Q, V2) + b2
    x = L0_attn_x
    xn = _layernorm(x, axis=-1)
    x = x + _L0_attn_ref(xn, L0_attn_w_attn, L0_attn_b_attn, L0_attn_w_proj, L0_attn_b_proj) + _L0_ffn_ref(xn, L0_ffn_w_red, L0_ffn_wg, L0_ffn_w1, L0_ffn_b1, L0_ffn_w2, L0_ffn_b2)
    xn = _layernorm(x, axis=-1)
    x = x + _L1_attn_ref(xn, L1_attn_mask, L1_attn_W_qk, L1_attn_W_v, L1_attn_W_out, L1_attn_b_out, L1_attn_conv) + _L1_ffn_ref(xn, L1_ffn_U1, L1_ffn_V1, L1_ffn_b1, L1_ffn_U2, L1_ffn_V2, L1_ffn_b2)
    return x

_drawn_inputs = setup_inputs


def setup_inputs(seed=0):
    import zlib

    import numpy as np

    out = dict(_drawn_inputs(seed))
    spreads = {'L0_attn_b_attn': (0.0, 0.1),
     'L0_attn_b_proj': (0.0, 0.1),
     'L1_attn_b_out': (0.0, 2.0),
     'L1_ffn_b1': (0.0, 0.8),
     'L1_ffn_b2': (0.0, 2.0)}
    factors = {'L0_attn_w_attn': 3.175,
     'L0_ffn_w_red': 2.864,
     'L0_ffn_wg': 2.852,
     'L0_ffn_w1': 2.807,
     'L0_ffn_b1': 8.0,
     'L0_ffn_w2': 2.722,
     'L0_ffn_b2': 8.0,
     'L1_attn_conv': 64.0,
     'L1_ffn_U1': 8.0,
     'L1_ffn_V1': 8.0,
     'L1_ffn_U2': 8.0,
     'L1_ffn_V2': 8.0,
     'L1_attn_W_qk': 8.0,
     'L1_attn_W_v': 5.926,
     'L1_attn_W_out': 6.277}
    for name, (base, spread) in spreads.items():
        noise = np.random.default_rng([zlib.crc32(name.encode()), seed]).standard_normal(out[name].shape)
        drawn = base * np.exp(spread * noise) if base else spread * noise
        out[name] = jnp.asarray(drawn.astype(out[name].dtype))
    for name, factor in factors.items():
        out[name] = (out[name] * factor).astype(out[name].dtype)
    return out
```

```python
from contextlib import ExitStack

import concourse.bass as bass
from concourse import mybir

F32 = mybir.dt.float32
BF16 = mybir.dt.bfloat16
I32 = mybir.dt.int32
ALU = mybir.AluOpType
ACT = mybir.ActivationFunctionType
AX = mybir.AxisListType

P = 128
CHUNK = 512
EPS = 1e-5
BIG = 1e30


def hold(engine, c):
    engine.sem_inc(c.passed, 1)


def build_constants(nc, c):
    with nc.semaphore("const_filled") as filled, nc.semaphore("const_made") as made, nc.Block() as block:
        @block.gpsimd
        def _(pool):
            pool.memset(c.ident[:], 0.0).then_inc(filled, 1)
            pool.memset(c.before[:], 1.0).then_inc(filled, 1)
            pool.memset(c.ones[:], 1.0).then_inc(filled, 1)
            pool.wait_ge(filled, 3)
            pool.affine_select(out=c.ident[:], in_=c.ident[:], compare_op=ALU.not_equal, fill=1.0,
                               base=0, pattern=[[-1, P]], channel_multiplier=1).then_inc(made, 1)
            pool.affine_select(out=c.before[:], in_=c.before[:], compare_op=ALU.is_gt, fill=0.0,
                               base=0, pattern=[[1, P]], channel_multiplier=-1).then_inc(made, 1)
            pool.wait_ge(made, 2)
            pool.tensor_copy(c.ident_bf[:], c.ident[:]).then_inc(made, 1)


def layernorm_transpose(nc, c, layer, X, XT):
    with ExitStack() as ctx:
        sb = lambda n, s, d=F32: ctx.enter_context(nc.sbuf_tensor(f"{layer}_{n}", s, d))
        sem = lambda n: c.sem(f"{layer}_{n}")
        stats = sb("ln_stats", [P, 2, 4, 6])
        meanvar = sb("ln_meanvar", [P, 2, 4, 2])
        std = sb("ln_std", [P, 2, 4])
        rstd = sb("ln_rstd", [P, 2, 4])
        newton = sb("ln_newton", [P, 2, 4])
        eps = sb("ln_eps", [P, 1])
        xn = sb("ln_xn", [P, 2, 4, 256])
        xt = sb("ln_xt", [P, 2, 2, CHUNK])
        xt_ps = ctx.enter_context(nc.psum_tensor(f"{layer}_ln_xt_ps", [P, 2, 2, CHUNK], F32))
        eps_set, stats_done, aggr_done, std_done = sem("eps_set"), sem("stats_done"), sem("aggr_done"), sem("std_done")
        rstd_done, xn_ready, xt_ready, xt_copied, xt_stored = (
            sem("rstd_done"), sem("xn_ready"), sem("xt_ready"), sem("xt_copied"), [sem(f"xt_stored{u}") for u in range(2)])
        block = ctx.enter_context(nc.Block())

        @block.vector
        def _(dve):
            dve.memset(eps[:], EPS).then_inc(eps_set, 1)
            with dve.Fori(0, 4) as it:
                for u in range(2):
                    g = it * 2 + u
                    for t in range(4):
                        last = dve.bn_stats(stats[:, u, t, :], X[:, bass.ds(g * 4 + t, 1), :])
                    last.then_inc(stats_done, 1)
                    dve.wait_ge(stats_done, g + 1)
                    hold(dve, c)
                    for t in range(4):
                        last = dve.bn_aggr(meanvar[:, u, t, :], stats[:, u, t, :])
                    last.then_inc(aggr_done, 1)
                    dve.wait_ge(std_done, g + 1)
                    dve.reciprocal(rstd[:, u, :], std[:, u, :]).then_inc(rstd_done, 1)
                    dve.wait_ge(rstd_done, g * 5 + 1)
                    dve.scalar_tensor_tensor(newton[:, u, :], meanvar[:, u, :, 1], EPS, rstd[:, u, :],
                                             ALU.add, ALU.mult).then_inc(rstd_done, 1)
                    dve.wait_ge(rstd_done, g * 5 + 2)
                    dve.tensor_tensor(newton[:, u, :], newton[:, u, :], rstd[:, u, :], ALU.mult).then_inc(rstd_done, 1)
                    dve.wait_ge(rstd_done, g * 5 + 3)
                    dve.tensor_scalar(newton[:, u, :], newton[:, u, :], -0.5, 1.5, ALU.mult, ALU.add).then_inc(rstd_done, 1)
                    dve.wait_ge(rstd_done, g * 5 + 4)
                    dve.tensor_tensor(rstd[:, u, :], newton[:, u, :], rstd[:, u, :], ALU.mult).then_inc(rstd_done, 1)
                    dve.wait_ge(rstd_done, g * 5 + 5)
                    dve.wait_ge(xt_ready, g + 1)
                    for t in range(4):
                        last = dve.tensor_scalar(xn[:, u, t, :], X[:, bass.ds(g * 4 + t, 1), :],
                                                 meanvar[:, u, t, 0:1], rstd[:, u, t:t + 1],
                                                 ALU.subtract, ALU.mult)
                    last.then_inc(xn_ready, 1)

        @block.scalar
        def _(act):
            act.wait_ge(eps_set, 1)
            with act.Fori(0, 4) as it:
                for u in range(2):
                    g = it * 2 + u
                    act.wait_ge(aggr_done, g + 1)
                    act.activation(std[:, u, :], meanvar[:, u, :, 1], ACT.Sqrt, bias=eps[:, 0:1]).then_inc(std_done, 1)
                    act.wait_ge(xt_ready, g + 3)
                    act.wait_ge(xt_stored[u], it * 16 + 16)
                    act.activation(xt[:, u, :, :], xt_ps[:, u, :, :], ACT.Copy).then_inc(xt_copied, 1)

        @block.sync
        def _(sp):
            for u in range(2):
                sp.sem_inc(xt_stored[u], 16)
            with sp.Fori(0, 4) as it:
                for u in range(2):
                    g = it * 2 + u
                    sp.wait_ge(xt_copied, g + 1)
                    sp.dma_start(XT[bass.ds(g, 1), :, :, :].rearrange("a p h t -> (a p) h t"), xt[:, u, :, :]).then_inc(xt_stored[u], 16)
            for u in range(2):
                sp.wait_ge(xt_stored[u], 5 * 16)

        @block.tensor
        def _(pe):
            pe.sem_inc(xt_ready, 2)
            with pe.Fori(0, 4) as it:
                for u in range(2):
                    g = it * 2 + u
                    pe.wait_ge(xn_ready, g + 1)
                    for half in range(2):
                        for t in range(4):
                            last = pe.transpose(xt_ps[:, u, half, t * P:(t + 1) * P],
                                                xn[:, u, t, half * P:(half + 1) * P], c.ident[:])
                    last.then_inc(xt_ready, 1)


def split3(dve, steps, n, full, high, mid, low, rest):
    dve.tensor_copy(high, full).then_inc(steps, 1)
    dve.wait_ge(steps, n + 1)
    dve.tensor_tensor(rest, full, high, ALU.subtract).then_inc(steps, 1)
    dve.wait_ge(steps, n + 2)
    dve.tensor_copy(mid, rest).then_inc(steps, 1)
    dve.wait_ge(steps, n + 3)
    dve.tensor_tensor(low, rest, mid, ALU.subtract).then_inc(steps, 1)


def project_qkv0(nc, c, XT, w_attn, b_attn, QS0, KS0, V0):
    NH, HD = 16, 16
    C = NH * HD
    SCALE = HD ** -0.5
    with ExitStack() as ctx:
        sb = lambda n, s, d=F32: ctx.enter_context(nc.sbuf_tensor(n, s, d))
        sem = c.sem
        w_rows = sb("p0_w_rows", [P, 6, C])
        wT = sb("p0_wT", [P, 2, 3 * C])
        bias = sb("p0_bias", [P, 4])
        bias_v = sb("p0_bias_v", [P, C])
        xt = sb("p0_xt", [P, 2, 2, CHUNK])
        full = sb("p0_full", [P, 4, CHUNK])
        high = sb("p0_high", [P, 4, CHUNK], BF16)
        mid = sb("p0_mid", [P, 4, CHUNK], BF16)
        low = sb("p0_low", [P, 4, CHUNK], BF16)
        rest = sb("p0_rest", [P, CHUNK])
        v_sb = sb("p0_v", [P, 2, 4, NH, 32])
        proj_ps = ctx.enter_context(nc.psum_tensor("p0_proj", [P, 4, CHUNK], F32))
        v_ps = ctx.enter_context(nc.psum_tensor("p0_v_ps", [P, 4, CHUNK], F32))
        w_loaded, wT_ready, wT_copied, bias_ready = sem("w_loaded"), sem("wT_ready"), sem("wT_copied"), sem("bias_ready")
        xt_loaded = [sem(f"xt_loaded{u}") for u in range(2)]
        proj_ready, full_ready, steps = sem("proj_ready"), sem("full_ready"), sem("split_steps")
        split_stored = [sem(f"split_stored{m}") for m in range(4)]
        v_ready, v_copied, ones_set = sem("v_ready"), sem("v_copied"), sem("ones_set")
        v_stored = [sem(f"v_stored{u}") for u in range(2)]
        block = ctx.enter_context(nc.Block())

        @block.sync
        def _(sp):
            sp.dma_start(w_rows[:], w_attn.rearrange("(n p) d -> p n d", p=P)).then_inc(w_loaded, 16)
            sp.dma_start(bias[:], b_attn[0:2 * C].rearrange("(n p) -> p n", p=P),
                         allow_slow_non_contiguous=True).then_inc(w_loaded, 16)
            sp.dma_start(bias_v[:], b_attn[2 * C:3 * C].rearrange("(a n) -> a n", a=1).broadcast_to([P, C])).then_inc(w_loaded, 16)
            with sp.Fori(0, 4) as it:
                for u in range(2):
                    ch = it * 2 + u
                    b, t0 = ch // 4, (ch % 4) * CHUNK
                    for m in range(4):
                        sp.wait_ge(steps, ch * 16 + m * 4 + 4 + 1)
                        dst = QS0 if m < 2 else KS0
                        order = (high, high, high, mid, mid, low) if m < 2 else (high, mid, low, high, mid, high)
                        for term, part in enumerate(order):
                            sp.dma_start(dst[bass.ds(b * NH + 8 * (m % 2), 8), term * HD:(term + 1) * HD, bass.ds(t0, CHUNK)],
                                           part[:, m, :]).then_inc(split_stored[m], 16)
                    sp.wait_ge(v_copied, ch * 4 + 4 + 1)
                    sp.dma_start(V0[bass.ds(b, 1), :, bass.ds((ch % 4) * 4, 4), :, :].rearrange("a p j h e -> (a p) j h e"),
                                   v_sb[:, u]).then_inc(v_stored[u], 16)
            for m in range(4):
                sp.wait_ge(split_stored[m], (8 + 1) * 6 * 16)
            for u in range(2):
                sp.wait_ge(v_stored[u], (4 + 1) * 16)

        @block.gpsimd
        def _(pool):
            pool.memset(v_sb[:], 1.0).then_inc(ones_set, 1)
            with pool.Fori(0, 4) as it:
                for u in range(2):
                    ch = it * 2 + u
                    pool.wait_ge(v_ready, ch * 4 + 4)
                    pool.dma_start(xt[:, u, :, :], XT[bass.ds(ch, 1), :, :, :].rearrange("a p h t -> (a p) h t")).then_inc(xt_loaded[u], 16)

        @block.scalar
        def _(act):
            act.sem_inc(full_ready, 1)
            act.wait_ge(w_loaded, 48)
            for n in range(6):
                act.wait_ge(wT_ready, n + 1)
                act.activation(wT[:, :, n * P:(n + 1) * P], v_ps[:, n % 4, 0:2 * P].rearrange("p (h o) -> p h o", h=2),
                               ACT.Copy).then_inc(wT_copied, 1)
            act.activation(bias[:, 0:2], bias[:, 0:2], ACT.Copy, scale=SCALE).then_inc(bias_ready, 1)
            act.wait_ge(bias_ready, 1)
            with act.Fori(0, 8) as ch:
                for m in range(4):
                    act.wait_ge(proj_ready, ch * 4 + m + 1)
                    act.wait_ge(steps, ch * 16 + 1)
                    act.activation(full[:, m, :], proj_ps[:, m, :], ACT.Identity,
                                   bias=bias[:, m:m + 1], scale=SCALE if m < 2 else 1.0).then_inc(full_ready, 1)

        @block.vector
        def _(dve):
            dve.sem_inc(steps, 1)
            dve.sem_inc(v_copied, 1)
            dve.wait_ge(ones_set, 1)
            for m in range(4):
                dve.sem_inc(split_stored[m], 6 * 16)
            for u in range(2):
                dve.sem_inc(v_stored[u], 16)
            with dve.Fori(0, 4) as it:
                for u in range(2):
                    ch = it * 2 + u
                    for m in range(4):
                        dve.wait_ge(full_ready, ch * 4 + m + 1 + 1)
                        dve.wait_ge(split_stored[m], (ch + 1) * 6 * 16)
                        split3(dve, steps, 1 + ch * 16 + m * 4, full[:, m, :], high[:, m, :], mid[:, m, :], low[:, m, :], rest[:])
                    dve.wait_ge(v_stored[u], (it + 1) * 16)
                    for t in range(4):
                        dve.wait_ge(v_ready, 8 + ch * 4 + t + 1)
                        dve.tensor_tensor(v_sb[:, u, t, :, 0:HD], v_ps[:, t, 0:C].rearrange("p (h e) -> p h e", h=NH),
                                          bias_v[:].rearrange("p (h e) -> p h e", h=NH), ALU.add).then_inc(v_copied, 1)

        @block.tensor
        def _(pe):
            pe.wait_ge(w_loaded, 48)
            for n in range(6):
                if n >= 4:
                    pe.wait_ge(wT_copied, n - 3)
                for half in range(2):
                    last = pe.transpose(v_ps[:, n % 4, half * P:(half + 1) * P], w_rows[:, n, half * P:(half + 1) * P], c.ident[:])
                last.then_inc(wT_ready, 1)
            pe.wait_ge(wT_copied, 6)
            pe.sem_inc(v_ready, 8)
            with pe.Fori(0, 4) as it:
                for u in range(2):
                    ch = it * 2 + u
                    pe.wait_ge(xt_loaded[u], it * 16 + 16)
                    pe.wait_ge(full_ready, ch * 4 + 1)
                    for m in range(4):
                        for half in range(2):
                            last = pe.matmul(proj_ps[:, m, :], wT[:, half, m * P:(m + 1) * P], xt[:, u, half, :],
                                             start=(half == 0), stop=(half == 1))
                        last.then_inc(proj_ready, 1)
                    pe.wait_ge(v_copied, ch * 4 + 1)
                    for t in range(4):
                        for half in range(2):
                            last = pe.matmul(v_ps[:, t, 0:C], xt[:, u, half, t * P:(t + 1) * P],
                                             wT[:, half, 2 * C:3 * C], start=(half == 0), stop=(half == 1))
                        last.then_inc(v_ready, 1)


def selective_attention(nc, c, QS0, KS0, V0, Y0):
    NB, T, NH, HD = 2, 2048, 16, 16
    ROWS = 6 * HD
    KR = ROWS + 3
    BUDGET = int(T * 0.2) - 1
    NG, GH = 4, 4
    tri = lambda k: k * (k + 1) // 2
    groups = lambda b, q4, g: b * 16 + q4 * 4 + g
    max_chunks = lambda b, q4, g: b * 640 + 64 * tri(q4) + g * (16 * (q4 + 1))
    key_steps = lambda b, q4, g: b * 160 + 16 * tri(q4) + g * (4 * (q4 + 1))
    ff_chunks = lambda b, q4, t: b * 40 + 4 * tri(q4) + t * (q4 + 1)
    blocks = lambda b, q4: b * 4 + q4

    with ExitStack() as ctx:
        sb = lambda n, s, d=F32: ctx.enter_context(nc.sbuf_tensor(n, s, d))
        sem = c.sem
        ps = lambda n, s: ctx.enter_context(nc.psum_tensor(n, s, F32))
        q0 = sb("a0_q0", [ROWS, 1, CHUNK], BF16)
        k0 = sb("a0_k0", [ROWS, 1, T], BF16)
        S = sb("a0_S", [P, T])
        carry = sb("a0_carry", [P, T])
        FF = sb("a0_FF", [P, 4, T])
        FFT = sb("a0_FFT", [P, T // P, CHUNK])
        thr = sb("a0_thr", [P, 4], I32)
        cand = sb("a0_cand", [P, 4], I32)
        bit = sb("a0_bit", [P, 4], I32)
        below = sb("a0_below", [P, 4])
        take = sb("a0_take", [P, 4], I32)
        need = sb("a0_need", [P, 4])
        less = sb("a0_less", [P, T], BF16)
        equal = sb("a0_equal", [P, T], BF16)
        kg = sb("a0_kg", [P, 2, GH, T], BF16)
        qg = sb("a0_qg", [P, 2, GH, CHUNK], BF16)
        vg = sb("a0_vg", [P, 2, T // P, GH, 2 * HD])
        part_max = sb("a0_part_max", [P, GH * 4, 4])
        neg_max = sb("a0_neg_max", [P, GH * 4])
        nm_rest = sb("a0_nm_rest", [P, GH * 4])
        nm_parts = sb("a0_nm_parts", [P, GH * 4, 3], BF16)
        trash = sb("a0_trash", [P, 2, CHUNK])
        probs = sb("a0_probs", [P, 2, GH, CHUNK])
        oT = sb("a0_oT", [P, CHUNK])
        recip = sb("a0_recip", [P, 4, GH])
        y = sb("a0_y", [P, 4, GH, HD])
        max_ps = ps("a0_max_ps", [P, 2, CHUNK])
        t_ps = ps("a0_t_ps", [P, 4, CHUNK])
        pv_ps = ps("a0_pv_ps", [P, CHUNK])
        tr_ps = ps("a0_tr_ps", [P, CHUNK])

        head0_loaded = sem("head0_loaded")
        s_raw, s_pos, s_masked = sem("s_raw"), sem("s_pos"), sem("s_masked")
        sums_ready, ff_done, ff_masked, chain = sem("sums_ready"), sem("ff_done"), sem("ff_masked"), sem("chain")
        kept, ff_final, fft_ready, fft_done = sem("kept"), sem("ff_final"), sem("fft_ready"), sem("fft_done")
        ones_set = sem("ones_set")
        g_loaded = [sem(f"g_loaded{u}") for u in range(2)]
        max_ready, max_done, nm_steps, nm_ready, rows_ready, rows_done = (
            sem("max_ready"), sem("max_done"), sem("nm_steps"), sem("nm_ready"), sem("rows_ready"), sem("rows_done"))
        t_ready, t_added, exp_done, pv_done = sem("t_ready"), sem("t_added"), sem("exp_done"), sem("pv_done")
        o_copied, o_turned, y_steps, y_stored, y_free = sem("o_copied"), sem("o_turned"), sem("y_steps"), sem("y_stored"), sem("y_free")
        NBIT = 31
        first_tile = lambda q4: 3 if q4 == 0 else 0
        block_steps = lambda q4: 2 + NBIT * (7 - first_tile(q4)) + 7 * (4 - first_tile(q4))
        sel_steps = lambda b, q4: b * sum(map(block_steps, range(4))) + sum(map(block_steps, range(q4)))
        block = ctx.enter_context(nc.Block())

        @block.gpsimd
        def _(pool):
            pool.sem_inc(y_free, 1)
            with pool.Fori(0, NB) as b:
                for q4 in range(4):
                    for t in range(4):
                        d0 = (4 * q4 + t) * P
                        n = ff_chunks(b, q4, t)
                        pool.wait_ge(s_pos, n + q4 + 1)
                        hold(pool, c)
                        pool.affine_select(out=S[:, d0:d0 + P], in_=S[:, d0:d0 + P], compare_op=ALU.is_gt, fill=0.0,
                                           base=0, pattern=[[-1, P]], channel_multiplier=1).then_inc(s_masked, 1)
                        pool.wait_ge(s_masked, (blocks(b, q4) * 4 + t) * 2 + 1)
                        hold(pool, c)
                        pool.memset(S[:, 0:1], 0.0).then_inc(s_masked, 1)
                        pool.wait_ge(ff_done, n + q4 + 1)
                        hold(pool, c)
                        pool.affine_select(out=FF[:, t, d0:d0 + P], in_=FF[:, t, d0:d0 + P], compare_op=ALU.is_ge, fill=BIG,
                                           base=0, pattern=[[-1, P]], channel_multiplier=1).then_inc(ff_masked, 1)
                    for t in range(4):
                        d0 = (4 * q4 + t) * P
                        pool.wait_ge(kept, blocks(b, q4) + 1)
                        hold(pool, c)
                        pool.affine_select(out=FF[:, t, d0:d0 + P], in_=FF[:, t, d0:d0 + P], compare_op=ALU.not_equal, fill=0.0,
                                           base=0, pattern=[[-1, P]], channel_multiplier=1).then_inc(ff_final, 1)
                    with pool.Fori(0, NG) as g:
                        pool.wait_ge(y_steps, groups(b, q4, g) * 2 + 2 + 1)
                        pool.dma_start(Y0[bass.ds(b, 1), q4 * CHUNK:(q4 + 1) * CHUNK, bass.ds(g * GH * HD, GH * HD)].rearrange("a (t p) f -> (a p) t f", p=P),
                                       y[:].rearrange("p t h e -> p t (h e)")).then_inc(y_stored, 16)
                        pool.wait_ge(y_stored, (groups(b, q4, g) + 1) * 16)
                        pool.sem_inc(y_free, 1)
            pool.wait_ge(y_stored, NB * 16 * 16)

        @block.sync
        def _(sp):
            with sp.Fori(0, NB) as b:
                for q4 in range(4):
                    W = CHUNK * (q4 + 1)
                    sp.wait_ge(s_raw, ff_chunks(b, q4, 0) + 1)
                    sp.dma_start(q0[:, 0, :], QS0[bass.ds(b * NH, 1), :, q4 * CHUNK:(q4 + 1) * CHUNK].rearrange("a r t -> (a r) t")).then_inc(head0_loaded, 16)
                    sp.dma_start(k0[:, 0, 0:W], KS0[bass.ds(b * NH, 1), :, 0:W].rearrange("a r t -> (a r) t")).then_inc(head0_loaded, 16)
                    with sp.Fori(0, NG // 2) as g2:
                        for u in range(2):
                            g = g2 * 2 + u
                            h = b * NH + g * GH
                            sp.wait_ge(pv_done, groups(b, q4, g) + 1)
                            sp.dma_start(kg[0:ROWS, u, :, 0:W], KS0[bass.ds(h, GH), :, 0:W].rearrange("h r t -> r h t")).then_inc(g_loaded[u], 16)
                            sp.dma_start(qg[0:ROWS, u, :, :], QS0[bass.ds(h, GH), :, q4 * CHUNK:(q4 + 1) * CHUNK].rearrange("h r t -> r h t")).then_inc(g_loaded[u], 16)
                            sp.dma_start(vg[:, u, 0:4 * (q4 + 1)], V0[bass.ds(b, 1), :, 0:4 * (q4 + 1), bass.ds(g * GH, GH), :].rearrange("a p j h e -> (a p) j h e")).then_inc(g_loaded[u], 16)

        @block.scalar
        def _(act):
            act.sem_inc(o_copied, 1)
            with act.Fori(0, NB) as b:
                for q4 in range(4):
                    for t in range(4):
                        for ch in range(q4 + 1):
                            n = ff_chunks(b, q4, t) + ch
                            w = min(CHUNK, (4 * q4 + t + 1) * P - ch * CHUNK)
                            act.wait_ge(s_raw, n + 1 + 1)
                            act.wait_ge(sums_ready, ff_chunks(b, q4, t) * 2 + 1)
                            act.activation(S[:, ch * CHUNK:ch * CHUNK + w], max_ps[:, (t * (q4 + 1) + ch) % 2, 0:w], ACT.Relu).then_inc(s_pos, 1)
                    for J in range(4 * (q4 + 1)):
                        c0 = max(0, J - 4 * q4) * P
                        act.wait_ge(fft_ready, b * 40 + 4 * tri(q4) + J + 1)
                        act.activation(FFT[:, J, c0:CHUNK], t_ps[:, J % 4, c0:CHUNK], ACT.Copy).then_inc(fft_done, 1)
                    with act.Fori(0, NG // 2) as g2:
                        for u in range(2):
                            g = g2 * 2 + u
                            gi = groups(b, q4, g)
                            act.wait_ge(rows_ready, gi + 1)
                            act.activation(qg[ROWS:KR, u, :, :], t_ps[0:3, :, :], ACT.Copy).then_inc(rows_done, 1)
                            for J in range(4 * (q4 + 1)):
                                c0 = max(0, J - 4 * q4) * P
                                act.wait_ge(t_added, (key_steps(b, q4, g) + J) * 2 + 2)
                                act.activation(probs[:, J % 2, :, c0:CHUNK], probs[:, J % 2, :, c0:CHUNK], ACT.Exp).then_inc(exp_done, 1)
                            act.wait_ge(pv_done, gi + 3)
                            act.activation(oT[:], pv_ps[:], ACT.Copy).then_inc(o_copied, 1)

        @block.tensor
        def _(pe):
            pe.sem_inc(s_raw, 1)
            pe.sem_inc(sums_ready, 1)
            pe.sem_inc(pv_done, 2)
            pe.wait_ge(ones_set, 1)
            with pe.Fori(0, NB) as b:
                for q4 in range(4):
                    nch, nj = q4 + 1, 4 * (q4 + 1)
                    pe.wait_ge(head0_loaded, (blocks(b, q4) + 1) * 32)
                    for t in range(4):
                        n = ff_chunks(b, q4, t)
                        w = lambda ch: min(CHUNK, (4 * q4 + t + 1) * P - ch * CHUNK)
                        for ch in range(nch):
                            k = t * nch + ch
                            if k >= 2:
                                pe.wait_ge(s_pos, n + ch - 1)
                            pe.matmul(max_ps[:, k % 2, 0:w(ch)], q0[:, 0, t * P:(t + 1) * P], k0[:, 0, ch * CHUNK:ch * CHUNK + w(ch)],
                                      start=True, stop=True).then_inc(s_raw, 1)
                        pe.wait_ge(s_masked, (blocks(b, q4) * 4 + t) * 2 + 2)
                        for ch in range(nch):
                            k = t * nch + ch
                            if k >= 2:
                                pe.wait_ge(ff_done, n + ch - 1)
                            s = S[:, ch * CHUNK:ch * CHUNK + w(ch)]
                            pe.matmul(t_ps[:, 2 * (k % 2), 0:w(ch)], c.before[:], s, start=True, stop=True).then_inc(sums_ready, 1)
                            pe.matmul(t_ps[:, 2 * (k % 2) + 1, 0:w(ch)], c.ones[:], s, start=True, stop=True).then_inc(sums_ready, 1)
                    pe.wait_ge(ff_final, (blocks(b, q4) + 1) * 4)
                    for J in range(nj):
                        if J >= 4:
                            pe.wait_ge(fft_done, b * 40 + 4 * tri(q4) + J - 3)
                        for t in range(max(0, J - 4 * q4), 4):
                            last = pe.transpose(t_ps[:, J % 4, t * P:(t + 1) * P], FF[:, t, J * P:(J + 1) * P], c.ident[:])
                        last.then_inc(fft_ready, 1)
                    pe.wait_ge(fft_done, b * 40 + 4 * tri(q4) + nj)
                    hold(pe, c)
                    with pe.Fori(0, NG // 2) as g2:
                        for u in range(2):
                            g = g2 * 2 + u
                            gi = groups(b, q4, g)
                            pe.wait_ge(g_loaded[u], (blocks(b, q4) * 2 + g2 + 1) * 48)
                            k = 0
                            for h in range(GH):
                                for t in range(4):
                                    n_keys = (4 * q4 + t + 1) * P
                                    for ch in range(nch):
                                        w = min(CHUNK, n_keys - ch * CHUNK)
                                        if k >= 2:
                                            pe.wait_ge(max_done, max_chunks(b, q4, g) + k - 1)
                                        pe.matmul(max_ps[:, k % 2, 0:w], qg[0:ROWS, u, h, t * P:(t + 1) * P],
                                                  kg[0:ROWS, u, h, ch * CHUNK:ch * CHUNK + w], start=True, stop=True).then_inc(max_ready, 1)
                                        k += 1
                            pe.wait_ge(nm_ready, gi + 1)
                            for h in range(GH):
                                for t in range(4):
                                    last = pe.matmul(t_ps[0:3, h, t * P:(t + 1) * P], nm_parts[:, h * 4 + t, :], c.ident_bf[:], start=True, stop=True)
                            last.then_inc(rows_ready, 1)
                            pe.wait_ge(rows_done, gi + 1)

                            def scores(J):
                                c0 = max(0, J - 4 * q4) * P
                                for h in range(GH):
                                    if h % 2 == 0 and J >= 1:
                                        pe.wait_ge(t_added, (key_steps(b, q4, g) + J - 1) * 2 + h // 2 + 1)
                                    m = pe.matmul(t_ps[:, h, c0:CHUNK], kg[0:KR, u, h, J * P:(J + 1) * P], qg[0:KR, u, h, c0:CHUNK],
                                                  start=True, stop=True)
                                    if h % 2 == 1:
                                        m.then_inc(t_ready, 1)

                            scores(0)
                            for J in range(nj):
                                c0 = max(0, J - 4 * q4) * P
                                if J + 1 < nj:
                                    scores(J + 1)
                                pe.wait_ge(exp_done, key_steps(b, q4, g) + J + 1)
                                if J == 0:
                                    pe.wait_ge(o_copied, gi + 1)
                                for h in range(GH):
                                    m = pe.matmul(pv_ps[32 * h:32 * h + 32, c0:CHUNK], vg[:, u, J, h, :], probs[:, J % 2, h, c0:CHUNK],
                                                  start=(J == 0), stop=(J == nj - 1), tile_position=(0, 32 * h))
                                if J == nj - 1:
                                    m.then_inc(pv_done, 1)
                            pe.wait_ge(o_copied, gi + 1 + 1)
                            pe.wait_ge(y_steps, gi * 2 + 1)
                            for t in range(4):
                                m = pe.transpose(tr_ps[:, t * P:(t + 1) * P], oT[:, t * P:(t + 1) * P], c.ident[:])
                            m.then_inc(o_turned, 1)

        @block.vector
        def _(dve):
            dve.sem_inc(y_steps, 1)
            dve.memset(kg[ROWS:P, :, :, :], 1.0).then_inc(ones_set, 1)
            with dve.Fori(0, NB) as b:
                for q4 in range(4):
                    nch, nj = q4 + 1, 4 * (q4 + 1)
                    bi = blocks(b, q4)
                    for t in range(4):
                        for ch in range(nch):
                            n = ff_chunks(b, q4, t) + ch
                            k = t * nch + ch
                            w = min(CHUNK, (4 * q4 + t + 1) * P - ch * CHUNK)
                            dve.wait_ge(sums_ready, n * 2 + 2 + 1)
                            have = min(w, max(0, (4 * q4 + t) * P - ch * CHUNK))
                            if have:
                                dve.wait_ge(ff_done, n)
                                old = slice(ch * CHUNK, ch * CHUNK + have)
                                dve.tensor_tensor(FF[:, t, old], t_ps[:, 2 * (k % 2), 0:have], carry[:, old], ALU.add)
                                m = dve.tensor_tensor(carry[:, old], t_ps[:, 2 * (k % 2) + 1, 0:have], carry[:, old], ALU.add)
                            if have < w:
                                new = slice(ch * CHUNK + have, ch * CHUNK + w)
                                dve.tensor_copy(FF[:, t, new], t_ps[:, 2 * (k % 2), have:w])
                                m = dve.tensor_copy(carry[:, new], t_ps[:, 2 * (k % 2) + 1, have:w])
                            m.then_inc(ff_done, 1)
                    t0 = first_tile(q4)
                    s0 = sel_steps(b, q4)
                    dve.memset(thr[:], 0).then_inc(chain, 1)
                    dve.memset(bit[:], 1 << (NBIT - 1)).then_inc(chain, 1)
                    dve.wait_ge(ff_masked, (bi + 1) * 4)
                    hold(dve, c)
                    with dve.Fori(0, NBIT) as i:
                        v = s0 + 2 + i * (3 + 4 - t0)
                        dve.wait_ge(chain, v)
                        dve.tensor_tensor(cand[:], thr[:], bit[:], ALU.bitwise_or).then_inc(chain, 1)
                        dve.wait_ge(chain, v + 1)
                        dve.tensor_scalar(bit[:], bit[:], 1, None, ALU.logical_shift_right)
                        for t in range(t0, 4):
                            n_keys = (4 * q4 + t + 1) * P
                            if t >= t0 + 2:
                                dve.wait_ge(chain, v + t - t0)
                            dve.tensor_scalar((less, equal)[t % 2][:, 0:n_keys], FF[:, t, 0:n_keys], cand[:].bitcast(F32)[:, t:t + 1], 0.0,
                                              ALU.is_lt, ALU.add, accum_out=below[:, t:t + 1]).then_inc(chain, 1)
                        v += 1 + 4 - t0
                        dve.wait_ge(chain, v)
                        dve.tensor_scalar(take[:, t0:4], below[:, t0:4], BUDGET - 0.5, None, ALU.is_lt).then_inc(chain, 1)
                        dve.wait_ge(chain, v + 1)
                        hold(dve, c)
                        dve.copy_predicated(thr[:, t0:4], take[:, t0:4], cand[:, t0:4]).then_inc(chain, 1)
                    s1 = s0 + 2 + NBIT * (3 + 4 - t0)
                    dve.wait_ge(chain, s1)
                    for t in range(t0, 4):
                        n_keys = (4 * q4 + t + 1) * P
                        th = thr[:].bitcast(F32)[:, t:t + 1]
                        v = s1 + (t - t0) * 7
                        dve.tensor_scalar(equal[:, 0:n_keys], FF[:, t, 0:n_keys], th, None, ALU.is_equal)
                        dve.tensor_scalar(less[:, 0:n_keys], FF[:, t, 0:n_keys], th, 0.0, ALU.is_lt, ALU.add,
                                          accum_out=below[:, t:t + 1]).then_inc(chain, 1)
                        dve.wait_ge(chain, v + 1)
                        dve.tensor_scalar(need[:, t:t + 1], below[:, t:t + 1], -1.0, float(BUDGET), ALU.mult, ALU.add).then_inc(chain, 1)
                        dve.tensor_tensor_scan(S[:, 0:n_keys], c.ones[:, 0:1].broadcast_to([P, n_keys]), equal[:, 0:n_keys], 0.0,
                                               ALU.mult, ALU.add).then_inc(chain, 1)
                        dve.wait_ge(chain, v + 3)
                        dve.scalar_tensor_tensor(equal[:, 0:n_keys], S[:, 0:n_keys], need[:, t:t + 1], equal[:, 0:n_keys],
                                                 ALU.is_le, ALU.mult).then_inc(chain, 1)
                        dve.wait_ge(chain, v + 4)
                        dve.tensor_tensor(less[:, 0:n_keys], less[:, 0:n_keys], equal[:, 0:n_keys], ALU.add).then_inc(chain, 1)
                        dve.wait_ge(chain, v + 5)
                        dve.tensor_scalar(less[:, 0:n_keys], less[:, 0:n_keys], 0.5, BIG, ALU.is_lt, ALU.mult).then_inc(chain, 1)
                        dve.wait_ge(chain, v + 6)
                        dve.tensor_tensor(FF[:, t, 0:n_keys], FF[:, t, 0:n_keys], less[:, 0:n_keys], ALU.add).then_inc(chain, 1)
                        dve.wait_ge(chain, v + 7)
                    dve.sem_inc(kept, 1)
                    dve.wait_ge(ff_final, (bi + 1) * 4)
                    hold(dve, c)
                    with dve.Fori(0, NG // 2) as g2:
                        for u in range(2):
                            g = g2 * 2 + u
                            gi = groups(b, q4, g)
                            k = 0
                            for h in range(GH):
                                for t in range(4):
                                    for ch in range(nch):
                                        w = min(CHUNK, (4 * q4 + t + 1) * P - ch * CHUNK)
                                        dve.wait_ge(max_ready, max_chunks(b, q4, g) + k + 1)
                                        if k >= 2:
                                            dve.wait_ge(max_done, max_chunks(b, q4, g) + k - 1)
                                        hold(dve, c)
                                        dve.tensor_tensor_reduce(trash[:, k % 2, 0:w], max_ps[:, k % 2, 0:w], FF[:, t, ch * CHUNK:ch * CHUNK + w],
                                                                 1.0, -BIG, ALU.subtract, ALU.max,
                                                                 accum_out=part_max[:, h * 4 + t, ch:ch + 1]).then_inc(max_done, 1)
                                        k += 1
                            dve.wait_ge(max_done, max_chunks(b, q4, g) + k)
                            dve.tensor_reduce(neg_max[:], part_max[:, :, 0:nch], AX.X, ALU.max, negate=True).then_inc(nm_steps, 1)
                            dve.wait_ge(nm_steps, gi * 4 + 1)
                            dve.tensor_copy(nm_parts[:, :, 0], neg_max[:]).then_inc(nm_steps, 1)
                            dve.wait_ge(nm_steps, gi * 4 + 2)
                            dve.tensor_tensor(nm_rest[:], neg_max[:], nm_parts[:, :, 0], ALU.subtract).then_inc(nm_steps, 1)
                            dve.wait_ge(nm_steps, gi * 4 + 3)
                            dve.tensor_copy(nm_parts[:, :, 1], nm_rest[:]).then_inc(nm_steps, 1)
                            dve.wait_ge(nm_steps, gi * 4 + 4)
                            dve.tensor_tensor(nm_parts[:, :, 2], nm_rest[:], nm_parts[:, :, 1], ALU.subtract).then_inc(nm_ready, 1)
                            for J in range(nj):
                                c0 = max(0, J - 4 * q4) * P
                                ks = key_steps(b, q4, g) + J
                                for half in range(2):
                                    dve.wait_ge(t_ready, ks * 2 + half + 1)
                                    dve.tensor_tensor(probs[:, J % 2, 2 * half:2 * half + 2, c0:CHUNK], t_ps[:, 2 * half:2 * half + 2, c0:CHUNK],
                                                      FFT[:, J:J + 1, c0:CHUNK].broadcast_to([P, 2, CHUNK - c0]), ALU.subtract).then_inc(t_added, 1)
                            dve.wait_ge(o_turned, gi + 1)
                            turned = tr_ps[:].rearrange("p (t h e) -> p t h e", t=4, h=GH)
                            dve.reciprocal(recip[:], turned[:, :, :, HD]).then_inc(y_steps, 1)
                            dve.wait_ge(y_steps, gi * 2 + 1 + 1)
                            dve.wait_ge(y_free, gi + 1)
                            dve.tensor_tensor(y[:], turned[:, :, :, 0:HD], recip[:].rearrange("p t (h a) -> p t h a", a=1).broadcast_to([P, 4, GH, HD]),
                                              ALU.mult).then_inc(y_steps, 1)


def experts_ffn(nc, c, XT, X, w_red, wg, w1, b1, w2, b2):
    NE, F, GD, D = 8, 1024, 16, 256
    NT = 32
    NF = F // P
    with ExitStack() as ctx:
        sb = lambda n, s, d=F32: ctx.enter_context(nc.sbuf_tensor(n, s, d))
        sem = c.sem
        ps = lambda n, s: ctx.enter_context(nc.psum_tensor(n, s, F32))
        w_red_sb = sb("e_w_red", [P, 2, GD])
        wg_sb = sb("e_wg", [NE, GD])
        wg_sq = sb("e_wg_sq", [NE, GD])
        wg_norm = sb("e_wg_norm", [NE, 1])
        wgT = sb("e_wgT", [GD, NE])
        xt = sb("e_xt", [P, 2, 2, CHUNK])
        redT = sb("e_redT", [GD, 2, CHUNK])
        logits = sb("e_logits", [P, NT, NE])
        gates = sb("e_gates", [P, NT, NE])
        order = sb("e_order", [P, NE])
        col = sb("e_col", [P, NT])
        b2_sb = sb("e_b2", [NE, D])
        gT = sb("e_gT", [NE, 2, P])
        w1_sb = sb("e_w1", [P, 2, 2, F])
        w2_sb = sb("e_w2", [P, 2, NF, D])
        b1_sb = sb("e_b1", [P, 2, NF])
        hid = sb("e_hid", [P, 2, CHUNK])
        h_ps = ps("e_h_ps", [P, 2, CHUNK])
        y_ps = ps("e_y_ps", [P, 4, CHUNK])
        small_loaded, norm, redT_ready, redT_done, logit_ready, logit_done = (
            sem("small_loaded"), sem("norm"), sem("redT_ready"), sem("redT_done"), sem("logit_ready"), sem("logit_done"))
        pick, gT_ready, gT_done, bias_ready, bias_done = sem("pick"), sem("gT_ready"), sem("gT_done"), sem("bias_ready"), sem("bias_done")
        xt_loaded = [sem(f"xt_loaded{u}") for u in range(2)]
        xt_again = [sem(f"xt_again{u}") for u in range(2)]
        w_loaded = [sem(f"w_loaded{u}") for u in range(2)]
        h_ready, h_done, y_ready, y_done = sem("h_ready"), sem("h_done"), sem("y_ready"), sem("y_done")
        order_set, exp_done = sem("order_set"), sem("exp_done")

        with nc.Block() as block:
            @block.sync
            def _(sp):
                sp.dma_start(w_red_sb[:], w_red.rearrange("(h p) r -> p h r", p=P)).then_inc(small_loaded, 16)
                sp.dma_start(wg_sb[:], wg).then_inc(small_loaded, 16)
                sp.dma_start(b2_sb[:], b2).then_inc(small_loaded, 16)
                with sp.Fori(0, 4) as it:
                    for u in range(2):
                        ch = it * 2 + u
                        sp.wait_ge(redT_ready, ch + 1)
                        sp.dma_start(xt[:, u, :, :], XT[bass.ds(ch, 1), :, :, :].rearrange("a p h t -> (a p) h t")).then_inc(xt_loaded[u], 16)

            @block.gpsimd
            def _(pool):
                pool.iota(order[:], pattern=[[1, NE]], base=-NE, channel_multiplier=0,
                          allow_small_or_imprecise_dtypes=True).then_inc(order_set, 1)

            @block.scalar
            def _(act):
                act.wait_ge(norm, 1)
                act.activation(wg_norm[:], wg_norm[:], ACT.Sqrt).then_inc(norm, 1)
                with act.Fori(0, 4) as it:
                    for u in range(2):
                        ch = it * 2 + u
                        act.wait_ge(redT_ready, ch + 3)
                        act.wait_ge(logit_ready, ch + 1)
                        act.activation(redT[:, u, :], h_ps[0:GD, u, :], ACT.Copy).then_inc(redT_done, 1)
                act.wait_ge(pick, 2)
                act.activation(gates[:], gates[:], ACT.Exp).then_inc(exp_done, 1)

            @block.tensor
            def _(pe):
                pe.sem_inc(logit_ready, 1)
                pe.sem_inc(redT_ready, 2)
                pe.wait_ge(norm, 5)
                pe.transpose(y_ps[0:GD, 3, 0:NE], wg_sb[:], c.ident[0:NE, 0:NE]).then_inc(logit_ready, 1)
                pe.wait_ge(norm, 6)
                with pe.Fori(0, 4) as it:
                    for u in range(2):
                        ch = it * 2 + u
                        pe.wait_ge(xt_loaded[u], it * 16 + 16)
                        for half in range(2):
                            m = pe.matmul(h_ps[0:GD, u, :], w_red_sb[:, half, :], xt[:, u, half, :], start=(half == 0), stop=(half == 1))
                        m.then_inc(redT_ready, 1)
                        pe.wait_ge(redT_done, ch + 1)
                        pe.wait_ge(logit_done, ch + 1)
                        for t in range(4):
                            m = pe.matmul(y_ps[:, t, 0:NE], redT[:, u, t * P:(t + 1) * P], wgT[:], start=True, stop=True)
                        m.then_inc(logit_ready, 1)

            @block.vector
            def _(dve):
                dve.sem_inc(logit_done, 1)
                dve.wait_ge(small_loaded, 48)
                dve.tensor_tensor_reduce(wg_sq[:], wg_sb[:], wg_sb[:], 1.0, 0.0, ALU.mult, ALU.add, accum_out=wg_norm[:]).then_inc(norm, 1)
                dve.wait_ge(norm, 2)
                dve.tensor_scalar(wg_norm[:], wg_norm[:], 1e-4, None, ALU.max).then_inc(norm, 1)
                dve.wait_ge(norm, 3)
                dve.reciprocal(wg_norm[:], wg_norm[:]).then_inc(norm, 1)
                dve.wait_ge(norm, 4)
                dve.tensor_scalar(wg_sb[:], wg_sb[:], wg_norm[:, 0:1], None, ALU.mult).then_inc(norm, 1)
                dve.wait_ge(logit_ready, 1 + 1)
                dve.tensor_copy(wgT[:], y_ps[0:GD, 3, 0:NE]).then_inc(norm, 1)
                with dve.Fori(0, 8) as ch:
                    dve.wait_ge(logit_ready, ch + 2 + 1)
                    dve.tensor_copy(logits[:, bass.ds(ch * 4, 4), :], y_ps[:, :, 0:NE]).then_inc(logit_done, 1)
                dve.wait_ge(logit_done, 8 + 1)
                over = lambda a: a[:].rearrange("p (t a) -> p t a", a=1).broadcast_to([P, NT, NE])
                dve.tensor_reduce(col[:], logits[:], AX.X, ALU.max).then_inc(pick, 1)
                dve.wait_ge(pick, 1)
                dve.tensor_tensor(gates[:], logits[:], over(col), ALU.subtract).then_inc(pick, 1)
                dve.wait_ge(exp_done, 1)
                dve.tensor_reduce(col[:], gates[:], AX.X, ALU.add).then_inc(pick, 1)
                dve.wait_ge(pick, 3)
                dve.reciprocal(col[:], col[:]).then_inc(pick, 1)
                dve.wait_ge(pick, 4)
                dve.tensor_tensor(gates[:], gates[:], over(col), ALU.mult).then_inc(pick, 1)
                dve.wait_ge(pick, 5)
                dve.tensor_reduce(col[:], gates[:], AX.X, ALU.max).then_inc(pick, 1)
                dve.wait_ge(pick, 6)
                dve.tensor_tensor(logits[:], gates[:], over(col), ALU.is_equal).then_inc(pick, 1)
                dve.wait_ge(pick, 7)
                dve.wait_ge(order_set, 1)
                dve.tensor_tensor(logits[:], logits[:], order[:].rearrange("p (a e) -> p a e", a=1).broadcast_to([P, NT, NE]), ALU.mult).then_inc(pick, 1)
                dve.wait_ge(pick, 8)
                dve.tensor_reduce(col[:], logits[:], AX.X, ALU.min).then_inc(pick, 1)
                dve.wait_ge(pick, 9)
                dve.tensor_tensor(logits[:], logits[:], over(col), ALU.is_equal).then_inc(pick, 1)
                dve.wait_ge(pick, 10)
                dve.tensor_tensor(gates[:], gates[:], logits[:], ALU.mult).then_inc(pick, 1)

        with nc.Block() as block:
            @block.sync
            def _(sp):
                with sp.Fori(0, NE // 2) as e2:
                    for u in range(2):
                        e = e2 * 2 + u
                        sp.wait_ge(y_ready, e * 8 + 8)
                        sp.dma_start(w1_sb[:, u], w1[bass.ds(e, 1), :, :].rearrange("a (h p) f -> (a p) h f", p=P)).then_inc(w_loaded[u], 16)
                        sp.dma_start(w2_sb[:, u], w2[bass.ds(e, 1), :, :].rearrange("a (n p) d -> (a p) n d", p=P)).then_inc(w_loaded[u], 16)
                        sp.dma_start(b1_sb[:, u], b1[bass.ds(e, 1), :].rearrange("a (n p) -> (a p) n", p=P), allow_slow_non_contiguous=True).then_inc(w_loaded[u], 16)

            @block.gpsimd
            def _(pool):
                with pool.Fori(0, NE * 4) as it:
                    for u in range(2):
                        n = it * 2 + u
                        pool.wait_ge(h_ready, n * NF + NF)
                        pool.dma_start(xt[:, u, :, :], XT[bass.ds(n % 8, 1), :, :, :].rearrange("a p h t -> (a p) h t")).then_inc(xt_again[u], 16)

            @block.scalar
            def _(act):
                with act.Fori(0, NE // 2) as e2:
                    for u in range(2):
                        with act.Fori(0, 8) as ch:
                            for f in range(NF):
                                n = ((e2 * 2 + u) * 8 + ch) * NF + f
                                act.wait_ge(h_ready, n + 17)
                                act.activation(hid[:, f % 2, :], h_ps[:, f % 2, :], ACT.Gelu, bias=b1_sb[:, u, f:f + 1]).then_inc(h_done, 1)

            @block.tensor
            def _(pe):
                pe.sem_inc(h_ready, 2 * NF)
                pe.sem_inc(y_ready, 2 * 8)
                with pe.Fori(0, NE // 2) as e2:
                    for u in range(2):
                        pe.wait_ge(w_loaded[u], e2 * 48 + 48)
                        hold(pe, c)
                        with pe.Fori(0, 4) as it:
                            for v in range(2):
                                n = (e2 * 2 + u) * 8 + it * 2 + v
                                pe.wait_ge(xt_again[v], ((e2 * 2 + u) * 4 + it) * 16 + 16)

                                def hidden(f):
                                    for half in range(2):
                                        m = pe.matmul(h_ps[:, f % 2, :], w1_sb[:, u, half, f * P:(f + 1) * P], xt[:, v, half, :],
                                                      start=(half == 0), stop=(half == 1))
                                    m.then_inc(h_ready, 1)

                                hidden(0)
                                for f in range(NF):
                                    if f + 1 < NF:
                                        hidden(f + 1)
                                    pe.wait_ge(h_done, n * NF + f + 1)
                                    if f == 0:
                                        pe.wait_ge(y_done, n + 1)
                                    for t in range(4):
                                        m = pe.matmul(y_ps[:, t, 0:D], hid[:, f % 2, t * P:(t + 1) * P], w2_sb[:, u, f, :],
                                                      start=(f == 0), stop=(f == NF - 1))
                                m.then_inc(y_ready, 1)

            @block.vector
            def _(dve):
                dve.sem_inc(y_done, 1)
                with dve.Fori(0, NE) as e:
                    with dve.Fori(0, 8) as ch:
                        n = e * 8 + ch
                        dve.wait_ge(y_ready, n + 17)
                        dve.wait_ge(y_done, n + 1)
                        for t in range(4):
                            m = dve.scalar_tensor_tensor(X[:, bass.ds(ch * 4 + t, 1), :], y_ps[:, t:t + 1, 0:D],
                                                         gates[:, bass.ds(ch * 4 + t, 1), bass.ds(e, 1)].rearrange("p a b -> p (a b)"),
                                                         X[:, bass.ds(ch * 4 + t, 1), :], ALU.mult, ALU.add)
                        m.then_inc(y_done, 1)

        with nc.Block() as block:
            @block.tensor
            def _(pe):
                for t in range(NT):
                    pe.transpose(h_ps[0:NE, t % 2, 0:P], gates[:, t, :], c.ident[:]).then_inc(gT_ready, 1)
                    pe.wait_ge(gT_done, t + 1)
                    if t >= 4:
                        pe.wait_ge(bias_done, t - 3)
                    pe.matmul(y_ps[:, t % 4, 0:D], gT[:, t % 2, :], b2_sb[:], start=True, stop=True).then_inc(bias_ready, 1)

            @block.scalar
            def _(act):
                for t in range(NT):
                    act.wait_ge(gT_ready, t + 1)
                    if t >= 2:
                        act.wait_ge(bias_ready, t - 1)
                    act.activation(gT[:, t % 2, :], h_ps[0:NE, t % 2, 0:P], ACT.Copy).then_inc(gT_done, 1)

            @block.vector
            def _(dve):
                for t in range(NT):
                    dve.wait_ge(bias_ready, t + 1)
                    dve.tensor_tensor(X[:, t, :], y_ps[:, t % 4, 0:D], X[:, t, :], ALU.add).then_inc(bias_done, 1)


def project_out(nc, c, layer, Y, X, w, bias, w_is_transposed):
    D = 256
    with ExitStack() as ctx:
        sb = lambda n, s, d=F32: ctx.enter_context(nc.sbuf_tensor(f"{layer}_{n}", s, d))
        sem = lambda n: c.sem(f"{layer}_{n}")
        ps = lambda n, s: ctx.enter_context(nc.psum_tensor(f"{layer}_{n}", s, F32))
        w_in = sb("o_w_in", [P, 2, D])
        W = sb("o_W", [P, 2, D])
        bias_row = sb("o_bias", [P, D])
        y = sb("o_y", [P, 2, 4, D])
        yT = sb("o_yT", [P, 2, 2, CHUNK])
        t_ps = ps("o_t_ps", [P, 2, 2, CHUNK])
        o_ps = ps("o_o_ps", [P, 4, CHUNK])
        w_loaded, w_turned, w_ready, biased = sem("w_loaded"), sem("w_turned"), sem("w_ready"), sem("biased")
        y_loaded = [sem(f"y_loaded{u}") for u in range(2)]
        yT_ready, yT_done, o_ready, o_done = sem("yT_ready"), sem("yT_done"), sem("o_ready"), sem("o_done")
        Yf = Y.rearrange("b t f -> (b t) f")
        block = ctx.enter_context(nc.Block())

        @block.sync
        def _(sp):
            sp.dma_start(w_in[:], w.rearrange("(h p) n -> p h n", p=P)).then_inc(w_loaded, 16)
            sp.dma_start(bias_row[:], bias.rearrange("(a n) -> a n", a=1).broadcast_to([P, D])).then_inc(w_loaded, 16)
            with sp.Fori(0, 4) as it:
                for u in range(2):
                    ch = it * 2 + u
                    sp.wait_ge(yT_ready, ch + 1)
                    sp.dma_start(y[:, u], Yf[bass.ds(ch * CHUNK, CHUNK), :].rearrange("(t p) f -> p t f", p=P)).then_inc(y_loaded[u], 16)

        @block.gpsimd
        def _(pool):
            pool.wait_ge(w_loaded, 32)
            pool.tensor_tensor(X[:], X[:], bias_row[:].rearrange("p (a n) -> p a n", a=1).broadcast_to([P, 32, D]), ALU.add).then_inc(biased, 1)

        @block.scalar
        def _(act):
            act.sem_inc(yT_done, 1)
            act.wait_ge(w_turned, 1)
            if w_is_transposed:
                act.activation(W[:], o_ps[:, 0:2, 0:D], ACT.Copy).then_inc(w_ready, 1)
            else:
                act.activation(W[:], w_in[:], ACT.Copy).then_inc(w_ready, 1)
            with act.Fori(0, 4) as it:
                for u in range(2):
                    ch = it * 2 + u
                    act.wait_ge(yT_ready, ch + 3)
                    act.wait_ge(o_ready, ch + 1)
                    act.activation(yT[:, u], t_ps[:, u], ACT.Copy).then_inc(yT_done, 1)

        @block.tensor
        def _(pe):
            pe.sem_inc(o_ready, 1)
            pe.sem_inc(yT_ready, 2)
            pe.wait_ge(w_loaded, 32)
            for out_half in range(2):
                for in_half in range(2):
                    m = pe.transpose(o_ps[:, in_half, out_half * P:(out_half + 1) * P],
                                     w_in[:, out_half, in_half * P:(in_half + 1) * P], c.ident[:])
            m.then_inc(w_turned, 1)
            pe.wait_ge(w_ready, 1)
            with pe.Fori(0, 4) as it:
                for u in range(2):
                    ch = it * 2 + u
                    pe.wait_ge(y_loaded[u], it * 16 + 16)
                    pe.wait_ge(yT_done, ch + 1)
                    for half in range(2):
                        for t in range(4):
                            m = pe.transpose(t_ps[:, u, half, t * P:(t + 1) * P], y[:, u, t, half * P:(half + 1) * P], c.ident[:])
                    m.then_inc(yT_ready, 1)
                    pe.wait_ge(yT_done, ch + 1 + 1)
                    pe.wait_ge(o_done, ch + 1)
                    for t in range(4):
                        for half in range(2):
                            m = pe.matmul(o_ps[:, t, 0:D], yT[:, u, half, t * P:(t + 1) * P], W[:, half, :], start=(half == 0), stop=(half == 1))
                    m.then_inc(o_ready, 1)

        @block.vector
        def _(dve):
            dve.sem_inc(o_done, 1)
            dve.wait_ge(biased, 1)
            with dve.Fori(0, 8) as ch:
                dve.wait_ge(o_ready, ch + 1 + 1)
                dve.tensor_tensor(X[:, bass.ds(ch * 4, 4), :], o_ps[:, :, 0:D], X[:, bass.ds(ch * 4, 4), :], ALU.add).then_inc(o_done, 1)


def project_qkv1(nc, c, XT, W_qk, W_v, QA1, KA1, V1):
    NH, DQ, DV, D = 8, 64, 32, 256
    SCALE = DQ ** -0.5
    with ExitStack() as ctx:
        sb = lambda n, s, d=F32: ctx.enter_context(nc.sbuf_tensor(n, s, d))
        sem = c.sem
        ps = lambda n, s: ctx.enter_context(nc.psum_tensor(n, s, F32))
        wqk = sb("p1_wqk", [P, 2, 2 * NH * DQ])
        wv = sb("p1_wv", [P, 2, D])
        xt = sb("p1_xt", [P, 2, 2, CHUNK])
        full = sb("p1_full", [P, 8, CHUNK])
        v_sb = sb("p1_v", [P, 2, 4, D])
        proj_ps = ps("p1_proj", [P, 4, CHUNK])
        v_ps = ps("p1_v_ps", [P, 4, CHUNK])
        w_loaded = sem("w_loaded")
        xt_loaded = [sem(f"xt_loaded{u}") for u in range(2)]
        proj_ready, full_ready, v_ready, v_copied = sem("proj_ready"), sem("full_ready"), sem("v_ready"), sem("v_copied")
        full_stored = [sem(f"full_stored{m}") for m in range(8)]
        v_stored = [sem(f"v_stored{u}") for u in range(2)]
        block = ctx.enter_context(nc.Block())

        @block.gpsimd
        def _(pool):
            pool.dma_start(wqk[:], W_qk.rearrange("(h p) n -> p h n", p=P)).then_inc(w_loaded, 16)
            pool.dma_start(wv[:], W_v.rearrange("(h p) n -> p h n", p=P)).then_inc(w_loaded, 16)
            with pool.Fori(0, 4) as it:
                for u in range(2):
                    ch = it * 2 + u
                    pool.wait_ge(v_ready, ch + 1)
                    pool.dma_start(xt[:, u, :, :], XT[bass.ds(ch, 1), :, :, :].rearrange("a p h t -> (a p) h t")).then_inc(xt_loaded[u], 16)

        @block.sync
        def _(sp):
            with sp.Fori(0, 4) as it:
                for u in range(2):
                    ch = it * 2 + u
                    b, t0 = ch // 4, (ch % 4) * CHUNK
                    for m in range(8):
                        sp.wait_ge(full_ready, ch * 8 + m + 1 + 1)
                        dst = QA1 if m < 4 else KA1
                        sp.dma_start(dst[bass.ds(b * NH + 2 * (m % 4), 2), 0:DQ, bass.ds(t0, CHUNK)], full[:, m, :]).then_inc(full_stored[m], 16)
                    sp.wait_ge(v_copied, ch + 1 + 1)
                    sp.dma_start(V1[bass.ds(b, 1), :, bass.ds((ch % 4) * 4, 4), :, :].rearrange("a p j h e -> (a p) j (h e)"),
                                 v_sb[:, u]).then_inc(v_stored[u], 16)
            for m in range(8):
                sp.wait_ge(full_stored[m], (8 + 1) * 16)
            for u in range(2):
                sp.wait_ge(v_stored[u], (4 + 1) * 16)

        @block.scalar
        def _(act):
            act.sem_inc(full_ready, 1)
            for m in range(8):
                act.sem_inc(full_stored[m], 16)
            with act.Fori(0, 8) as ch:
                for m in range(8):
                    act.wait_ge(proj_ready, ch * 8 + m + 1)
                    act.wait_ge(full_stored[m], (ch + 1) * 16)
                    act.activation(full[:, m, :], proj_ps[:, m % 4, :], ACT.Copy, scale=SCALE if m < 4 else 1.0).then_inc(full_ready, 1)

        @block.vector
        def _(dve):
            dve.sem_inc(v_copied, 1)
            for u in range(2):
                dve.sem_inc(v_stored[u], 16)
            with dve.Fori(0, 4) as it:
                for u in range(2):
                    ch = it * 2 + u
                    dve.wait_ge(v_ready, ch + 3)
                    dve.wait_ge(v_stored[u], (it + 1) * 16)
                    dve.tensor_copy(v_sb[:, u], v_ps[:, :, 0:D]).then_inc(v_copied, 1)

        @block.tensor
        def _(pe):
            pe.wait_ge(w_loaded, 32)
            pe.sem_inc(v_ready, 2)
            with pe.Fori(0, 4) as it:
                for u in range(2):
                    ch = it * 2 + u
                    pe.wait_ge(xt_loaded[u], it * 16 + 16)
                    for m in range(8):
                        if m >= 4:
                            pe.wait_ge(full_ready, ch * 8 + m - 3 + 1)
                        elif m == 0:
                            pe.wait_ge(full_ready, ch * 8 + 1)
                        for half in range(2):
                            last = pe.matmul(proj_ps[:, m % 4, :], wqk[:, half, m * P:(m + 1) * P], xt[:, u, half, :],
                                             start=(half == 0), stop=(half == 1))
                        last.then_inc(proj_ready, 1)
                    pe.wait_ge(v_copied, ch + 1)
                    for t in range(4):
                        for half in range(2):
                            last = pe.matmul(v_ps[:, t, 0:D], xt[:, u, half, t * P:(t + 1) * P], wv[:, half, :],
                                             start=(half == 0), stop=(half == 1))
                    last.then_inc(v_ready, 1)


BAND = 9
BW = P + 2 * BAND


def bias_operands(nc, c, conv, QA1, KA1, EXT, BQ, BK):
    NH, NT, T, NREL = 8, 16, 2048, 21
    L = BW + P - 1
    FAR = (L - NREL) // 2
    with ExitStack() as ctx:
        sb = lambda n, s, d=F32: ctx.enter_context(nc.sbuf_tensor(n, s, d))
        sem = c.sem
        ext = sb("b_ext", [P, 2, NH, L])
        cb = sb("b_cb", [P, NH, NREL])
        band = sb("b_band", [P, 2, NH, BW])
        tile_of = sb("b_tile_of", [NT, T])
        before = sb("b_before", [NT, T])
        after = sb("b_after", [NT, T])
        base = sb("b_base", [NT, NH, T])
        loaded, ext_steps, ext_stored, band_loaded, band_done, filled, masks, base_half, base_done, stored = (
            sem("loaded"), sem("ext_steps"), sem("ext_stored"), sem("band_loaded"), sem("band_done"), sem("filled"),
            sem("masks"), sem("base_half"), sem("base_done"), sem("stored"))
        block = ctx.enter_context(nc.Block())

        @block.sync
        def _(sp):
            sp.dma_start(cb[:], conv.rearrange("(a h) r -> a h r", a=1).broadcast_to([P, NH, NREL])).then_inc(loaded, 16)
            sp.wait_ge(ext_steps, 3 + NREL)
            sp.dma_start(EXT, ext[:].rearrange("p s h l -> p (s h l)")).then_inc(ext_stored, 16)
            sp.wait_ge(ext_stored, 16)
            sp.dma_start(band[:].rearrange("p s h w -> p (s h) w"),
                         bass.AP(tensor=EXT.tensor, offset=EXT.offset + P - 1,
                                 ap=[[2 * NH * L - 1, P], [L, 2 * NH], [1, BW]])).then_inc(band_loaded, 16)
            sp.wait_ge(band_done, 4)
            sp.dma_start(BQ.rearrange("h p w -> p h w"), band[:, 0]).then_inc(stored, 16)
            sp.dma_start(BK.rearrange("h p w -> p h w"), band[:, 1]).then_inc(stored, 16)
            sp.wait_ge(masks, 4)
            for bh in range(2 * NH):
                sp.dma_start(QA1[bh, 64:64 + NT, :], tile_of[:]).then_inc(stored, 16)
            sp.wait_ge(base_done, NH)
            for b in range(2):
                sp.dma_start(KA1[b * NH:(b + 1) * NH, 64:64 + NT, :].rearrange("h r t -> r h t"), base[:]).then_inc(stored, 16)
            sp.wait_ge(stored, 20 * 16)

        @block.gpsimd
        def _(pool):
            pool.memset(tile_of[:], 1.0).then_inc(filled, 1)
            pool.memset(before[:], 1.0).then_inc(filled, 1)
            pool.memset(after[:], 1.0).then_inc(filled, 1)
            pool.wait_ge(filled, 3)
            pool.affine_select(out=before[:], in_=before[:], compare_op=ALU.is_gt, fill=0.0, base=0,
                               pattern=[[-1, T]], channel_multiplier=P).then_inc(masks, 1)
            pool.affine_select(out=after[:], in_=after[:], compare_op=ALU.is_ge, fill=0.0, base=-P,
                               pattern=[[1, T]], channel_multiplier=-P).then_inc(masks, 1)
            pool.wait_ge(masks, 2)
            pool.tensor_tensor(tile_of[:], tile_of[:], before[:], ALU.subtract).then_inc(masks, 1)
            pool.wait_ge(masks, 3)
            pool.tensor_tensor(tile_of[:], tile_of[:], after[:], ALU.subtract).then_inc(masks, 1)

        @block.vector
        def _(dve):
            dve.wait_ge(loaded, 16)
            wide = lambda r, n: cb[:, :, r:r + 1].broadcast_to([P, NH, n])
            dve.tensor_copy(ext[:, 0, :, 0:FAR], wide(0, FAR))
            dve.tensor_copy(ext[:, 0, :, FAR:FAR + NREL], cb[:]).then_inc(ext_steps, 1)
            dve.tensor_copy(ext[:, 0, :, FAR + NREL:L], wide(NREL - 1, FAR)).then_inc(ext_steps, 1)
            dve.tensor_copy(ext[:, 1, :, 0:FAR], wide(NREL - 1, FAR))
            dve.tensor_copy(ext[:, 1, :, FAR + NREL:L], wide(0, FAR)).then_inc(ext_steps, 1)
            for r in range(NREL):
                dve.tensor_copy(ext[:, 1, :, FAR + r:FAR + r + 1], cb[:, :, NREL - 1 - r:NREL - r]).then_inc(ext_steps, 1)
            dve.wait_ge(masks, 4)
            for h in range(NH):
                dve.tensor_scalar(base[:, h, :], before[:], cb[0:NT, h, 0:1], None, ALU.mult).then_inc(base_half, 1)
                dve.wait_ge(base_half, h + 1)
                dve.scalar_tensor_tensor(base[:, h, :], after[:], cb[0:NT, h, NREL - 1:NREL], base[:, h, :],
                                         ALU.mult, ALU.add).then_inc(base_done, 1)
            dve.wait_ge(band_loaded, 16)
            first, last = slice(0, BAND), slice(P + BAND, BW)
            for s, cols, r in ((0, first, 0), (0, last, NREL - 1), (1, first, NREL - 1), (1, last, 0)):
                dve.tensor_tensor(band[:, s, :, cols], band[:, s, :, cols], cb[:, :, r:r + 1].broadcast_to([P, NH, BAND]),
                                  ALU.subtract).then_inc(band_done, 1)


def relative_attention(nc, c, QA1, KA1, V1, BQ, BK, Y1):
    NB, T, NH, DQ, DV = 2, 2048, 8, 64, 32
    NT = T // P
    SR, ONE, KR = DQ + NT, 96, 97
    GH = 4
    NCH = T // CHUNK
    NPAIR = 4
    MC = 16 * NCH
    with ExitStack() as ctx:
        sb = lambda n, s, d=F32: ctx.enter_context(nc.sbuf_tensor(n, s, d))
        sem = c.sem
        ps = lambda n, s: ctx.enter_context(nc.psum_tensor(n, s, F32))
        kg = sb("a1_kg", [P, GH, T])
        qg = sb("a1_qg", [P, 2, GH, CHUNK])
        vg = sb("a1_vg", [P, NT, GH, DV])
        bq = sb("a1_bq", [P, GH, BW])
        bk = sb("a1_bk", [P, GH, BW])
        part_max = sb("a1_part_max", [P, GH * 4, NCH])
        neg_max = sb("a1_neg_max", [P, GH * 4])
        probs = sb("a1_probs", [P, 2, GH, CHUNK])
        oT = sb("a1_oT", [P, 2, CHUNK])
        recip = sb("a1_recip", [P, 4, GH])
        y = sb("a1_y", [P, 4, GH, DV])
        max_ps = ps("a1_max_ps", [P, 2, CHUNK])
        t_ps = ps("a1_t_ps", [P, 4, CHUNK])
        pv_ps = ps("a1_pv_ps", [P, 2, CHUNK])
        fixed_set, k_loaded, max_ready, max_done, nm_ready, rows_ready, rows_done = (
            sem("fixed_set"), sem("k_loaded"), sem("max_ready"), sem("max_done"), sem("nm_ready"), sem("rows_ready"), sem("rows_done"))
        q_loaded = [sem(f"q_loaded{u}") for u in range(2)]
        t_ready, exp_done, pv_done, o_copied, o_turned, y_steps, y_stored, y_free = (
            sem("t_ready"), sem("exp_done"), sem("pv_done"), sem("o_copied"), sem("o_turned"), sem("y_steps"), sem("y_stored"), sem("y_free"))
        block = ctx.enter_context(nc.Block())

        def pieces(lo, hi, b0, b1):
            lo, hi = max(lo, b0), min(hi, b1)
            while lo < hi:
                end = min(hi, (lo // CHUNK + 1) * CHUNK)
                yield lo, end
                lo = end

        @block.sync
        def _(sp):
            sp.wait_ge(fixed_set, 3)
            with sp.Fori(0, NPAIR) as pr:
                b, g = pr // 2, pr % 2
                h = pr * GH
                sp.wait_ge(pv_done, pr * 4 + 1)
                sp.dma_start(kg[0:SR], KA1[bass.ds(h, GH), :, :].rearrange("h r t -> r h t")).then_inc(k_loaded, 16)
                sp.dma_start(bq[:], BQ[bass.ds(g * GH, GH), :, :].rearrange("h p w -> p h w")).then_inc(k_loaded, 16)
                sp.dma_start(bk[:], BK[bass.ds(g * GH, GH), :, :].rearrange("h p w -> p h w")).then_inc(k_loaded, 16)
                sp.dma_start(vg[:], V1[bass.ds(b, 1), :, :, bass.ds(g * GH, GH), :].rearrange("a p j h e -> (a p) j h e")).then_inc(k_loaded, 16)
                for q4 in range(4):
                    u = q4 % 2
                    if q4 >= 2:
                        sp.wait_ge(pv_done, pr * 4 + q4 - 1 + 1)
                    sp.dma_start(qg[0:SR, u], QA1[bass.ds(h, GH), :, q4 * CHUNK:(q4 + 1) * CHUNK].rearrange("h r t -> r h t")).then_inc(q_loaded[u], 16)

        @block.gpsimd
        def _(pool):
            pool.sem_inc(y_free, 1)
            with pool.Fori(0, NPAIR) as pr:
                b, g = pr // 2, pr % 2
                for q4 in range(4):
                    pool.wait_ge(y_steps, (pr * 4 + q4) * 2 + 2 + 1)
                    pool.dma_start(Y1[bass.ds(b, 1), q4 * CHUNK:(q4 + 1) * CHUNK, bass.ds(g * GH * DV, GH * DV)].rearrange("a (t p) f -> (a p) t f", p=P),
                                   y[:].rearrange("p t h e -> p t (h e)")).then_inc(y_stored, 16)
                    pool.wait_ge(y_stored, (pr * 4 + q4 + 1) * 16)
                    pool.sem_inc(y_free, 1)
            pool.wait_ge(y_stored, 16 * 16)

        @block.scalar
        def _(act):
            act.sem_inc(o_copied, 1)
            with act.Fori(0, NPAIR) as pr:
                for q4 in range(4):
                    gi = pr * 4 + q4
                    act.wait_ge(rows_ready, gi + 1)
                    act.activation(qg[ONE:KR, q4 % 2], t_ps[0:1, :, :], ACT.Copy).then_inc(rows_done, 1)
                    for J in range(NT):
                        for half in range(2):
                            hs = slice(2 * half, 2 * half + 2)
                            act.wait_ge(t_ready, (gi * NT + J) * 2 + half + 1)
                            act.activation(probs[:, J % 2, hs, :], t_ps[:, hs, :], ACT.Exp).then_inc(exp_done, 1)
                    act.wait_ge(pv_done, gi + 1 + 1)
                    act.activation(oT[:], pv_ps[:], ACT.Copy).then_inc(o_copied, 1)

        @block.tensor
        def _(pe):
            pe.sem_inc(pv_done, 1)
            pe.wait_ge(fixed_set, 3)
            with pe.Fori(0, NPAIR) as pr:
                pe.wait_ge(k_loaded, pr * 64 + 64)
                for q4 in range(4):
                    gi = pr * 4 + q4
                    u = q4 % 2
                    pe.wait_ge(q_loaded[u], (pr * 2 + q4 // 2) * 16 + 16)
                    k = 0
                    for h in range(GH):
                        for t in range(4):
                            i0 = (4 * q4 + t) * P
                            for ch in range(NCH):
                                if k >= 2:
                                    pe.wait_ge(max_done, gi * MC + k - 1)
                                near = [x for x in pieces(i0 - BAND, i0 + P + BAND, 0, T) if x[0] // CHUNK == ch]
                                m = pe.matmul(max_ps[:, k % 2, :], qg[0:SR, u, h, t * P:(t + 1) * P], kg[0:SR, h, ch * CHUNK:(ch + 1) * CHUNK],
                                              start=True, stop=not near)
                                for lo, hi in near:
                                    off = i0 - BAND
                                    m = pe.matmul(max_ps[:, k % 2, lo - ch * CHUNK:hi - ch * CHUNK], c.ident[:], bq[:, h, lo - off:hi - off],
                                                  start=False, stop=True)
                                m.then_inc(max_ready, 1)
                                k += 1
                    pe.wait_ge(nm_ready, gi + 1)
                    pe.wait_ge(y_steps, gi * 2 + 1)
                    for h in range(GH):
                        for t in range(4):
                            m = pe.matmul(t_ps[0:1, h, t * P:(t + 1) * P], neg_max[:, h * 4 + t:h * 4 + t + 1], c.ident[:], start=True, stop=True)
                    m.then_inc(rows_ready, 1)
                    pe.wait_ge(rows_done, gi + 1)

                    def scores(J):
                        near = list(pieces(J * P - BAND, J * P + P + BAND, q4 * CHUNK, (q4 + 1) * CHUNK))
                        for h in range(GH):
                            if h % 2 == 0 and J >= 1:
                                pe.wait_ge(exp_done, (gi * NT + J - 1) * 2 + h // 2 + 1)
                            m = pe.matmul(t_ps[:, h, :], kg[0:KR, h, J * P:(J + 1) * P], qg[0:KR, u, h, :], start=True, stop=not near)
                            for lo, hi in near:
                                off, q0 = J * P - BAND, q4 * CHUNK
                                m = pe.matmul(t_ps[:, h, lo - q0:hi - q0], c.ident[:], bk[:, h, lo - off:hi - off], start=False, stop=True)
                            if h % 2 == 1:
                                m.then_inc(t_ready, 1)

                    scores(0)
                    for J in range(NT):
                        if J + 1 < NT:
                            scores(J + 1)
                        pe.wait_ge(exp_done, (gi * NT + J) * 2 + 2)
                        if J == 0:
                            pe.wait_ge(o_copied, gi + 1)
                        for h in range(GH):
                            rows = slice(32 * h, 32 * h + 32)
                            pe.matmul(pv_ps[rows, 0, :], vg[:, J, h, :], probs[:, J % 2, h, :], start=(J == 0), stop=(J == NT - 1),
                                      tile_position=(0, 32 * h))
                        for h in range(GH):
                            rows = slice(32 * h, 32 * h + 32)
                            m = pe.matmul(pv_ps[rows, 1, :], c.ones[:, 0:32], probs[:, J % 2, h, :], start=(J == 0), stop=(J == NT - 1),
                                          tile_position=(0, 32 * h))
                        if J == NT - 1:
                            m.then_inc(pv_done, 1)
                    pe.wait_ge(o_copied, gi + 1 + 1)
                    for s in range(2):
                        for t in range(4):
                            m = pe.transpose(t_ps[:, s, t * P:(t + 1) * P], oT[:, s, t * P:(t + 1) * P], c.ident[:])
                    m.then_inc(o_turned, 1)

        @block.vector
        def _(dve):
            dve.sem_inc(y_steps, 1)
            dve.memset(kg[64:96], 0.0).then_inc(fixed_set, 1)
            dve.memset(qg[64:96], 0.0).then_inc(fixed_set, 1)
            dve.memset(kg[96:97], 1.0).then_inc(fixed_set, 1)
            with dve.Fori(0, NPAIR) as pr:
                for q4 in range(4):
                    gi = pr * 4 + q4
                    for k in range(MC):
                        dve.wait_ge(max_ready, gi * MC + k + 1)
                        dve.tensor_reduce(part_max[:, k // NCH, k % NCH:k % NCH + 1], max_ps[:, k % 2, :], AX.X, ALU.max).then_inc(max_done, 1)
                    dve.wait_ge(max_done, (gi + 1) * MC)
                    dve.tensor_reduce(neg_max[:], part_max[:], AX.X, ALU.max, negate=True).then_inc(nm_ready, 1)
                    dve.wait_ge(o_turned, gi + 1)
                    turned = lambda s: t_ps[:, s, :].rearrange("p (t h e) -> p t h e", t=4, h=GH)
                    dve.wait_ge(y_free, gi + 1)
                    dve.reciprocal(recip[:], turned(1)[:, :, :, 0]).then_inc(y_steps, 1)
                    dve.wait_ge(y_steps, gi * 2 + 1 + 1)
                    dve.tensor_tensor(y[:], turned(0), recip[:].rearrange("p t (h a) -> p t h a", a=1).broadcast_to([P, 4, GH, DV]),
                                      ALU.mult).then_inc(y_steps, 1)


def lowrank_ffn(nc, c, XT, X, U1, V1w, b1, U2, V2, b2):
    D, R, F = 256, 64, 1024
    NF = F // P
    with ExitStack() as ctx:
        sb = lambda n, s, d=F32: ctx.enter_context(nc.sbuf_tensor(n, s, d))
        sem = c.sem
        ps = lambda n, s: ctx.enter_context(nc.psum_tensor(n, s, F32))
        u1 = sb("f_u1", [P, 2, R])
        v1 = sb("f_v1", [R, F])
        u2 = sb("f_u2", [P, NF, R])
        v2 = sb("f_v2", [R, D])
        b1_sb = sb("f_b1", [P, NF])
        b2_row = sb("f_b2", [P, D])
        xt = sb("f_xt", [P, 2, 2, CHUNK])
        pT = sb("f_pT", [R, CHUNK])
        hid = sb("f_hid", [P, 2, CHUNK])
        qT = sb("f_qT", [R, CHUNK])
        p_ps = ps("f_p_ps", [P, CHUNK])
        h_ps = ps("f_h_ps", [P, 2, CHUNK])
        q_ps = ps("f_q_ps", [P, CHUNK])
        o_ps = ps("f_o_ps", [P, 4, CHUNK])
        w_loaded, biased, p_ready, p_done, h_ready, h_done, q_ready, q_done, o_ready, o_done = map(sem, (
            "w_loaded", "biased", "p_ready", "p_done", "h_ready", "h_done", "q_ready", "q_done", "o_ready", "o_done"))
        xt_loaded = [sem(f"xt_loaded{u}") for u in range(2)]
        block = ctx.enter_context(nc.Block())

        @block.sync
        def _(sp):
            sp.dma_start(u1[:], U1.rearrange("(h p) r -> p h r", p=P)).then_inc(w_loaded, 16)
            sp.dma_start(v1[:], V1w).then_inc(w_loaded, 16)
            sp.dma_start(u2[:], U2.rearrange("(n p) r -> p n r", p=P)).then_inc(w_loaded, 16)
            sp.dma_start(v2[:], V2).then_inc(w_loaded, 16)
            sp.dma_start(b1_sb[:], b1.rearrange("(n p) -> p n", p=P), allow_slow_non_contiguous=True).then_inc(w_loaded, 16)
            sp.dma_start(b2_row[:], b2.rearrange("(a n) -> a n", a=1).broadcast_to([P, D])).then_inc(w_loaded, 16)
            with sp.Fori(0, 4) as it:
                for u in range(2):
                    ch = it * 2 + u
                    sp.wait_ge(p_ready, ch + 1)
                    sp.dma_start(xt[:, u, :, :], XT[bass.ds(ch, 1), :, :, :].rearrange("a p h t -> (a p) h t")).then_inc(xt_loaded[u], 16)

        @block.gpsimd
        def _(pool):
            pool.wait_ge(w_loaded, 96)
            pool.tensor_tensor(X[:], X[:], b2_row[:].rearrange("p (a n) -> p a n", a=1).broadcast_to([P, 32, D]), ALU.add).then_inc(biased, 1)

        @block.scalar
        def _(act):
            act.wait_ge(w_loaded, 96)
            with act.Fori(0, 8) as ch:
                act.wait_ge(p_ready, ch + 3)
                act.activation(pT[:], p_ps[0:R, :], ACT.Copy).then_inc(p_done, 1)
                for f in range(NF):
                    act.wait_ge(h_ready, ch * NF + f + 1)
                    act.activation(hid[:, f % 2, :], h_ps[:, f % 2, :], ACT.Gelu_apprx_tanh, bias=b1_sb[:, f:f + 1]).then_inc(h_done, 1)
                act.wait_ge(q_ready, ch + 1)
                act.activation(qT[:], q_ps[0:R, :], ACT.Copy).then_inc(q_done, 1)

        @block.tensor
        def _(pe):
            pe.wait_ge(w_loaded, 96)
            pe.sem_inc(p_ready, 2)
            with pe.Fori(0, 4) as it:
                for u in range(2):
                    ch = it * 2 + u
                    pe.wait_ge(xt_loaded[u], it * 16 + 16)
                    for half in range(2):
                        m = pe.matmul(p_ps[0:R, :], u1[:, half, :], xt[:, u, half, :], start=(half == 0), stop=(half == 1))
                    m.then_inc(p_ready, 1)
                    pe.wait_ge(p_done, ch + 1)

                    def hidden(f):
                        pe.matmul(h_ps[:, f % 2, :], v1[:, f * P:(f + 1) * P], pT[:], start=True, stop=True).then_inc(h_ready, 1)

                    hidden(0)
                    for f in range(NF):
                        if f + 1 < NF:
                            hidden(f + 1)
                        pe.wait_ge(h_done, ch * NF + f + 1)
                        m = pe.matmul(q_ps[0:R, :], u2[:, f, :], hid[:, f % 2, :], start=(f == 0), stop=(f == NF - 1))
                    m.then_inc(q_ready, 1)
                    pe.wait_ge(q_done, ch + 1)
                    pe.wait_ge(o_done, ch + 1)
                    for t in range(4):
                        m = pe.matmul(o_ps[:, t, 0:D], qT[:, t * P:(t + 1) * P], v2[:], start=True, stop=True)
                    m.then_inc(o_ready, 1)

        @block.vector
        def _(dve):
            dve.sem_inc(o_done, 1)
            dve.wait_ge(biased, 1)
            with dve.Fori(0, 8) as ch:
                dve.wait_ge(o_ready, ch + 1)
                dve.tensor_tensor(X[:, bass.ds(ch * 4, 4), :], o_ps[:, :, 0:D], X[:, bass.ds(ch * 4, 4), :], ALU.add).then_inc(o_done, 1)


def build(nc, x, w_attn, b_attn, w_proj, b_proj, w_red, wg, w1, b1, w2, b2,
          W_qk, W_v, W_out, b_out, conv, U1, V1w, fb1, U2, V2, fb2, out):
    scratch = lambda n, s, d=F32: nc.dram_tensor(n, s, d, kind="Internal").ap()
    XT = scratch("XT", (8, P, 2, CHUNK))
    QS0 = scratch("QS0", (32, 96, 2048), BF16)
    KS0 = scratch("KS0", (32, 96, 2048), BF16)
    V0 = scratch("V0", (2, P, 16, 16, 32))
    Y0 = scratch("Y0", (2, 2048, 256))
    XT1 = scratch("XT1", (8, P, 2, CHUNK))
    QA1 = scratch("QA1", (16, 80, 2048))
    KA1 = scratch("KA1", (16, 80, 2048))
    V1 = scratch("V1", (2, P, 16, 8, 32))
    Y1 = scratch("Y1", (2, 2048, 256))
    EXT = scratch("EXT", (P, 16 * (BW + P - 1)))
    BQ = scratch("BQ", (8, P, BW))
    BK = scratch("BK", (8, P, BW))
    tokens = lambda a: a.rearrange("b (n p) d -> p (b n) d", p=P)
    with ExitStack() as ctx:
        sb = lambda n, s, d=F32: ctx.enter_context(nc.sbuf_tensor(n, s, d))

        class c:
            ident = sb("ident", [P, P])
            ident_bf = sb("ident_bf", [P, P], BF16)
            before = sb("before", [P, P])
            ones = sb("ones", [P, P])

        taken = []
        c.stage = 0

        def sem(name):
            taken.append(nc.alloc_semaphore(name=f"s{c.stage}_{name}"))
            return taken[-1]

        c.sem = sem
        c.passed = ctx.enter_context(nc.semaphore("passed"))
        X = sb("X", [P, 32, 256])
        x_moved = ctx.enter_context(nc.semaphore("x_moved"))
        build_constants(nc, c)
        with nc.Block() as block:
            @block.sync
            def _(sp):
                sp.dma_start(X[:], tokens(x)).then_inc(x_moved, 16)
                sp.wait_ge(x_moved, 16)
        stages = (
            (layernorm_transpose, "l0", X, XT),
            (project_qkv0, XT, w_attn, b_attn, QS0, KS0, V0),
            (experts_ffn, XT, X, w_red, wg, w1, b1, w2, b2),
            (selective_attention, QS0, KS0, V0, Y0),
            (project_out, "l0", Y0, X, w_proj, b_proj, True),
            (layernorm_transpose, "l1", X, XT1),
            (project_qkv1, XT1, W_qk, W_v, QA1, KA1, V1),
            (bias_operands, conv, QA1, KA1, EXT, BQ, BK),
            (lowrank_ffn, XT1, X, U1, V1w, fb1, U2, V2, fb2),
            (relative_attention, QA1, KA1, V1, BQ, BK, Y1),
            (project_out, "l1", Y1, X, W_out, b_out, False),
        )
        for c.stage, (stage, *operands) in enumerate(stages):
            stage(nc, c, *operands)
            nc.clear_and_free_semaphores(taken)
            taken.clear()
            nc.all_engine_barrier()
        with nc.Block() as block:
            @block.sync
            def _(sp):
                sp.dma_start(tokens(out), X[:]).then_inc(x_moved, 16)
                sp.wait_ge(x_moved, 32)


_INS = ['L0_attn_x', 'L0_attn_w_attn', 'L0_attn_b_attn', 'L0_attn_w_proj', 'L0_attn_b_proj', 'L0_ffn_w_red', 'L0_ffn_wg',
        'L0_ffn_w1', 'L0_ffn_b1', 'L0_ffn_w2', 'L0_ffn_b2', 'L1_attn_W_qk', 'L1_attn_W_v', 'L1_attn_W_out', 'L1_attn_b_out',
        'L1_attn_conv', 'L1_ffn_U1', 'L1_ffn_V1', 'L1_ffn_b1', 'L1_ffn_U2', 'L1_ffn_V2', 'L1_ffn_b2']


def kernel(**inputs):
    import numpy as np
    import concourse.bacc as bacc
    from concourse.bass_utils import run_bass_kernel_spmd

    nc = bacc.Bacc("TRN2", target_bir_lowering=False, num_devices=1)
    arrays, args = {}, []
    for name in _INS:
        a = np.ascontiguousarray(inputs[name])
        arrays[f"in_{name}_dram"] = a
        args.append(nc.dram_tensor(f"in_{name}_dram", a.shape, mybir.dt.from_np(a.dtype), kind="ExternalInput").ap())
    out = nc.dram_tensor("out_dram", (2, 2048, 256), F32, kind="ExternalOutput").ap()
    build(nc, *args, out)
    r = run_bass_kernel_spmd(nc, [arrays], core_ids=[0])
    return r.results[0]["out_dram"]
```

```python
from contextlib import ExitStack

import concourse.bass as bass
from concourse import mybir

F32 = mybir.dt.float32
BF16 = mybir.dt.bfloat16
I32 = mybir.dt.int32
ALU = mybir.AluOpType
ACT = mybir.ActivationFunctionType
AX = mybir.AxisListType

P = 128
CHUNK = 512
EPS = 1e-5
BIG = 1e30


def hold(engine, c):
    engine.sem_inc(c.passed, 1)


def build_constants(nc, c):
    with nc.semaphore("const_filled") as filled, nc.semaphore("const_made") as made, nc.Block() as block:
        @block.gpsimd
        def _(pool):
            pool.memset(c.ident[:], 0.0).then_inc(filled, 1)
            pool.memset(c.before[:], 1.0).then_inc(filled, 1)
            pool.memset(c.ones[:], 1.0).then_inc(filled, 1)
            pool.wait_ge(filled, 3)
            pool.affine_select(out=c.ident[:], in_=c.ident[:], compare_op=ALU.not_equal, fill=1.0,
                               base=0, pattern=[[-1, P]], channel_multiplier=1).then_inc(made, 1)
            pool.affine_select(out=c.before[:], in_=c.before[:], compare_op=ALU.is_gt, fill=0.0,
                               base=0, pattern=[[1, P]], channel_multiplier=-1).then_inc(made, 1)
            pool.wait_ge(made, 2)
            pool.tensor_copy(c.ident_bf[:], c.ident[:]).then_inc(made, 1)


def layernorm_transpose(nc, c, layer, X, XT):
    with ExitStack() as ctx:
        sb = lambda n, s, d=F32: ctx.enter_context(nc.sbuf_tensor(f"{layer}_{n}", s, d))
        sem = lambda n: c.sem(f"{layer}_{n}")
        stats = sb("ln_stats", [P, 2, 4, 6])
        meanvar = sb("ln_meanvar", [P, 2, 4, 2])
        std = sb("ln_std", [P, 2, 4])
        rstd = sb("ln_rstd", [P, 2, 4])
        newton = sb("ln_newton", [P, 2, 4])
        eps = sb("ln_eps", [P, 1])
        xn = sb("ln_xn", [P, 2, 4, 256])
        xt = sb("ln_xt", [P, 2, 2, CHUNK])
        xt_ps = ctx.enter_context(nc.psum_tensor(f"{layer}_ln_xt_ps", [P, 2, 2, CHUNK], F32))
        eps_set, stats_done, aggr_done, std_done = sem("eps_set"), sem("stats_done"), sem("aggr_done"), sem("std_done")
        rstd_done, xn_ready, xt_ready, xt_copied, xt_stored = (
            sem("rstd_done"), sem("xn_ready"), sem("xt_ready"), sem("xt_copied"), [sem(f"xt_stored{u}") for u in range(2)])
        block = ctx.enter_context(nc.Block())

        @block.vector
        def _(dve):
            dve.memset(eps[:], EPS).then_inc(eps_set, 1)
            with dve.Fori(0, 4) as it:
                for u in range(2):
                    g = it * 2 + u
                    for t in range(4):
                        last = dve.bn_stats(stats[:, u, t, :], X[:, bass.ds(g * 4 + t, 1), :])
                    last.then_inc(stats_done, 1)
                    dve.wait_ge(stats_done, g + 1)
                    hold(dve, c)
                    for t in range(4):
                        last = dve.bn_aggr(meanvar[:, u, t, :], stats[:, u, t, :])
                    last.then_inc(aggr_done, 1)
                    dve.wait_ge(std_done, g + 1)
                    dve.reciprocal(rstd[:, u, :], std[:, u, :]).then_inc(rstd_done, 1)
                    dve.wait_ge(rstd_done, g * 5 + 1)
                    dve.scalar_tensor_tensor(newton[:, u, :], meanvar[:, u, :, 1], EPS, rstd[:, u, :],
                                             ALU.add, ALU.mult).then_inc(rstd_done, 1)
                    dve.wait_ge(rstd_done, g * 5 + 2)
                    dve.tensor_tensor(newton[:, u, :], newton[:, u, :], rstd[:, u, :], ALU.mult).then_inc(rstd_done, 1)
                    dve.wait_ge(rstd_done, g * 5 + 3)
                    dve.tensor_scalar(newton[:, u, :], newton[:, u, :], -0.5, 1.5, ALU.mult, ALU.add).then_inc(rstd_done, 1)
                    dve.wait_ge(rstd_done, g * 5 + 4)
                    dve.tensor_tensor(rstd[:, u, :], newton[:, u, :], rstd[:, u, :], ALU.mult).then_inc(rstd_done, 1)
                    dve.wait_ge(rstd_done, g * 5 + 5)
                    dve.wait_ge(xt_ready, g + 1)
                    for t in range(4):
                        last = dve.tensor_scalar(xn[:, u, t, :], X[:, bass.ds(g * 4 + t, 1), :],
                                                 meanvar[:, u, t, 0:1], rstd[:, u, t:t + 1],
                                                 ALU.subtract, ALU.mult)
                    last.then_inc(xn_ready, 1)

        @block.scalar
        def _(act):
            act.wait_ge(eps_set, 1)
            with act.Fori(0, 4) as it:
                for u in range(2):
                    g = it * 2 + u
                    act.wait_ge(aggr_done, g + 1)
                    act.activation(std[:, u, :], meanvar[:, u, :, 1], ACT.Sqrt, bias=eps[:, 0:1]).then_inc(std_done, 1)
                    act.wait_ge(xt_ready, g + 3)
                    act.wait_ge(xt_stored[u], it * 16 + 16)
                    act.activation(xt[:, u, :, :], xt_ps[:, u, :, :], ACT.Copy).then_inc(xt_copied, 1)

        @block.sync
        def _(sp):
            for u in range(2):
                sp.sem_inc(xt_stored[u], 16)
            with sp.Fori(0, 4) as it:
                for u in range(2):
                    g = it * 2 + u
                    sp.wait_ge(xt_copied, g + 1)
                    sp.dma_start(XT[bass.ds(g, 1), :, :, :].rearrange("a p h t -> (a p) h t"), xt[:, u, :, :]).then_inc(xt_stored[u], 16)
            for u in range(2):
                sp.wait_ge(xt_stored[u], 5 * 16)

        @block.tensor
        def _(pe):
            pe.sem_inc(xt_ready, 2)
            with pe.Fori(0, 4) as it:
                for u in range(2):
                    g = it * 2 + u
                    pe.wait_ge(xn_ready, g + 1)
                    for half in range(2):
                        for t in range(4):
                            last = pe.transpose(xt_ps[:, u, half, t * P:(t + 1) * P],
                                                xn[:, u, t, half * P:(half + 1) * P], c.ident[:])
                    last.then_inc(xt_ready, 1)


def split3(dve, steps, n, full, high, mid, low, rest):
    dve.tensor_copy(high, full).then_inc(steps, 1)
    dve.wait_ge(steps, n + 1)
    dve.tensor_tensor(rest, full, high, ALU.subtract).then_inc(steps, 1)
    dve.wait_ge(steps, n + 2)
    dve.tensor_copy(mid, rest).then_inc(steps, 1)
    dve.wait_ge(steps, n + 3)
    dve.tensor_tensor(low, rest, mid, ALU.subtract).then_inc(steps, 1)


def project_qkv0(nc, c, XT, w_attn, b_attn, QS0, KS0, V0):
    NH, HD = 16, 16
    C = NH * HD
    SCALE = HD ** -0.5
    with ExitStack() as ctx:
        sb = lambda n, s, d=F32: ctx.enter_context(nc.sbuf_tensor(n, s, d))
        sem = c.sem
        w_rows = sb("p0_w_rows", [P, 6, C])
        wT = sb("p0_wT", [P, 2, 3 * C])
        bias = sb("p0_bias", [P, 4])
        bias_v = sb("p0_bias_v", [P, C])
        xt = sb("p0_xt", [P, 2, 2, CHUNK])
        full = sb("p0_full", [P, 4, CHUNK])
        high = sb("p0_high", [P, 4, CHUNK], BF16)
        mid = sb("p0_mid", [P, 4, CHUNK], BF16)
        low = sb("p0_low", [P, 4, CHUNK], BF16)
        rest = sb("p0_rest", [P, CHUNK])
        v_sb = sb("p0_v", [P, 2, 4, NH, 32])
        proj_ps = ctx.enter_context(nc.psum_tensor("p0_proj", [P, 4, CHUNK], F32))
        v_ps = ctx.enter_context(nc.psum_tensor("p0_v_ps", [P, 4, CHUNK], F32))
        w_loaded, wT_ready, wT_copied, bias_ready = sem("w_loaded"), sem("wT_ready"), sem("wT_copied"), sem("bias_ready")
        xt_loaded = [sem(f"xt_loaded{u}") for u in range(2)]
        proj_ready, full_ready, steps = sem("proj_ready"), sem("full_ready"), sem("split_steps")
        split_stored = [sem(f"split_stored{m}") for m in range(4)]
        v_ready, v_copied, ones_set = sem("v_ready"), sem("v_copied"), sem("ones_set")
        v_stored = [sem(f"v_stored{u}") for u in range(2)]
        block = ctx.enter_context(nc.Block())

        @block.sync
        def _(sp):
            sp.dma_start(w_rows[:], w_attn.rearrange("(n p) d -> p n d", p=P)).then_inc(w_loaded, 16)
            sp.dma_start(bias[:], b_attn[0:2 * C].rearrange("(n p) -> p n", p=P),
                         allow_slow_non_contiguous=True).then_inc(w_loaded, 16)
            sp.dma_start(bias_v[:], b_attn[2 * C:3 * C].rearrange("(a n) -> a n", a=1).broadcast_to([P, C])).then_inc(w_loaded, 16)
            with sp.Fori(0, 4) as it:
                for u in range(2):
                    ch = it * 2 + u
                    b, t0 = ch // 4, (ch % 4) * CHUNK
                    for m in range(4):
                        sp.wait_ge(steps, ch * 16 + m * 4 + 4 + 1)
                        dst = QS0 if m < 2 else KS0
                        order = (high, high, high, mid, mid, low) if m < 2 else (high, mid, low, high, mid, high)
                        for term, part in enumerate(order):
                            sp.dma_start(dst[bass.ds(b * NH + 8 * (m % 2), 8), term * HD:(term + 1) * HD, bass.ds(t0, CHUNK)],
                                           part[:, m, :]).then_inc(split_stored[m], 16)
                    sp.wait_ge(v_copied, ch * 4 + 4 + 1)
                    sp.dma_start(V0[bass.ds(b, 1), :, bass.ds((ch % 4) * 4, 4), :, :].rearrange("a p j h e -> (a p) j h e"),
                                   v_sb[:, u]).then_inc(v_stored[u], 16)
            for m in range(4):
                sp.wait_ge(split_stored[m], (8 + 1) * 6 * 16)
            for u in range(2):
                sp.wait_ge(v_stored[u], (4 + 1) * 16)

        @block.gpsimd
        def _(pool):
            pool.memset(v_sb[:], 1.0).then_inc(ones_set, 1)
            with pool.Fori(0, 4) as it:
                for u in range(2):
                    ch = it * 2 + u
                    pool.wait_ge(v_ready, ch * 4 + 4)
                    pool.dma_start(xt[:, u, :, :], XT[bass.ds(ch, 1), :, :, :].rearrange("a p h t -> (a p) h t")).then_inc(xt_loaded[u], 16)

        @block.scalar
        def _(act):
            act.sem_inc(full_ready, 1)
            act.wait_ge(w_loaded, 48)
            for n in range(6):
                act.wait_ge(wT_ready, n + 1)
                act.activation(wT[:, :, n * P:(n + 1) * P], v_ps[:, n % 4, 0:2 * P].rearrange("p (h o) -> p h o", h=2),
                               ACT.Copy).then_inc(wT_copied, 1)
            act.activation(bias[:, 0:2], bias[:, 0:2], ACT.Copy, scale=SCALE).then_inc(bias_ready, 1)
            act.wait_ge(bias_ready, 1)
            with act.Fori(0, 8) as ch:
                for m in range(4):
                    act.wait_ge(proj_ready, ch * 4 + m + 1)
                    act.wait_ge(steps, ch * 16 + 1)
                    act.activation(full[:, m, :], proj_ps[:, m, :], ACT.Identity,
                                   bias=bias[:, m:m + 1], scale=SCALE if m < 2 else 1.0).then_inc(full_ready, 1)

        @block.vector
        def _(dve):
            dve.sem_inc(steps, 1)
            dve.sem_inc(v_copied, 1)
            dve.wait_ge(ones_set, 1)
            for m in range(4):
                dve.sem_inc(split_stored[m], 6 * 16)
            for u in range(2):
                dve.sem_inc(v_stored[u], 16)
            with dve.Fori(0, 4) as it:
                for u in range(2):
                    ch = it * 2 + u
                    for m in range(4):
                        dve.wait_ge(full_ready, ch * 4 + m + 1 + 1)
                        dve.wait_ge(split_stored[m], (ch + 1) * 6 * 16)
                        split3(dve, steps, 1 + ch * 16 + m * 4, full[:, m, :], high[:, m, :], mid[:, m, :], low[:, m, :], rest[:])
                    dve.wait_ge(v_stored[u], (it + 1) * 16)
                    for t in range(4):
                        dve.wait_ge(v_ready, 8 + ch * 4 + t + 1)
                        dve.tensor_tensor(v_sb[:, u, t, :, 0:HD], v_ps[:, t, 0:C].rearrange("p (h e) -> p h e", h=NH),
                                          bias_v[:].rearrange("p (h e) -> p h e", h=NH), ALU.add).then_inc(v_copied, 1)

        @block.tensor
        def _(pe):
            pe.wait_ge(w_loaded, 48)
            for n in range(6):
                if n >= 4:
                    pe.wait_ge(wT_copied, n - 3)
                for half in range(2):
                    last = pe.transpose(v_ps[:, n % 4, half * P:(half + 1) * P], w_rows[:, n, half * P:(half + 1) * P], c.ident[:])
                last.then_inc(wT_ready, 1)
            pe.wait_ge(wT_copied, 6)
            pe.sem_inc(v_ready, 8)
            with pe.Fori(0, 4) as it:
                for u in range(2):
                    ch = it * 2 + u
                    pe.wait_ge(xt_loaded[u], it * 16 + 16)
                    pe.wait_ge(full_ready, ch * 4 + 1)
                    for m in range(4):
                        for half in range(2):
                            last = pe.matmul(proj_ps[:, m, :], wT[:, half, m * P:(m + 1) * P], xt[:, u, half, :],
                                             start=(half == 0), stop=(half == 1))
                        last.then_inc(proj_ready, 1)
                    pe.wait_ge(v_copied, ch * 4 + 1)
                    for t in range(4):
                        for half in range(2):
                            last = pe.matmul(v_ps[:, t, 0:C], xt[:, u, half, t * P:(t + 1) * P],
                                             wT[:, half, 2 * C:3 * C], start=(half == 0), stop=(half == 1))
                        last.then_inc(v_ready, 1)


def experts_and_penalties(nc, c, XT, X, w_red, wg, w1, b1, w2, b2, QS0, KS0, FFQ, FFK):
    NB, T, NH, HD = 2, 2048, 16, 16
    ROWS = 6 * HD
    BUDGET = int(T * 0.2) - 1
    tri = lambda k: k * (k + 1) // 2
    ff_chunks = lambda b, q4, t: b * 40 + 4 * tri(q4) + t * (q4 + 1)
    blocks = lambda b, q4: b * 4 + q4
    NE, F, GD, D = 8, 1024, 16, 256
    NT = 32
    NF = F // P
    with ExitStack() as ctx:
        sb = lambda n, s, d=F32: ctx.enter_context(nc.sbuf_tensor(n, s, d))
        sem = c.sem
        ps = lambda n, s: ctx.enter_context(nc.psum_tensor(n, s, F32))
        w_red_sb = sb("e_w_red", [P, 2, GD])
        wg_sb = sb("e_wg", [NE, GD])
        wg_sq = sb("e_wg_sq", [NE, GD])
        wg_norm = sb("e_wg_norm", [NE, 1])
        wgT = sb("e_wgT", [GD, NE])
        xt = sb("e_xt", [P, 2, 2, CHUNK])
        redT = sb("e_redT", [GD, 2, CHUNK])
        logits = sb("e_logits", [P, NT, NE])
        gates = sb("e_gates", [P, NT, NE])
        order = sb("e_order", [P, NE])
        col = sb("e_col", [P, NT])
        b2_sb = sb("e_b2", [NE, D])
        gT = sb("e_gT", [NE, 2, P])
        w1_sb = sb("e_w1", [P, 2, 2, F])
        w2_sb = sb("e_w2", [P, 2, NF, D])
        b1_sb = sb("e_b1", [P, 2, NF])
        hid = sb("e_hid", [P, 2, CHUNK])
        y_sb = sb("e_y_sb", [P, 2, 4, D])
        q0 = sb("s_q0", [ROWS, CHUNK], BF16)
        k0 = sb("s_k0", [ROWS, T], BF16)
        S = sb("s_S", [P, T])
        carry = sb("s_carry", [P, T])
        FF = sb("s_FF", [P, 4, T])
        FFT = sb("s_FFT", [P, T // P, CHUNK])
        thr = sb("s_thr", [P, 4], I32)
        cand = sb("s_cand", [P, 4], I32)
        bit = sb("s_bit", [P, 4], I32)
        below = sb("s_below", [P, 4])
        take = sb("s_take", [P, 4], I32)
        need = sb("s_need", [P, 4])
        less = sb("s_less", [P, T], BF16)
        equal = sb("s_equal", [P, T], BF16)
        h_ps = ps("e_h_ps", [P, 2, CHUNK])
        y_ps = ps("e_y_ps", [P, 4, CHUNK])
        small_loaded, norm, redT_ready, redT_done, logit_ready, logit_done = (
            sem("small_loaded"), sem("norm"), sem("redT_ready"), sem("redT_done"), sem("logit_ready"), sem("logit_done"))
        pick, gT_ready, gT_done, bias_ready, bias_done = sem("pick"), sem("gT_ready"), sem("gT_done"), sem("bias_ready"), sem("bias_done")
        xt_loaded = [sem(f"xt_loaded{u}") for u in range(2)]
        xt_again = [sem(f"xt_again{u}") for u in range(2)]
        w_loaded = [sem(f"w_loaded{u}") for u in range(2)]
        h_ready, h_done, y_ready, y_done = sem("h_ready"), sem("h_done"), sem("y_ready"), sem("y_done")
        order_set, exp_done, y_scaled, y_added = sem("order_set"), sem("exp_done"), sem("y_scaled"), sem("y_added")
        head0_loaded, s_raw, s_pos, s_masked = sem("head0_loaded"), sem("s_raw"), sem("s_pos"), sem("s_masked")
        sums_ready, ff_done, ff_masked, chain = sem("sums_ready"), sem("ff_done"), sem("ff_masked"), sem("chain")
        kept, ff_final, fft_ready, fft_done = sem("kept"), sem("ff_final"), sem("fft_ready"), sem("fft_done")
        ff_stored, fft_stored, ff_free = sem("ff_stored"), sem("fft_stored"), sem("ff_free")
        NBIT = 31
        first_tile = lambda q4: 3 if q4 == 0 else 0
        block_steps = lambda q4: 2 + NBIT * (7 - first_tile(q4)) + 7 * (4 - first_tile(q4))
        sel_steps = lambda b, q4: b * sum(map(block_steps, range(4))) + sum(map(block_steps, range(q4)))

        with nc.Block() as block:
            @block.sync
            def _(sp):
                sp.dma_start(w_red_sb[:], w_red.rearrange("(h p) r -> p h r", p=P)).then_inc(small_loaded, 16)
                sp.dma_start(wg_sb[:], wg).then_inc(small_loaded, 16)
                sp.dma_start(b2_sb[:], b2).then_inc(small_loaded, 16)
                with sp.Fori(0, 4) as it:
                    for u in range(2):
                        ch = it * 2 + u
                        sp.wait_ge(redT_ready, ch + 1)
                        sp.dma_start(xt[:, u, :, :], XT[bass.ds(ch, 1), :, :, :].rearrange("a p h t -> (a p) h t")).then_inc(xt_loaded[u], 16)

            @block.gpsimd
            def _(pool):
                pool.iota(order[:], pattern=[[1, NE]], base=-NE, channel_multiplier=0,
                          allow_small_or_imprecise_dtypes=True).then_inc(order_set, 1)

            @block.scalar
            def _(act):
                act.wait_ge(norm, 1)
                act.activation(wg_norm[:], wg_norm[:], ACT.Sqrt).then_inc(norm, 1)
                with act.Fori(0, 4) as it:
                    for u in range(2):
                        ch = it * 2 + u
                        act.wait_ge(redT_ready, ch + 3)
                        act.wait_ge(logit_ready, ch + 1)
                        act.activation(redT[:, u, :], h_ps[0:GD, u, :], ACT.Copy).then_inc(redT_done, 1)
                act.wait_ge(pick, 2)
                act.activation(gates[:], gates[:], ACT.Exp).then_inc(exp_done, 1)

            @block.tensor
            def _(pe):
                pe.sem_inc(logit_ready, 1)
                pe.sem_inc(redT_ready, 2)
                pe.wait_ge(norm, 5)
                pe.transpose(y_ps[0:GD, 3, 0:NE], wg_sb[:], c.ident[0:NE, 0:NE]).then_inc(logit_ready, 1)
                pe.wait_ge(norm, 6)
                with pe.Fori(0, 4) as it:
                    for u in range(2):
                        ch = it * 2 + u
                        pe.wait_ge(xt_loaded[u], it * 16 + 16)
                        for half in range(2):
                            m = pe.matmul(h_ps[0:GD, u, :], w_red_sb[:, half, :], xt[:, u, half, :], start=(half == 0), stop=(half == 1))
                        m.then_inc(redT_ready, 1)
                        pe.wait_ge(redT_done, ch + 1)
                        pe.wait_ge(logit_done, ch + 1)
                        for t in range(4):
                            m = pe.matmul(y_ps[:, t, 0:NE], redT[:, u, t * P:(t + 1) * P], wgT[:], start=True, stop=True)
                        m.then_inc(logit_ready, 1)

            @block.vector
            def _(dve):
                dve.sem_inc(logit_done, 1)
                dve.wait_ge(small_loaded, 48)
                dve.tensor_tensor_reduce(wg_sq[:], wg_sb[:], wg_sb[:], 1.0, 0.0, ALU.mult, ALU.add, accum_out=wg_norm[:]).then_inc(norm, 1)
                dve.wait_ge(norm, 2)
                dve.tensor_scalar(wg_norm[:], wg_norm[:], 1e-4, None, ALU.max).then_inc(norm, 1)
                dve.wait_ge(norm, 3)
                dve.reciprocal(wg_norm[:], wg_norm[:]).then_inc(norm, 1)
                dve.wait_ge(norm, 4)
                dve.tensor_scalar(wg_sb[:], wg_sb[:], wg_norm[:, 0:1], None, ALU.mult).then_inc(norm, 1)
                dve.wait_ge(logit_ready, 1 + 1)
                dve.tensor_copy(wgT[:], y_ps[0:GD, 3, 0:NE]).then_inc(norm, 1)
                with dve.Fori(0, 8) as ch:
                    dve.wait_ge(logit_ready, ch + 2 + 1)
                    dve.tensor_copy(logits[:, bass.ds(ch * 4, 4), :], y_ps[:, :, 0:NE]).then_inc(logit_done, 1)
                dve.wait_ge(logit_done, 8 + 1)
                over = lambda a: a[:].rearrange("p (t a) -> p t a", a=1).broadcast_to([P, NT, NE])
                dve.tensor_reduce(col[:], logits[:], AX.X, ALU.max).then_inc(pick, 1)
                dve.wait_ge(pick, 1)
                dve.tensor_tensor(gates[:], logits[:], over(col), ALU.subtract).then_inc(pick, 1)
                dve.wait_ge(exp_done, 1)
                dve.tensor_reduce(col[:], gates[:], AX.X, ALU.add).then_inc(pick, 1)
                dve.wait_ge(pick, 3)
                dve.reciprocal(col[:], col[:]).then_inc(pick, 1)
                dve.wait_ge(pick, 4)
                dve.tensor_tensor(gates[:], gates[:], over(col), ALU.mult).then_inc(pick, 1)
                dve.wait_ge(pick, 5)
                dve.tensor_reduce(col[:], gates[:], AX.X, ALU.max).then_inc(pick, 1)
                dve.wait_ge(pick, 6)
                dve.tensor_tensor(logits[:], gates[:], over(col), ALU.is_equal).then_inc(pick, 1)
                dve.wait_ge(pick, 7)
                dve.wait_ge(order_set, 1)
                dve.tensor_tensor(logits[:], logits[:], order[:].rearrange("p (a e) -> p a e", a=1).broadcast_to([P, NT, NE]), ALU.mult).then_inc(pick, 1)
                dve.wait_ge(pick, 8)
                dve.tensor_reduce(col[:], logits[:], AX.X, ALU.min).then_inc(pick, 1)
                dve.wait_ge(pick, 9)
                dve.tensor_tensor(logits[:], logits[:], over(col), ALU.is_equal).then_inc(pick, 1)
                dve.wait_ge(pick, 10)
                dve.tensor_tensor(gates[:], gates[:], logits[:], ALU.mult).then_inc(pick, 1)

        with nc.Block() as block:
            @block.sync
            def _(sp):
                with sp.Fori(0, NB) as b:
                    for q4 in range(4):
                        e, u, W = blocks(b, q4), q4 % 2, CHUNK * (q4 + 1)
                        sp.wait_ge(y_ready, e * 8 + 8)
                        sp.dma_start(w1_sb[:, u], w1[bass.ds(e, 1), :, :].rearrange("a (h p) f -> (a p) h f", p=P)).then_inc(w_loaded[u], 16)
                        sp.dma_start(w2_sb[:, u], w2[bass.ds(e, 1), :, :].rearrange("a (n p) d -> (a p) n d", p=P)).then_inc(w_loaded[u], 16)
                        sp.dma_start(b1_sb[:, u], b1[bass.ds(e, 1), :].rearrange("a (n p) -> (a p) n", p=P), allow_slow_non_contiguous=True).then_inc(w_loaded[u], 16)
                        sp.wait_ge(s_raw, ff_chunks(b, q4, 0) + 1)
                        sp.dma_start(q0[:], QS0[bass.ds(b * NH, 1), :, q4 * CHUNK:(q4 + 1) * CHUNK].rearrange("a r t -> (a r) t")).then_inc(head0_loaded, 16)
                        sp.dma_start(k0[:, 0:W], KS0[bass.ds(b * NH, 1), :, 0:W].rearrange("a r t -> (a r) t")).then_inc(head0_loaded, 16)
                        with sp.Fori(0, 4) as it:
                            for v in range(2):
                                ch = it * 2 + v
                                sp.wait_ge(h_ready, (e * 8 + ch) * NF + NF)
                                sp.dma_start(xt[:, v, :, :], XT[bass.ds(ch, 1), :, :, :].rearrange("a p h t -> (a p) h t")).then_inc(xt_again[v], 16)

            @block.gpsimd
            def _(pool):
                pool.sem_inc(y_added, 2)
                pool.sem_inc(ff_free, 1)
                with pool.Fori(0, NB) as b:
                    for q4 in range(4):
                        e = blocks(b, q4)
                        for t in range(4):
                            d0 = (4 * q4 + t) * P
                            n = ff_chunks(b, q4, t)
                            pool.wait_ge(s_pos, n + q4 + 1)
                            hold(pool, c)
                            pool.affine_select(out=S[:, d0:d0 + P], in_=S[:, d0:d0 + P], compare_op=ALU.is_gt, fill=0.0,
                                               base=0, pattern=[[-1, P]], channel_multiplier=1).then_inc(s_masked, 1)
                            pool.wait_ge(s_masked, (blocks(b, q4) * 4 + t) * 2 + 1)
                            hold(pool, c)
                            pool.memset(S[:, 0:1], 0.0).then_inc(s_masked, 1)
                            pool.wait_ge(ff_done, n + q4 + 1)
                            hold(pool, c)
                            pool.affine_select(out=FF[:, t, d0:d0 + P], in_=FF[:, t, d0:d0 + P], compare_op=ALU.is_ge, fill=BIG,
                                               base=0, pattern=[[-1, P]], channel_multiplier=1).then_inc(ff_masked, 1)
                        with pool.Fori(0, 4) as it:
                            for v in range(2):
                                n = e * 8 + it * 2 + v
                                rows = bass.ds((it * 2 + v) * 4, 4)
                                pool.wait_ge(y_done, n + 1 + 1)
                                pool.tensor_tensor(y_sb[:, v], y_sb[:, v], gates[:, rows, bass.ds(e, 1)].broadcast_to([P, 4, D]), ALU.mult).then_inc(y_scaled, 1)
                                pool.wait_ge(y_scaled, n + 1)
                                pool.tensor_tensor(X[:, rows, :], X[:, rows, :], y_sb[:, v], ALU.add).then_inc(y_added, 1)
                                pool.wait_ge(y_added, n + 1 + 2)
                        for t in range(4):
                            d0 = (4 * q4 + t) * P
                            pool.wait_ge(kept, blocks(b, q4) + 1)
                            hold(pool, c)
                            pool.affine_select(out=FF[:, t, d0:d0 + P], in_=FF[:, t, d0:d0 + P], compare_op=ALU.not_equal, fill=0.0,
                                               base=0, pattern=[[-1, P]], channel_multiplier=1).then_inc(ff_final, 1)
                        pool.wait_ge(ff_final, (e + 1) * 4)
                        hold(pool, c)
                        for t in range(4):
                            n_keys = (4 * q4 + t + 1) * P
                            pool.dma_start(FFQ[bass.ds(e, 1), :, t, 0:n_keys].rearrange("a p k -> (a p) k"), FF[:, t, 0:n_keys]).then_inc(ff_stored, 16)
                        pool.wait_ge(fft_done, b * 40 + 4 * tri(q4 + 1))
                        hold(pool, c)
                        if q4:
                            pool.dma_start(FFK[bass.ds(e, 1), :, 0:4 * q4, :].rearrange("a p j q -> (a p) j q"), FFT[:, 0:4 * q4, :]).then_inc(fft_stored, 16)
                        for t in range(4):
                            pool.dma_start(FFK[bass.ds(e, 1), :, 4 * q4 + t, t * P:CHUNK].rearrange("a p q -> (a p) q"), FFT[:, 4 * q4 + t, t * P:CHUNK]).then_inc(fft_stored, 16)
                        pool.wait_ge(ff_stored, (e + 1) * 64)
                        pool.sem_inc(ff_free, 1)
                        pool.wait_ge(fft_stored, b * 19 * 16 + (4 * (q4 + 1) + q4) * 16)
                pool.wait_ge(ff_stored, NB * 16 * 16)

            @block.scalar
            def _(act):
                act.sem_inc(y_done, 1)
                with act.Fori(0, NB) as b:
                    for q4 in range(4):
                        e, u = blocks(b, q4), q4 % 2
                        for t in range(4):
                            for ch in range(q4 + 1):
                                n = ff_chunks(b, q4, t) + ch
                                w = min(CHUNK, (4 * q4 + t + 1) * P - ch * CHUNK)
                                act.wait_ge(s_raw, n + 1 + 1)
                                act.wait_ge(sums_ready, ff_chunks(b, q4, t) * 2 + 1)
                                act.activation(S[:, ch * CHUNK:ch * CHUNK + w], h_ps[:, (t * (q4 + 1) + ch) % 2, 0:w], ACT.Relu).then_inc(s_pos, 1)
                        with act.Fori(0, 4) as it:
                            for v in range(2):
                                n = e * 8 + it * 2 + v
                                for f in range(NF):
                                    act.wait_ge(h_ready, n * NF + f + 17)
                                    act.activation(hid[:, f % 2, :], h_ps[:, f % 2, :], ACT.Gelu, bias=b1_sb[:, u, f:f + 1]).then_inc(h_done, 1)
                                act.wait_ge(y_ready, n + 17)
                                act.wait_ge(y_added, n + 1)
                                act.activation(y_sb[:, v], y_ps[:, :, 0:D], ACT.Copy).then_inc(y_done, 1)
                        for J in range(4 * (q4 + 1)):
                            c0 = max(0, J - 4 * q4) * P
                            act.wait_ge(fft_ready, b * 40 + 4 * tri(q4) + J + 1)
                            act.activation(FFT[:, J, c0:CHUNK], y_ps[:, J % 4, c0:CHUNK], ACT.Copy).then_inc(fft_done, 1)

            @block.tensor
            def _(pe):
                pe.sem_inc(h_ready, 2 * NF)
                pe.sem_inc(y_ready, 2 * 8)
                pe.sem_inc(s_raw, 1)
                pe.sem_inc(sums_ready, 1)
                with pe.Fori(0, NB) as b:
                    for q4 in range(4):
                        nch, nj = q4 + 1, 4 * (q4 + 1)
                        e, u = blocks(b, q4), q4 % 2
                        pe.wait_ge(head0_loaded, (blocks(b, q4) + 1) * 32)
                        for t in range(4):
                            n = ff_chunks(b, q4, t)
                            w = lambda ch: min(CHUNK, (4 * q4 + t + 1) * P - ch * CHUNK)
                            for ch in range(nch):
                                k = t * nch + ch
                                if k >= 2:
                                    pe.wait_ge(s_pos, n + ch - 1)
                                pe.matmul(h_ps[:, k % 2, 0:w(ch)], q0[:, t * P:(t + 1) * P], k0[:, ch * CHUNK:ch * CHUNK + w(ch)],
                                          start=True, stop=True).then_inc(s_raw, 1)
                            pe.wait_ge(s_masked, (blocks(b, q4) * 4 + t) * 2 + 2)
                            for ch in range(nch):
                                k = t * nch + ch
                                if k >= 2:
                                    pe.wait_ge(ff_done, n + ch - 1)
                                s = S[:, ch * CHUNK:ch * CHUNK + w(ch)]
                                pe.matmul(y_ps[:, 2 * (k % 2), 0:w(ch)], c.before[:], s, start=True, stop=True).then_inc(sums_ready, 1)
                                pe.matmul(y_ps[:, 2 * (k % 2) + 1, 0:w(ch)], c.ones[:], s, start=True, stop=True).then_inc(sums_ready, 1)
                        pe.wait_ge(ff_done, ff_chunks(b, q4, 4))
                        pe.wait_ge(w_loaded[u], (b * 2 + q4 // 2 + 1) * 48)
                        hold(pe, c)
                        with pe.Fori(0, 4) as it:
                            for v in range(2):
                                n = e * 8 + it * 2 + v
                                pe.wait_ge(xt_again[v], (e * 4 + it) * 16 + 16)

                                def hidden(f):
                                    for half in range(2):
                                        m = pe.matmul(h_ps[:, f % 2, :], w1_sb[:, u, half, f * P:(f + 1) * P], xt[:, v, half, :],
                                                      start=(half == 0), stop=(half == 1))
                                    m.then_inc(h_ready, 1)

                                hidden(0)
                                for f in range(NF):
                                    if f + 1 < NF:
                                        hidden(f + 1)
                                    pe.wait_ge(h_done, n * NF + f + 1)
                                    if f == 0:
                                        pe.wait_ge(y_done, n + 1)
                                    for t in range(4):
                                        m = pe.matmul(y_ps[:, t, 0:D], hid[:, f % 2, t * P:(t + 1) * P], w2_sb[:, u, f, :],
                                                      start=(f == 0), stop=(f == NF - 1))
                                m.then_inc(y_ready, 1)
                        pe.wait_ge(y_done, (e + 1) * 8 + 1)
                        pe.wait_ge(ff_final, (blocks(b, q4) + 1) * 4)
                        for J in range(nj):
                            if J >= 4:
                                pe.wait_ge(fft_done, b * 40 + 4 * tri(q4) + J - 3)
                            for t in range(max(0, J - 4 * q4), 4):
                                last = pe.transpose(y_ps[:, J % 4, t * P:(t + 1) * P], FF[:, t, J * P:(J + 1) * P], c.ident[:])
                            last.then_inc(fft_ready, 1)
                        pe.wait_ge(fft_done, b * 40 + 4 * tri(q4) + nj)

            @block.vector
            def _(dve):
                with dve.Fori(0, NB) as b:
                    for q4 in range(4):
                        nch = q4 + 1
                        bi = blocks(b, q4)
                        dve.wait_ge(ff_free, bi + 1)
                        for t in range(4):
                            for ch in range(nch):
                                n = ff_chunks(b, q4, t) + ch
                                k = t * nch + ch
                                w = min(CHUNK, (4 * q4 + t + 1) * P - ch * CHUNK)
                                dve.wait_ge(sums_ready, n * 2 + 2 + 1)
                                have = min(w, max(0, (4 * q4 + t) * P - ch * CHUNK))
                                if have:
                                    dve.wait_ge(ff_done, n)
                                    old = slice(ch * CHUNK, ch * CHUNK + have)
                                    dve.tensor_tensor(FF[:, t, old], y_ps[:, 2 * (k % 2), 0:have], carry[:, old], ALU.add)
                                    m = dve.tensor_tensor(carry[:, old], y_ps[:, 2 * (k % 2) + 1, 0:have], carry[:, old], ALU.add)
                                if have < w:
                                    new = slice(ch * CHUNK + have, ch * CHUNK + w)
                                    dve.tensor_copy(FF[:, t, new], y_ps[:, 2 * (k % 2), have:w])
                                    m = dve.tensor_copy(carry[:, new], y_ps[:, 2 * (k % 2) + 1, have:w])
                                m.then_inc(ff_done, 1)
                        t0 = first_tile(q4)
                        s0 = sel_steps(b, q4)
                        dve.memset(thr[:], 0).then_inc(chain, 1)
                        dve.memset(bit[:], 1 << (NBIT - 1)).then_inc(chain, 1)
                        dve.wait_ge(ff_masked, (bi + 1) * 4)
                        hold(dve, c)
                        with dve.Fori(0, NBIT) as i:
                            v = s0 + 2 + i * (3 + 4 - t0)
                            dve.wait_ge(chain, v)
                            dve.tensor_tensor(cand[:], thr[:], bit[:], ALU.bitwise_or).then_inc(chain, 1)
                            dve.wait_ge(chain, v + 1)
                            dve.tensor_scalar(bit[:], bit[:], 1, None, ALU.logical_shift_right)
                            for t in range(t0, 4):
                                n_keys = (4 * q4 + t + 1) * P
                                if t >= t0 + 2:
                                    dve.wait_ge(chain, v + t - t0)
                                dve.tensor_scalar((less, equal)[t % 2][:, 0:n_keys], FF[:, t, 0:n_keys], cand[:].bitcast(F32)[:, t:t + 1], 0.0,
                                                  ALU.is_lt, ALU.add, accum_out=below[:, t:t + 1]).then_inc(chain, 1)
                            v += 1 + 4 - t0
                            dve.wait_ge(chain, v)
                            dve.tensor_scalar(take[:, t0:4], below[:, t0:4], BUDGET - 0.5, None, ALU.is_lt).then_inc(chain, 1)
                            dve.wait_ge(chain, v + 1)
                            hold(dve, c)
                            dve.copy_predicated(thr[:, t0:4], take[:, t0:4], cand[:, t0:4]).then_inc(chain, 1)
                        s1 = s0 + 2 + NBIT * (3 + 4 - t0)
                        dve.wait_ge(chain, s1)
                        for t in range(t0, 4):
                            n_keys = (4 * q4 + t + 1) * P
                            th = thr[:].bitcast(F32)[:, t:t + 1]
                            v = s1 + (t - t0) * 7
                            dve.tensor_scalar(equal[:, 0:n_keys], FF[:, t, 0:n_keys], th, None, ALU.is_equal)
                            dve.tensor_scalar(less[:, 0:n_keys], FF[:, t, 0:n_keys], th, 0.0, ALU.is_lt, ALU.add,
                                              accum_out=below[:, t:t + 1]).then_inc(chain, 1)
                            dve.wait_ge(chain, v + 1)
                            dve.tensor_scalar(need[:, t:t + 1], below[:, t:t + 1], -1.0, float(BUDGET), ALU.mult, ALU.add).then_inc(chain, 1)
                            dve.tensor_tensor_scan(S[:, 0:n_keys], c.ones[:, 0:1].broadcast_to([P, n_keys]), equal[:, 0:n_keys], 0.0,
                                                   ALU.mult, ALU.add).then_inc(chain, 1)
                            dve.wait_ge(chain, v + 3)
                            dve.scalar_tensor_tensor(equal[:, 0:n_keys], S[:, 0:n_keys], need[:, t:t + 1], equal[:, 0:n_keys],
                                                     ALU.is_le, ALU.mult).then_inc(chain, 1)
                            dve.wait_ge(chain, v + 4)
                            dve.tensor_tensor(less[:, 0:n_keys], less[:, 0:n_keys], equal[:, 0:n_keys], ALU.add).then_inc(chain, 1)
                            dve.wait_ge(chain, v + 5)
                            dve.tensor_scalar(less[:, 0:n_keys], less[:, 0:n_keys], 0.5, BIG, ALU.is_lt, ALU.mult).then_inc(chain, 1)
                            dve.wait_ge(chain, v + 6)
                            dve.tensor_tensor(FF[:, t, 0:n_keys], FF[:, t, 0:n_keys], less[:, 0:n_keys], ALU.add).then_inc(chain, 1)
                            dve.wait_ge(chain, v + 7)
                        dve.sem_inc(kept, 1)

        with nc.Block() as block:
            @block.tensor
            def _(pe):
                for t in range(NT):
                    pe.transpose(h_ps[0:NE, t % 2, 0:P], gates[:, t, :], c.ident[:]).then_inc(gT_ready, 1)
                    pe.wait_ge(gT_done, t + 1)
                    if t >= 4:
                        pe.wait_ge(bias_done, t - 3)
                    pe.matmul(y_ps[:, t % 4, 0:D], gT[:, t % 2, :], b2_sb[:], start=True, stop=True).then_inc(bias_ready, 1)

            @block.scalar
            def _(act):
                for t in range(NT):
                    act.wait_ge(gT_ready, t + 1)
                    if t >= 2:
                        act.wait_ge(bias_ready, t - 1)
                    act.activation(gT[:, t % 2, :], h_ps[0:NE, t % 2, 0:P], ACT.Copy).then_inc(gT_done, 1)

            @block.vector
            def _(dve):
                for t in range(NT):
                    dve.wait_ge(bias_ready, t + 1)
                    dve.tensor_tensor(X[:, t, :], y_ps[:, t % 4, 0:D], X[:, t, :], ALU.add).then_inc(bias_done, 1)


def selective_attention(nc, c, QS0, KS0, V0, FFQ, FFK, Y0):
    NB, T, NH, HD = 2, 2048, 16, 16
    ROWS = 6 * HD
    KR = ROWS + 3
    NG, GH = 4, 4
    tri = lambda k: k * (k + 1) // 2
    groups = lambda b, q4, g: b * 16 + q4 * 4 + g
    max_chunks = lambda b, q4, g: b * 640 + 64 * tri(q4) + g * (16 * (q4 + 1))
    key_steps = lambda b, q4, g: b * 160 + 16 * tri(q4) + g * (4 * (q4 + 1))
    blocks = lambda b, q4: b * 4 + q4

    with ExitStack() as ctx:
        sb = lambda n, s, d=F32: ctx.enter_context(nc.sbuf_tensor(n, s, d))
        sem = c.sem
        ps = lambda n, s: ctx.enter_context(nc.psum_tensor(n, s, F32))
        FF = sb("a0_FF", [P, 4, T])
        FFT = sb("a0_FFT", [P, T // P, CHUNK])
        kg = sb("a0_kg", [P, 2, GH, T], BF16)
        qg = sb("a0_qg", [P, 2, GH, CHUNK], BF16)
        vg = sb("a0_vg", [P, 2, T // P, GH, 2 * HD])
        part_max = sb("a0_part_max", [P, GH * 4, 4])
        neg_max = sb("a0_neg_max", [P, GH * 4])
        nm_rest = sb("a0_nm_rest", [P, GH * 4])
        nm_parts = sb("a0_nm_parts", [P, GH * 4, 3], BF16)
        trash = sb("a0_trash", [P, 2, CHUNK])
        probs = sb("a0_probs", [P, 2, GH, CHUNK])
        oT = sb("a0_oT", [P, CHUNK])
        recip = sb("a0_recip", [P, 4, GH])
        y = sb("a0_y", [P, 4, GH, HD])
        max_ps = ps("a0_max_ps", [P, 2, CHUNK])
        t_ps = ps("a0_t_ps", [P, 4, CHUNK])
        pv_ps = ps("a0_pv_ps", [P, CHUNK])
        tr_ps = ps("a0_tr_ps", [P, CHUNK])

        ff_loaded, fft_loaded = sem("ff_loaded"), sem("fft_loaded")
        ones_set = sem("ones_set")
        g_loaded = [sem(f"g_loaded{u}") for u in range(2)]
        max_ready, max_done, nm_steps, nm_ready, rows_ready, rows_done = (
            sem("max_ready"), sem("max_done"), sem("nm_steps"), sem("nm_ready"), sem("rows_ready"), sem("rows_done"))
        t_ready, t_added, exp_done, pv_done = sem("t_ready"), sem("t_added"), sem("exp_done"), sem("pv_done")
        o_copied, o_turned, y_steps, y_stored, y_free = sem("o_copied"), sem("o_turned"), sem("y_steps"), sem("y_stored"), sem("y_free")
        block = ctx.enter_context(nc.Block())

        @block.gpsimd
        def _(pool):
            pool.sem_inc(y_free, 1)
            with pool.Fori(0, NB) as b:
                for q4 in range(4):
                    bi = blocks(b, q4)
                    pool.wait_ge(y_steps, bi * 8 + 1)
                    hold(pool, c)
                    if q4:
                        pool.dma_start(FFT[:, 0:4 * q4, :], FFK[bass.ds(bi, 1), :, 0:4 * q4, :].rearrange("a p j q -> (a p) j q")).then_inc(fft_loaded, 16)
                    for t in range(4):
                        pool.dma_start(FFT[:, 4 * q4 + t, t * P:CHUNK], FFK[bass.ds(bi, 1), :, 4 * q4 + t, t * P:CHUNK].rearrange("a p q -> (a p) q")).then_inc(fft_loaded, 16)
                    with pool.Fori(0, NG) as g:
                        pool.wait_ge(y_steps, groups(b, q4, g) * 2 + 2 + 1)
                        pool.dma_start(Y0[bass.ds(b, 1), q4 * CHUNK:(q4 + 1) * CHUNK, bass.ds(g * GH * HD, GH * HD)].rearrange("a (t p) f -> (a p) t f", p=P),
                                       y[:].rearrange("p t h e -> p t (h e)")).then_inc(y_stored, 16)
                        pool.wait_ge(y_stored, (groups(b, q4, g) + 1) * 16)
                        pool.sem_inc(y_free, 1)
            pool.wait_ge(y_stored, NB * 16 * 16)

        @block.sync
        def _(sp):
            with sp.Fori(0, NB) as b:
                for q4 in range(4):
                    W = CHUNK * (q4 + 1)
                    bi = blocks(b, q4)
                    sp.wait_ge(nm_ready, bi * 4 + 1)
                    for t in range(4):
                        n_keys = (4 * q4 + t + 1) * P
                        sp.dma_start(FF[:, t, 0:n_keys], FFQ[bass.ds(bi, 1), :, t, 0:n_keys].rearrange("a p k -> (a p) k")).then_inc(ff_loaded, 16)
                    with sp.Fori(0, NG // 2) as g2:
                        for u in range(2):
                            g = g2 * 2 + u
                            h = b * NH + g * GH
                            sp.wait_ge(pv_done, groups(b, q4, g) + 1)
                            sp.dma_start(kg[0:ROWS, u, :, 0:W], KS0[bass.ds(h, GH), :, 0:W].rearrange("h r t -> r h t")).then_inc(g_loaded[u], 16)
                            sp.dma_start(qg[0:ROWS, u, :, :], QS0[bass.ds(h, GH), :, q4 * CHUNK:(q4 + 1) * CHUNK].rearrange("h r t -> r h t")).then_inc(g_loaded[u], 16)
                            sp.dma_start(vg[:, u, 0:4 * (q4 + 1)], V0[bass.ds(b, 1), :, 0:4 * (q4 + 1), bass.ds(g * GH, GH), :].rearrange("a p j h e -> (a p) j h e")).then_inc(g_loaded[u], 16)

        @block.scalar
        def _(act):
            act.sem_inc(o_copied, 1)
            with act.Fori(0, NB) as b:
                for q4 in range(4):
                    with act.Fori(0, NG // 2) as g2:
                        for u in range(2):
                            g = g2 * 2 + u
                            gi = groups(b, q4, g)
                            act.wait_ge(rows_ready, gi + 1)
                            act.activation(qg[ROWS:KR, u, :, :], t_ps[0:3, :, :], ACT.Copy).then_inc(rows_done, 1)
                            for J in range(4 * (q4 + 1)):
                                c0 = max(0, J - 4 * q4) * P
                                act.wait_ge(t_added, (key_steps(b, q4, g) + J) * 2 + 2)
                                act.activation(probs[:, J % 2, :, c0:CHUNK], probs[:, J % 2, :, c0:CHUNK], ACT.Exp).then_inc(exp_done, 1)
                            act.wait_ge(pv_done, gi + 3)
                            act.activation(oT[:], pv_ps[:], ACT.Copy).then_inc(o_copied, 1)

        @block.tensor
        def _(pe):
            pe.sem_inc(pv_done, 2)
            pe.wait_ge(ones_set, 1)
            with pe.Fori(0, NB) as b:
                for q4 in range(4):
                    nch, nj = q4 + 1, 4 * (q4 + 1)
                    with pe.Fori(0, NG // 2) as g2:
                        for u in range(2):
                            g = g2 * 2 + u
                            gi = groups(b, q4, g)
                            pe.wait_ge(g_loaded[u], (blocks(b, q4) * 2 + g2 + 1) * 48)
                            k = 0
                            for h in range(GH):
                                for t in range(4):
                                    n_keys = (4 * q4 + t + 1) * P
                                    for ch in range(nch):
                                        w = min(CHUNK, n_keys - ch * CHUNK)
                                        if k >= 2:
                                            pe.wait_ge(max_done, max_chunks(b, q4, g) + k - 1)
                                        pe.matmul(max_ps[:, k % 2, 0:w], qg[0:ROWS, u, h, t * P:(t + 1) * P],
                                                  kg[0:ROWS, u, h, ch * CHUNK:ch * CHUNK + w], start=True, stop=True).then_inc(max_ready, 1)
                                        k += 1
                            pe.wait_ge(nm_ready, gi + 1 + 1)
                            for h in range(GH):
                                for t in range(4):
                                    last = pe.matmul(t_ps[0:3, h, t * P:(t + 1) * P], nm_parts[:, h * 4 + t, :], c.ident_bf[:], start=True, stop=True)
                            last.then_inc(rows_ready, 1)
                            pe.wait_ge(rows_done, gi + 1)

                            def scores(J):
                                c0 = max(0, J - 4 * q4) * P
                                for h in range(GH):
                                    if h % 2 == 0 and J >= 1:
                                        pe.wait_ge(t_added, (key_steps(b, q4, g) + J - 1) * 2 + h // 2 + 1)
                                    m = pe.matmul(t_ps[:, h, c0:CHUNK], kg[0:KR, u, h, J * P:(J + 1) * P], qg[0:KR, u, h, c0:CHUNK],
                                                  start=True, stop=True)
                                    if h % 2 == 1:
                                        m.then_inc(t_ready, 1)

                            scores(0)
                            for J in range(nj):
                                c0 = max(0, J - 4 * q4) * P
                                if J + 1 < nj:
                                    scores(J + 1)
                                pe.wait_ge(exp_done, key_steps(b, q4, g) + J + 1)
                                if J == 0:
                                    pe.wait_ge(o_copied, gi + 1)
                                for h in range(GH):
                                    m = pe.matmul(pv_ps[32 * h:32 * h + 32, c0:CHUNK], vg[:, u, J, h, :], probs[:, J % 2, h, c0:CHUNK],
                                                  start=(J == 0), stop=(J == nj - 1), tile_position=(0, 32 * h))
                                if J == nj - 1:
                                    m.then_inc(pv_done, 1)
                            pe.wait_ge(o_copied, gi + 1 + 1)
                            pe.wait_ge(y_steps, gi * 2 + 1)
                            for t in range(4):
                                m = pe.transpose(tr_ps[:, t * P:(t + 1) * P], oT[:, t * P:(t + 1) * P], c.ident[:])
                            m.then_inc(o_turned, 1)

        @block.vector
        def _(dve):
            dve.sem_inc(y_steps, 1)
            dve.sem_inc(nm_ready, 1)
            dve.memset(kg[ROWS:P, :, :, :], 1.0).then_inc(ones_set, 1)
            with dve.Fori(0, NB) as b:
                for q4 in range(4):
                    nch, nj = q4 + 1, 4 * (q4 + 1)
                    bi = blocks(b, q4)
                    dve.wait_ge(ff_loaded, (bi + 1) * 64)
                    hold(dve, c)
                    with dve.Fori(0, NG // 2) as g2:
                        for u in range(2):
                            g = g2 * 2 + u
                            gi = groups(b, q4, g)
                            k = 0
                            for h in range(GH):
                                for t in range(4):
                                    for ch in range(nch):
                                        w = min(CHUNK, (4 * q4 + t + 1) * P - ch * CHUNK)
                                        dve.wait_ge(max_ready, max_chunks(b, q4, g) + k + 1)
                                        if k >= 2:
                                            dve.wait_ge(max_done, max_chunks(b, q4, g) + k - 1)
                                        hold(dve, c)
                                        dve.tensor_tensor_reduce(trash[:, k % 2, 0:w], max_ps[:, k % 2, 0:w], FF[:, t, ch * CHUNK:ch * CHUNK + w],
                                                                 1.0, -BIG, ALU.subtract, ALU.max,
                                                                 accum_out=part_max[:, h * 4 + t, ch:ch + 1]).then_inc(max_done, 1)
                                        k += 1
                            dve.wait_ge(max_done, max_chunks(b, q4, g) + k)
                            dve.tensor_reduce(neg_max[:], part_max[:, :, 0:nch], AX.X, ALU.max, negate=True).then_inc(nm_steps, 1)
                            dve.wait_ge(nm_steps, gi * 4 + 1)
                            dve.tensor_copy(nm_parts[:, :, 0], neg_max[:]).then_inc(nm_steps, 1)
                            dve.wait_ge(nm_steps, gi * 4 + 2)
                            dve.tensor_tensor(nm_rest[:], neg_max[:], nm_parts[:, :, 0], ALU.subtract).then_inc(nm_steps, 1)
                            dve.wait_ge(nm_steps, gi * 4 + 3)
                            dve.tensor_copy(nm_parts[:, :, 1], nm_rest[:]).then_inc(nm_steps, 1)
                            dve.wait_ge(nm_steps, gi * 4 + 4)
                            dve.tensor_tensor(nm_parts[:, :, 2], nm_rest[:], nm_parts[:, :, 1], ALU.subtract).then_inc(nm_ready, 1)
                            dve.wait_ge(fft_loaded, b * 19 * 16 + (4 * (q4 + 1) + q4) * 16)
                            for J in range(nj):
                                c0 = max(0, J - 4 * q4) * P
                                ks = key_steps(b, q4, g) + J
                                for half in range(2):
                                    dve.wait_ge(t_ready, ks * 2 + half + 1)
                                    dve.tensor_tensor(probs[:, J % 2, 2 * half:2 * half + 2, c0:CHUNK], t_ps[:, 2 * half:2 * half + 2, c0:CHUNK],
                                                      FFT[:, J:J + 1, c0:CHUNK].broadcast_to([P, 2, CHUNK - c0]), ALU.subtract).then_inc(t_added, 1)
                            dve.wait_ge(o_turned, gi + 1)
                            turned = tr_ps[:].rearrange("p (t h e) -> p t h e", t=4, h=GH)
                            dve.reciprocal(recip[:], turned[:, :, :, HD]).then_inc(y_steps, 1)
                            dve.wait_ge(y_steps, gi * 2 + 1 + 1)
                            dve.wait_ge(y_free, gi + 1)
                            dve.tensor_tensor(y[:], turned[:, :, :, 0:HD], recip[:].rearrange("p t (h a) -> p t h a", a=1).broadcast_to([P, 4, GH, HD]),
                                              ALU.mult).then_inc(y_steps, 1)


def project_out(nc, c, layer, Y, X, w, bias, w_is_transposed):
    D = 256
    with ExitStack() as ctx:
        sb = lambda n, s, d=F32: ctx.enter_context(nc.sbuf_tensor(f"{layer}_{n}", s, d))
        sem = lambda n: c.sem(f"{layer}_{n}")
        ps = lambda n, s: ctx.enter_context(nc.psum_tensor(f"{layer}_{n}", s, F32))
        w_in = sb("o_w_in", [P, 2, D])
        W = sb("o_W", [P, 2, D])
        bias_row = sb("o_bias", [P, D])
        y = sb("o_y", [P, 2, 4, D])
        yT = sb("o_yT", [P, 2, 2, CHUNK])
        t_ps = ps("o_t_ps", [P, 2, 2, CHUNK])
        o_ps = ps("o_o_ps", [P, 4, CHUNK])
        w_loaded, w_turned, w_ready, biased = sem("w_loaded"), sem("w_turned"), sem("w_ready"), sem("biased")
        y_loaded = [sem(f"y_loaded{u}") for u in range(2)]
        yT_ready, yT_done, o_ready, o_done = sem("yT_ready"), sem("yT_done"), sem("o_ready"), sem("o_done")
        Yf = Y.rearrange("b t f -> (b t) f")
        block = ctx.enter_context(nc.Block())

        @block.sync
        def _(sp):
            sp.dma_start(w_in[:], w.rearrange("(h p) n -> p h n", p=P)).then_inc(w_loaded, 16)
            sp.dma_start(bias_row[:], bias.rearrange("(a n) -> a n", a=1).broadcast_to([P, D])).then_inc(w_loaded, 16)
            with sp.Fori(0, 4) as it:
                for u in range(2):
                    ch = it * 2 + u
                    sp.wait_ge(yT_ready, ch + 1)
                    sp.dma_start(y[:, u], Yf[bass.ds(ch * CHUNK, CHUNK), :].rearrange("(t p) f -> p t f", p=P)).then_inc(y_loaded[u], 16)

        @block.gpsimd
        def _(pool):
            pool.wait_ge(w_loaded, 32)
            pool.tensor_tensor(X[:], X[:], bias_row[:].rearrange("p (a n) -> p a n", a=1).broadcast_to([P, 32, D]), ALU.add).then_inc(biased, 1)

        @block.scalar
        def _(act):
            act.sem_inc(yT_done, 1)
            act.wait_ge(w_turned, 1)
            if w_is_transposed:
                act.activation(W[:], o_ps[:, 0:2, 0:D], ACT.Copy).then_inc(w_ready, 1)
            else:
                act.activation(W[:], w_in[:], ACT.Copy).then_inc(w_ready, 1)
            with act.Fori(0, 4) as it:
                for u in range(2):
                    ch = it * 2 + u
                    act.wait_ge(yT_ready, ch + 3)
                    act.wait_ge(o_ready, ch + 1)
                    act.activation(yT[:, u], t_ps[:, u], ACT.Copy).then_inc(yT_done, 1)

        @block.tensor
        def _(pe):
            pe.sem_inc(o_ready, 1)
            pe.sem_inc(yT_ready, 2)
            pe.wait_ge(w_loaded, 32)
            for out_half in range(2):
                for in_half in range(2):
                    m = pe.transpose(o_ps[:, in_half, out_half * P:(out_half + 1) * P],
                                     w_in[:, out_half, in_half * P:(in_half + 1) * P], c.ident[:])
            m.then_inc(w_turned, 1)
            pe.wait_ge(w_ready, 1)
            with pe.Fori(0, 4) as it:
                for u in range(2):
                    ch = it * 2 + u
                    pe.wait_ge(y_loaded[u], it * 16 + 16)
                    pe.wait_ge(yT_done, ch + 1)
                    for half in range(2):
                        for t in range(4):
                            m = pe.transpose(t_ps[:, u, half, t * P:(t + 1) * P], y[:, u, t, half * P:(half + 1) * P], c.ident[:])
                    m.then_inc(yT_ready, 1)
                    pe.wait_ge(yT_done, ch + 1 + 1)
                    pe.wait_ge(o_done, ch + 1)
                    for t in range(4):
                        for half in range(2):
                            m = pe.matmul(o_ps[:, t, 0:D], yT[:, u, half, t * P:(t + 1) * P], W[:, half, :], start=(half == 0), stop=(half == 1))
                    m.then_inc(o_ready, 1)

        @block.vector
        def _(dve):
            dve.sem_inc(o_done, 1)
            dve.wait_ge(biased, 1)
            with dve.Fori(0, 8) as ch:
                dve.wait_ge(o_ready, ch + 1 + 1)
                dve.tensor_tensor(X[:, bass.ds(ch * 4, 4), :], o_ps[:, :, 0:D], X[:, bass.ds(ch * 4, 4), :], ALU.add).then_inc(o_done, 1)


def project_qkv1(nc, c, XT, W_qk, W_v, QA1, KA1, V1):
    NH, DQ, DV, D = 8, 64, 32, 256
    SCALE = DQ ** -0.5
    with ExitStack() as ctx:
        sb = lambda n, s, d=F32: ctx.enter_context(nc.sbuf_tensor(n, s, d))
        sem = c.sem
        ps = lambda n, s: ctx.enter_context(nc.psum_tensor(n, s, F32))
        wqk = sb("p1_wqk", [P, 2, 2 * NH * DQ])
        wv = sb("p1_wv", [P, 2, D])
        xt = sb("p1_xt", [P, 2, 2, CHUNK])
        full = sb("p1_full", [P, 8, CHUNK])
        v_sb = sb("p1_v", [P, 2, 4, D])
        proj_ps = ps("p1_proj", [P, 4, CHUNK])
        v_ps = ps("p1_v_ps", [P, 4, CHUNK])
        w_loaded = sem("w_loaded")
        xt_loaded = [sem(f"xt_loaded{u}") for u in range(2)]
        proj_ready, full_ready, v_ready, v_copied = sem("proj_ready"), sem("full_ready"), sem("v_ready"), sem("v_copied")
        full_stored = [sem(f"full_stored{m}") for m in range(8)]
        v_stored = [sem(f"v_stored{u}") for u in range(2)]
        block = ctx.enter_context(nc.Block())

        @block.gpsimd
        def _(pool):
            pool.dma_start(wqk[:], W_qk.rearrange("(h p) n -> p h n", p=P)).then_inc(w_loaded, 16)
            pool.dma_start(wv[:], W_v.rearrange("(h p) n -> p h n", p=P)).then_inc(w_loaded, 16)
            with pool.Fori(0, 4) as it:
                for u in range(2):
                    ch = it * 2 + u
                    pool.wait_ge(v_ready, ch + 1)
                    pool.dma_start(xt[:, u, :, :], XT[bass.ds(ch, 1), :, :, :].rearrange("a p h t -> (a p) h t")).then_inc(xt_loaded[u], 16)

        @block.sync
        def _(sp):
            with sp.Fori(0, 4) as it:
                for u in range(2):
                    ch = it * 2 + u
                    b, t0 = ch // 4, (ch % 4) * CHUNK
                    for m in range(8):
                        sp.wait_ge(full_ready, ch * 8 + m + 1 + 1)
                        dst = QA1 if m < 4 else KA1
                        sp.dma_start(dst[bass.ds(b * NH + 2 * (m % 4), 2), 0:DQ, bass.ds(t0, CHUNK)], full[:, m, :]).then_inc(full_stored[m], 16)
                    sp.wait_ge(v_copied, ch + 1 + 1)
                    sp.dma_start(V1[bass.ds(b, 1), :, bass.ds((ch % 4) * 4, 4), :, :].rearrange("a p j h e -> (a p) j (h e)"),
                                 v_sb[:, u]).then_inc(v_stored[u], 16)
            for m in range(8):
                sp.wait_ge(full_stored[m], (8 + 1) * 16)
            for u in range(2):
                sp.wait_ge(v_stored[u], (4 + 1) * 16)

        @block.scalar
        def _(act):
            act.sem_inc(full_ready, 1)
            for m in range(8):
                act.sem_inc(full_stored[m], 16)
            with act.Fori(0, 8) as ch:
                for m in range(8):
                    act.wait_ge(proj_ready, ch * 8 + m + 1)
                    act.wait_ge(full_stored[m], (ch + 1) * 16)
                    act.activation(full[:, m, :], proj_ps[:, m % 4, :], ACT.Copy, scale=SCALE if m < 4 else 1.0).then_inc(full_ready, 1)

        @block.vector
        def _(dve):
            dve.sem_inc(v_copied, 1)
            for u in range(2):
                dve.sem_inc(v_stored[u], 16)
            with dve.Fori(0, 4) as it:
                for u in range(2):
                    ch = it * 2 + u
                    dve.wait_ge(v_ready, ch + 3)
                    dve.wait_ge(v_stored[u], (it + 1) * 16)
                    dve.tensor_copy(v_sb[:, u], v_ps[:, :, 0:D]).then_inc(v_copied, 1)

        @block.tensor
        def _(pe):
            pe.wait_ge(w_loaded, 32)
            pe.sem_inc(v_ready, 2)
            with pe.Fori(0, 4) as it:
                for u in range(2):
                    ch = it * 2 + u
                    pe.wait_ge(xt_loaded[u], it * 16 + 16)
                    for m in range(8):
                        if m >= 4:
                            pe.wait_ge(full_ready, ch * 8 + m - 3 + 1)
                        elif m == 0:
                            pe.wait_ge(full_ready, ch * 8 + 1)
                        for half in range(2):
                            last = pe.matmul(proj_ps[:, m % 4, :], wqk[:, half, m * P:(m + 1) * P], xt[:, u, half, :],
                                             start=(half == 0), stop=(half == 1))
                        last.then_inc(proj_ready, 1)
                    pe.wait_ge(v_copied, ch + 1)
                    for t in range(4):
                        for half in range(2):
                            last = pe.matmul(v_ps[:, t, 0:D], xt[:, u, half, t * P:(t + 1) * P], wv[:, half, :],
                                             start=(half == 0), stop=(half == 1))
                    last.then_inc(v_ready, 1)


BAND = 9
BW = P + 2 * BAND


def bias_operands(nc, c, conv, QA1, KA1, EXT, BQ, BK):
    NH, NT, T, NREL = 8, 16, 2048, 21
    L = BW + P - 1
    FAR = (L - NREL) // 2
    with ExitStack() as ctx:
        sb = lambda n, s, d=F32: ctx.enter_context(nc.sbuf_tensor(n, s, d))
        sem = c.sem
        ext = sb("b_ext", [P, 2, NH, L])
        cb = sb("b_cb", [P, NH, NREL])
        band = sb("b_band", [P, 2, NH, BW])
        tile_of = sb("b_tile_of", [NT, T])
        before = sb("b_before", [NT, T])
        after = sb("b_after", [NT, T])
        base = sb("b_base", [NT, NH, T])
        loaded, ext_steps, ext_stored, band_loaded, band_done, filled, masks, base_half, base_done, stored = (
            sem("loaded"), sem("ext_steps"), sem("ext_stored"), sem("band_loaded"), sem("band_done"), sem("filled"),
            sem("masks"), sem("base_half"), sem("base_done"), sem("stored"))
        block = ctx.enter_context(nc.Block())

        @block.sync
        def _(sp):
            sp.dma_start(cb[:], conv.rearrange("(a h) r -> a h r", a=1).broadcast_to([P, NH, NREL])).then_inc(loaded, 16)
            sp.wait_ge(ext_steps, 3 + NREL)
            sp.dma_start(EXT, ext[:].rearrange("p s h l -> p (s h l)")).then_inc(ext_stored, 16)
            sp.wait_ge(ext_stored, 16)
            sp.dma_start(band[:].rearrange("p s h w -> p (s h) w"),
                         bass.AP(tensor=EXT.tensor, offset=EXT.offset + P - 1,
                                 ap=[[2 * NH * L - 1, P], [L, 2 * NH], [1, BW]])).then_inc(band_loaded, 16)
            sp.wait_ge(band_done, 4)
            sp.dma_start(BQ.rearrange("h p w -> p h w"), band[:, 0]).then_inc(stored, 16)
            sp.dma_start(BK.rearrange("h p w -> p h w"), band[:, 1]).then_inc(stored, 16)
            sp.wait_ge(masks, 4)
            for bh in range(2 * NH):
                sp.dma_start(QA1[bh, 64:64 + NT, :], tile_of[:]).then_inc(stored, 16)
            sp.wait_ge(base_done, NH)
            for b in range(2):
                sp.dma_start(KA1[b * NH:(b + 1) * NH, 64:64 + NT, :].rearrange("h r t -> r h t"), base[:]).then_inc(stored, 16)
            sp.wait_ge(stored, 20 * 16)

        @block.gpsimd
        def _(pool):
            pool.memset(tile_of[:], 1.0).then_inc(filled, 1)
            pool.memset(before[:], 1.0).then_inc(filled, 1)
            pool.memset(after[:], 1.0).then_inc(filled, 1)
            pool.wait_ge(filled, 3)
            pool.affine_select(out=before[:], in_=before[:], compare_op=ALU.is_gt, fill=0.0, base=0,
                               pattern=[[-1, T]], channel_multiplier=P).then_inc(masks, 1)
            pool.affine_select(out=after[:], in_=after[:], compare_op=ALU.is_ge, fill=0.0, base=-P,
                               pattern=[[1, T]], channel_multiplier=-P).then_inc(masks, 1)
            pool.wait_ge(masks, 2)
            pool.tensor_tensor(tile_of[:], tile_of[:], before[:], ALU.subtract).then_inc(masks, 1)
            pool.wait_ge(masks, 3)
            pool.tensor_tensor(tile_of[:], tile_of[:], after[:], ALU.subtract).then_inc(masks, 1)

        @block.vector
        def _(dve):
            dve.wait_ge(loaded, 16)
            wide = lambda r, n: cb[:, :, r:r + 1].broadcast_to([P, NH, n])
            dve.tensor_copy(ext[:, 0, :, 0:FAR], wide(0, FAR))
            dve.tensor_copy(ext[:, 0, :, FAR:FAR + NREL], cb[:]).then_inc(ext_steps, 1)
            dve.tensor_copy(ext[:, 0, :, FAR + NREL:L], wide(NREL - 1, FAR)).then_inc(ext_steps, 1)
            dve.tensor_copy(ext[:, 1, :, 0:FAR], wide(NREL - 1, FAR))
            dve.tensor_copy(ext[:, 1, :, FAR + NREL:L], wide(0, FAR)).then_inc(ext_steps, 1)
            for r in range(NREL):
                dve.tensor_copy(ext[:, 1, :, FAR + r:FAR + r + 1], cb[:, :, NREL - 1 - r:NREL - r]).then_inc(ext_steps, 1)
            dve.wait_ge(masks, 4)
            for h in range(NH):
                dve.tensor_scalar(base[:, h, :], before[:], cb[0:NT, h, 0:1], None, ALU.mult).then_inc(base_half, 1)
                dve.wait_ge(base_half, h + 1)
                dve.scalar_tensor_tensor(base[:, h, :], after[:], cb[0:NT, h, NREL - 1:NREL], base[:, h, :],
                                         ALU.mult, ALU.add).then_inc(base_done, 1)
            dve.wait_ge(band_loaded, 16)
            first, last = slice(0, BAND), slice(P + BAND, BW)
            for s, cols, r in ((0, first, 0), (0, last, NREL - 1), (1, first, NREL - 1), (1, last, 0)):
                dve.tensor_tensor(band[:, s, :, cols], band[:, s, :, cols], cb[:, :, r:r + 1].broadcast_to([P, NH, BAND]),
                                  ALU.subtract).then_inc(band_done, 1)


def relative_attention(nc, c, QA1, KA1, V1, BQ, BK, Y1):
    NB, T, NH, DQ, DV = 2, 2048, 8, 64, 32
    NT = T // P
    SR, ONE, KR = DQ + NT, 96, 97
    GH = 4
    NG = NH // GH
    NS = NG * 4
    NCH = T // CHUNK
    MC = 16 * NCH
    B2, R2 = 96, 112
    with ExitStack() as ctx:
        sb = lambda n, s, d=F32: ctx.enter_context(nc.sbuf_tensor(n, s, d))
        sem = c.sem
        ps = lambda n, s: ctx.enter_context(nc.psum_tensor(n, s, F32))
        kg = sb("a1_kg", [P, NG, GH, T])
        qg = sb("a1_qg", [P, 2, GH, CHUNK])
        ks = sb("a1_ks", [P, 2, GH, T], BF16)
        qs = sb("a1_qs", [P, 2, GH, CHUNK], BF16)
        vg = sb("a1_vg", [P, NG, NT, GH, DV])
        bq = sb("a1_bq", [P, GH, BW])
        bk = sb("a1_bk", [P, NG, GH, BW])
        part_max = sb("a1_part_max", [P, GH * 4, NCH])
        neg_max = sb("a1_neg_max", [P, GH * 4])
        nmT = sb("a1_nmT", [GH * 4, P])
        probs = sb("a1_probs", [P, 2, GH, CHUNK])
        total = sb("a1_total", [P, GH, CHUNK])
        oT = sb("a1_oT", [P, 2, CHUNK])
        recip = sb("a1_recip", [P, 4, GH])
        y = sb("a1_y", [P, 4, GH, DV])
        max_ps = ps("a1_max_ps", [P, 2, CHUNK])
        t_ps = ps("a1_t_ps", [P, 4, CHUNK])
        pv_ps = ps("a1_pv_ps", [P, 2, CHUNK])
        fixed_set, bq_loaded, max_ready, max_done, nm_ready, nm_turned, nm_copied, rows_loaded = (
            sem("fixed_set"), sem("bq_loaded"), sem("max_ready"), sem("max_done"), sem("nm_ready"), sem("nm_turned"),
            sem("nm_copied"), sem("rows_loaded"))
        q_loaded = [sem(f"q_loaded{u}") for u in range(2)]
        k_loaded = [sem(f"k_loaded{g}") for g in range(NG)]
        bkv_loaded = [sem(f"bkv_loaded{g}") for g in range(NG)]
        q_high, q_mid, k_high, k_mid = sem("q_high"), sem("q_mid"), sem("k_high"), sem("k_mid")
        t_ready, exp_done, added, pv_done, o_copied, o_turned, y_steps, y_stored = (
            sem("t_ready"), sem("exp_done"), sem("added"), sem("pv_done"), sem("o_copied"), sem("o_turned"), sem("y_steps"), sem("y_stored"))
        block = ctx.enter_context(nc.Block())

        def pieces(lo, hi, b0, b1):
            lo, hi = max(lo, b0), min(hi, b1)
            while lo < hi:
                end = min(hi, (lo // CHUNK + 1) * CHUNK)
                yield lo, end
                lo = end

        def max_slots(s, J):
            if s + 1 == NS:
                return range(0)
            first, each = (5, 8) if (s + 1) % 4 == 0 else (2, 6)
            k = max(0, J - first) * each
            return range(min(k, MC), min(k + each, MC) if J >= first else min(k, MC))

        @block.sync
        def _(sp):
            sp.sem_inc(y_stored, 16)
            sp.wait_ge(fixed_set, 5)
            with sp.Fori(0, NB) as b:
                def load_k(g):
                    h = b * NH + g * GH
                    sp.wait_ge(pv_done, b * NS + 4 * g + 4)
                    sp.dma_start(kg[0:SR, g], KA1[bass.ds(h, GH), :, :].rearrange("h r t -> r h t")).then_inc(k_loaded[g], 16)

                def load_bias_and_v(g):
                    sp.dma_start(bk[:, g], BK[g * GH:(g + 1) * GH, :, :].rearrange("h p w -> p h w")).then_inc(bkv_loaded[g], 16)
                    sp.dma_start(vg[:, g], V1[bass.ds(b, 1), :, :, g * GH:(g + 1) * GH, :].rearrange("a p j h e -> (a p) j h e")).then_inc(bkv_loaded[g], 16)

                def load_bq(g):
                    sp.wait_ge(nm_ready, b * NS + 4 * g + 1)
                    sp.dma_start(bq[:], BQ[g * GH:(g + 1) * GH, :, :].rearrange("h p w -> p h w")).then_inc(bq_loaded, 16)

                def load_q(s):
                    sp.dma_start(qg[0:SR, s % 2], QA1[bass.ds(b * NH + (s // 4) * GH, GH), :, (s % 4) * CHUNK:(s % 4 + 1) * CHUNK].rearrange("h r t -> r h t")).then_inc(q_loaded[s % 2], 16)

                def store_y(s):
                    sp.wait_ge(y_steps, (b * NS + s) * 2 + 2 + 1)
                    sp.dma_start(Y1[bass.ds(b, 1), (s % 4) * CHUNK:(s % 4 + 1) * CHUNK, (s // 4) * GH * DV:(s // 4 + 1) * GH * DV].rearrange("a (t p) f -> (a p) t f", p=P),
                                 y[:].rearrange("p t h e -> p t (h e)")).then_inc(y_stored, 16)

                load_k(0)
                load_q(0)
                load_bq(0)
                load_bias_and_v(0)
                for s in range(NS):
                    if s + 1 < NS:
                        sp.wait_ge(t_ready, (b * NS + s) * 2 * NT + 1)
                        load_q(s + 1)
                    if s == 0:
                        load_k(1)
                        load_bias_and_v(1)
                    if s == 3:
                        load_bq(1)
                    if s >= 1:
                        store_y(s - 1)
                store_y(NS - 1)
            sp.wait_ge(y_stored, (NB * NS + 1) * 16)

        @block.gpsimd
        def _(pool):
            pool.sem_inc(added, 2)
            with pool.Fori(0, NB) as b:
                for s in range(NS):
                    gi = b * NS + s
                    for J in range(NT):
                        pool.wait_ge(exp_done, (gi * NT + J) * 2 + 2)
                        if J == 0:
                            pool.wait_ge(pv_done, gi + NS)
                            hold(pool, c)
                            pool.tensor_copy(total[:], probs[:, J % 2]).then_inc(added, 1)
                        else:
                            pool.wait_ge(added, gi * NT + J + 2)
                            pool.tensor_tensor(total[:], total[:], probs[:, J % 2], ALU.add).then_inc(added, 1)

        @block.scalar
        def _(act):
            act.sem_inc(o_copied, 1)
            act.wait_ge(fixed_set, 5)
            with act.Fori(0, NB) as b:
                def q_parts(s, ops):
                    if 0 in ops:
                        act.wait_ge(q_loaded[s % 2], (b * (NS // 2) + s // 2 + 1) * 16)
                    steps = ((qs[0:DQ, 0], qg[0:DQ, s % 2]), (qs[0:DQ, 1], qg[0:DQ, s % 2]), (qs[DQ:SR, 1], qg[DQ:SR, s % 2]),
                             (qs[B2:R2, 1], qg[DQ:SR, s % 2]))
                    for i in ops:
                        act.activation(*steps[i], ACT.Copy).then_inc(q_high, 1)

                def k_parts(g, h):
                    if h == 0:
                        act.wait_ge(k_loaded[g], (b + 1) * 16)
                    act.activation(ks[0:DQ, 0, h], kg[0:DQ, g, h], ACT.Copy).then_inc(k_high, 1)
                    act.activation(ks[DQ:P, 0, h], kg[0:DQ, g, h], ACT.Copy).then_inc(k_high, 1)
                    act.activation(ks[DQ:SR, 1, h], kg[DQ:SR, g, h], ACT.Copy).then_inc(k_high, 1)

                def maxima_rows(s):
                    act.wait_ge(nm_turned, b * NS + s + 1)
                    act.activation(nmT[:], max_ps[0:GH * 4, 0, 0:P], ACT.Copy).then_inc(nm_copied, 1)
                    act.wait_ge(nm_copied, b * NS + s + 1)
                    act.dma_start(qg[ONE:KR, s % 2].rearrange("o h (t p) -> o (h t) p", p=P), nmT[:]).then_inc(rows_loaded, 16)

                q_parts(0, range(4))
                for h in range(GH):
                    k_parts(0, h)
                maxima_rows(0)
                for s in range(NS):
                    gi = b * NS + s
                    for J in range(NT):
                        for half in range(2):
                            hs = slice(2 * half, 2 * half + 2)
                            act.wait_ge(t_ready, (gi * NT + J) * 2 + half + 1 + 1)
                            act.wait_ge(added, gi * NT + J + 1)
                            act.activation(probs[:, J % 2, hs, :], t_ps[:, hs, :], ACT.Exp).then_inc(exp_done, 1)
                        if J == 0 and s > 0:
                            act.wait_ge(pv_done, gi + NS)
                            act.activation(oT[:], pv_ps[:], ACT.Copy).then_inc(o_copied, 1)
                        if s + 1 < NS:
                            if J < 2:
                                q_parts(s + 1, range(2 * J, 2 * J + 2))
                            if s == 3 and J >= 2 and J % 2 == 0 and J < 2 + 2 * GH:
                                k_parts(1, (J - 2) // 2)
                            if J == NT - 2:
                                maxima_rows(s + 1)
                act.wait_ge(pv_done, b * NS + 2 * NS)
                act.activation(oT[:], pv_ps[:], ACT.Copy).then_inc(o_copied, 1)

        @block.tensor
        def _(pe):
            pe.sem_inc(pv_done, NS)
            pe.sem_inc(t_ready, 1)
            pe.wait_ge(fixed_set, 5)
            with pe.Fori(0, NB) as b:
                def max_chunk(s, k):
                    gi, g, q4 = b * NS + s, s // 4, s % 4
                    h, t, ch = k // (4 * NCH), k // NCH % 4, k % NCH
                    if k == 0:
                        pe.wait_ge(q_high, (gi + 1) * 4)
                        pe.wait_ge(q_mid, gi + 1)
                        pe.wait_ge(bq_loaded, (b * NG + g + 1) * 16)
                        pe.wait_ge(y_steps, b * NS * 2 + 2 * max(0, s - 1) + 1)
                    if k % MC % (4 * NCH) == 0 and q4 == 0:
                        pe.wait_ge(k_high, (b * NG + g) * 3 * GH + 3 * h + 3)
                        pe.wait_ge(k_mid, (b * NG + g) * 2 * GH + 2 * h + 2)
                    if k >= 2:
                        pe.wait_ge(max_done, gi * MC + k - 1)
                    i0 = (4 * q4 + t) * P
                    near = [x for x in pieces(i0 - BAND, i0 + P + BAND, 0, T) if x[0] // CHUNK == ch]
                    keys = slice(ch * CHUNK, (ch + 1) * CHUNK)
                    pe.matmul(max_ps[:, k % 2, :], qs[:, 0, h, t * P:(t + 1) * P], ks[:, 0, h, keys], start=True, stop=False)
                    m = pe.matmul(max_ps[:, k % 2, :], qs[0:R2, 1, h, t * P:(t + 1) * P], ks[0:R2, 1, h, keys], start=False, stop=not near)
                    for lo, hi in near:
                        off = i0 - BAND
                        m = pe.matmul(max_ps[:, k % 2, lo - ch * CHUNK:hi - ch * CHUNK], c.ident[:], bq[:, h, lo - off:hi - off],
                                      start=False, stop=True)
                    m.then_inc(max_ready, 1)

                def turn_maxima(s):
                    pe.wait_ge(nm_ready, b * NS + s + 1 + 1)
                    pe.transpose(max_ps[0:GH * 4, 0, 0:P], neg_max[:], c.ident[:]).then_inc(nm_turned, 1)

                def scores(s, J, slots=()):
                    slots = list(slots)
                    gi, g, q4, u = b * NS + s, s // 4, s % 4, s % 2
                    near = list(pieces(J * P - BAND, J * P + P + BAND, q4 * CHUNK, (q4 + 1) * CHUNK))
                    for h in range(GH):
                        if h % 2 == 0 and (J or s):
                            pe.wait_ge(exp_done, (gi * NT + J - 1) * 2 + h // 2 + 1)
                        m = pe.matmul(t_ps[:, h, :], kg[0:KR, g, h, J * P:(J + 1) * P], qg[0:KR, u, h, :], start=True, stop=not near)
                        for lo, hi in near:
                            off, q0 = J * P - BAND, q4 * CHUNK
                            m = pe.matmul(t_ps[:, h, lo - q0:hi - q0], c.ident[:], bk[:, g, h, lo - off:hi - off], start=False, stop=True)
                        if h % 2 == 1:
                            m.then_inc(t_ready, 1)
                        if slots:
                            max_chunk(s + 1, slots.pop(0))
                    return slots

                def sums(s):
                    pe.wait_ge(added, (b * NS + s) * NT + NT + 2)
                    for h in range(GH):
                        m = pe.matmul(pv_ps[32 * h:32 * h + 32, 1, :], c.ones[:, 0:32], total[:, h, :], start=True, stop=True,
                                      tile_position=(0, 32 * h))
                    m.then_inc(pv_done, 1)

                def turn_outputs(s):
                    pe.wait_ge(o_copied, b * NS + s + 1 + 1)
                    pe.wait_ge(y_steps, (b * NS + s) * 2 + 1)
                    for half in range(2):
                        for t in range(4):
                            m = pe.transpose(max_ps[:, half, t * P:(t + 1) * P], oT[:, half, t * P:(t + 1) * P], c.ident[:])
                    m.then_inc(o_turned, 1)

                for k in range(MC):
                    max_chunk(0, k)
                turn_maxima(0)
                for s in range(NS):
                    gi, g = b * NS + s, s // 4
                    if s % 4 == 0:
                        pe.wait_ge(k_loaded[g], (b + 1) * 16)
                        pe.wait_ge(bkv_loaded[g], (b + 1) * 32)
                    pe.wait_ge(q_loaded[s % 2], (b * (NS // 2) + s // 2 + 1) * 16)
                    pe.wait_ge(rows_loaded, (gi + 1) * 16)
                    scores(s, 0)
                    if s > 0:
                        sums(s - 1)
                    for J in range(NT):
                        slots = max_slots(s, J)
                        if J + 1 < NT:
                            slots = scores(s, J + 1, slots)
                        if J == 0 and s > 0:
                            turn_outputs(s - 1)
                        pe.wait_ge(exp_done, (gi * NT + J) * 2 + 2)
                        for h in range(GH):
                            pe.matmul(pv_ps[32 * h:32 * h + 32, 0, :], vg[:, g, J, h, :], probs[:, J % 2, h, :], start=(J == 0), stop=(J == NT - 1),
                                      tile_position=(0, 32 * h))
                        for k in slots:
                            max_chunk(s + 1, k)
                        if J == NT - 2 and s + 1 < NS:
                            turn_maxima(s + 1)
                sums(NS - 1)
                turn_outputs(NS - 1)

        @block.vector
        def _(dve):
            dve.sem_inc(y_steps, 1)
            dve.sem_inc(nm_ready, 1)
            dve.memset(kg[64:96], 0.0).then_inc(fixed_set, 1)
            dve.memset(qg[64:96], 0.0).then_inc(fixed_set, 1)
            dve.memset(kg[96:97], 1.0).then_inc(fixed_set, 1)
            dve.memset(ks[64:P, 1], 0.0).then_inc(fixed_set, 1)
            dve.memset(qs[64:P, 1], 0.0).then_inc(fixed_set, 1)
            with dve.Fori(0, NB) as b:
                def q_rest(s):
                    dve.wait_ge(q_high, (b * NS + s) * 4 + 1)
                    dve.tensor_tensor(qs[DQ:P, 0], qg[0:DQ, s % 2], qs[0:DQ, 0], ALU.subtract).then_inc(q_mid, 1)

                def k_rest(g, h):
                    dve.wait_ge(k_high, (b * NG + g) * 3 * GH + 3 * h + 3)
                    dve.tensor_tensor(ks[0:DQ, 1, h], kg[0:DQ, g, h], ks[0:DQ, 0, h], ALU.subtract).then_inc(k_mid, 1)
                    dve.tensor_tensor(ks[B2:R2, 1, h], kg[DQ:SR, g, h], ks[DQ:SR, 1, h], ALU.subtract).then_inc(k_mid, 1)

                def maxima(s):
                    gi, g = b * NS + s, s // 4
                    if s % 4 == 0:
                        k_rest(g, 0)
                    for k in range(MC):
                        h, t, ch = k // (4 * NCH), k // NCH % 4, k % NCH
                        if s % 4 == 0 and k % (4 * NCH) == 2 * NCH and h + 1 < GH:
                            k_rest(g, h + 1)
                        dve.wait_ge(max_ready, gi * MC + k + 1)
                        dve.tensor_reduce(part_max[:, h * 4 + t, ch:ch + 1], max_ps[:, k % 2, :], AX.X, ALU.max).then_inc(max_done, 1)
                    dve.wait_ge(max_done, (gi + 1) * MC)
                    dve.tensor_reduce(neg_max[:], part_max[:], AX.X, ALU.max, negate=True).then_inc(nm_ready, 1)

                def outputs(s):
                    gi = b * NS + s
                    dve.wait_ge(o_turned, gi + 1)
                    turned = lambda half: max_ps[:, half, :].rearrange("p (t h e) -> p t h e", t=4, h=GH)
                    dve.reciprocal(recip[:], turned(1)[:, :, :, 0]).then_inc(y_steps, 1)
                    dve.wait_ge(y_steps, gi * 2 + 1 + 1)
                    dve.wait_ge(y_stored, (gi + 1) * 16)
                    dve.tensor_tensor(y[:], turned(0), recip[:].rearrange("p t (h a) -> p t h a", a=1).broadcast_to([P, 4, GH, DV]),
                                      ALU.mult).then_inc(y_steps, 1)

                q_rest(0)
                maxima(0)
                for s in range(NS):
                    if s > 0:
                        outputs(s - 1)
                    if s + 1 < NS:
                        q_rest(s + 1)
                        maxima(s + 1)
                outputs(NS - 1)


def lowrank_ffn(nc, c, XT, X, U1, V1w, b1, U2, V2, b2):
    D, R, F = 256, 64, 1024
    NF = F // P
    with ExitStack() as ctx:
        sb = lambda n, s, d=F32: ctx.enter_context(nc.sbuf_tensor(n, s, d))
        sem = c.sem
        ps = lambda n, s: ctx.enter_context(nc.psum_tensor(n, s, F32))
        u1 = sb("f_u1", [P, 2, R])
        v1 = sb("f_v1", [R, F])
        u2 = sb("f_u2", [P, NF, R])
        v2 = sb("f_v2", [R, D])
        b1_sb = sb("f_b1", [P, NF])
        b2_row = sb("f_b2", [P, D])
        xt = sb("f_xt", [P, 2, 2, CHUNK])
        pT = sb("f_pT", [R, CHUNK])
        hid = sb("f_hid", [P, 2, CHUNK])
        qT = sb("f_qT", [R, CHUNK])
        p_ps = ps("f_p_ps", [P, CHUNK])
        h_ps = ps("f_h_ps", [P, 2, CHUNK])
        q_ps = ps("f_q_ps", [P, CHUNK])
        o_ps = ps("f_o_ps", [P, 4, CHUNK])
        w_loaded, biased, p_ready, p_done, h_ready, h_done, q_ready, q_done, o_ready, o_done = map(sem, (
            "w_loaded", "biased", "p_ready", "p_done", "h_ready", "h_done", "q_ready", "q_done", "o_ready", "o_done"))
        xt_loaded = [sem(f"xt_loaded{u}") for u in range(2)]
        block = ctx.enter_context(nc.Block())

        @block.sync
        def _(sp):
            sp.dma_start(u1[:], U1.rearrange("(h p) r -> p h r", p=P)).then_inc(w_loaded, 16)
            sp.dma_start(v1[:], V1w).then_inc(w_loaded, 16)
            sp.dma_start(u2[:], U2.rearrange("(n p) r -> p n r", p=P)).then_inc(w_loaded, 16)
            sp.dma_start(v2[:], V2).then_inc(w_loaded, 16)
            sp.dma_start(b1_sb[:], b1.rearrange("(n p) -> p n", p=P), allow_slow_non_contiguous=True).then_inc(w_loaded, 16)
            sp.dma_start(b2_row[:], b2.rearrange("(a n) -> a n", a=1).broadcast_to([P, D])).then_inc(w_loaded, 16)
            with sp.Fori(0, 4) as it:
                for u in range(2):
                    ch = it * 2 + u
                    sp.wait_ge(p_ready, ch + 1)
                    sp.dma_start(xt[:, u, :, :], XT[bass.ds(ch, 1), :, :, :].rearrange("a p h t -> (a p) h t")).then_inc(xt_loaded[u], 16)

        @block.gpsimd
        def _(pool):
            pool.wait_ge(w_loaded, 96)
            pool.tensor_tensor(X[:], X[:], b2_row[:].rearrange("p (a n) -> p a n", a=1).broadcast_to([P, 32, D]), ALU.add).then_inc(biased, 1)

        @block.scalar
        def _(act):
            act.wait_ge(w_loaded, 96)
            with act.Fori(0, 8) as ch:
                act.wait_ge(p_ready, ch + 3)
                act.activation(pT[:], p_ps[0:R, :], ACT.Copy).then_inc(p_done, 1)
                for f in range(NF):
                    act.wait_ge(h_ready, ch * NF + f + 1)
                    act.activation(hid[:, f % 2, :], h_ps[:, f % 2, :], ACT.Gelu_apprx_tanh, bias=b1_sb[:, f:f + 1]).then_inc(h_done, 1)
                act.wait_ge(q_ready, ch + 1)
                act.activation(qT[:], q_ps[0:R, :], ACT.Copy).then_inc(q_done, 1)

        @block.tensor
        def _(pe):
            pe.wait_ge(w_loaded, 96)
            pe.sem_inc(p_ready, 2)
            with pe.Fori(0, 4) as it:
                for u in range(2):
                    ch = it * 2 + u
                    pe.wait_ge(xt_loaded[u], it * 16 + 16)
                    for half in range(2):
                        m = pe.matmul(p_ps[0:R, :], u1[:, half, :], xt[:, u, half, :], start=(half == 0), stop=(half == 1))
                    m.then_inc(p_ready, 1)
                    pe.wait_ge(p_done, ch + 1)

                    def hidden(f):
                        pe.matmul(h_ps[:, f % 2, :], v1[:, f * P:(f + 1) * P], pT[:], start=True, stop=True).then_inc(h_ready, 1)

                    hidden(0)
                    for f in range(NF):
                        if f + 1 < NF:
                            hidden(f + 1)
                        pe.wait_ge(h_done, ch * NF + f + 1)
                        m = pe.matmul(q_ps[0:R, :], u2[:, f, :], hid[:, f % 2, :], start=(f == 0), stop=(f == NF - 1))
                    m.then_inc(q_ready, 1)
                    pe.wait_ge(q_done, ch + 1)
                    pe.wait_ge(o_done, ch + 1)
                    for t in range(4):
                        m = pe.matmul(o_ps[:, t, 0:D], qT[:, t * P:(t + 1) * P], v2[:], start=True, stop=True)
                    m.then_inc(o_ready, 1)

        @block.vector
        def _(dve):
            dve.sem_inc(o_done, 1)
            dve.wait_ge(biased, 1)
            with dve.Fori(0, 8) as ch:
                dve.wait_ge(o_ready, ch + 1)
                dve.tensor_tensor(X[:, bass.ds(ch * 4, 4), :], o_ps[:, :, 0:D], X[:, bass.ds(ch * 4, 4), :], ALU.add).then_inc(o_done, 1)


def build(nc, x, w_attn, b_attn, w_proj, b_proj, w_red, wg, w1, b1, w2, b2,
          W_qk, W_v, W_out, b_out, conv, U1, V1w, fb1, U2, V2, fb2, out):
    scratch = lambda n, s, d=F32: nc.dram_tensor(n, s, d, kind="Internal").ap()
    XT = scratch("XT", (8, P, 2, CHUNK))
    QS0 = scratch("QS0", (32, 96, 2048), BF16)
    KS0 = scratch("KS0", (32, 96, 2048), BF16)
    V0 = scratch("V0", (2, P, 16, 16, 32))
    FFQ = scratch("FFQ", (8, P, 4, 2048))
    FFK = scratch("FFK", (8, P, 16, CHUNK))
    Y0 = scratch("Y0", (2, 2048, 256))
    XT1 = scratch("XT1", (8, P, 2, CHUNK))
    QA1 = scratch("QA1", (16, 80, 2048))
    KA1 = scratch("KA1", (16, 80, 2048))
    V1 = scratch("V1", (2, P, 16, 8, 32))
    Y1 = scratch("Y1", (2, 2048, 256))
    EXT = scratch("EXT", (P, 16 * (BW + P - 1)))
    BQ = scratch("BQ", (8, P, BW))
    BK = scratch("BK", (8, P, BW))
    tokens = lambda a: a.rearrange("b (n p) d -> p (b n) d", p=P)
    with ExitStack() as ctx:
        sb = lambda n, s, d=F32: ctx.enter_context(nc.sbuf_tensor(n, s, d))

        class c:
            ident = sb("ident", [P, P])
            ident_bf = sb("ident_bf", [P, P], BF16)
            before = sb("before", [P, P])
            ones = sb("ones", [P, P])

        taken = []
        c.stage = 0

        def sem(name):
            taken.append(nc.alloc_semaphore(name=f"s{c.stage}_{name}"))
            return taken[-1]

        c.sem = sem
        c.passed = ctx.enter_context(nc.semaphore("passed"))
        X = sb("X", [P, 32, 256])
        x_moved = ctx.enter_context(nc.semaphore("x_moved"))
        build_constants(nc, c)
        with nc.Block() as block:
            @block.sync
            def _(sp):
                sp.dma_start(X[:], tokens(x)).then_inc(x_moved, 16)
                sp.wait_ge(x_moved, 16)
        stages = (
            (layernorm_transpose, "l0", X, XT),
            (project_qkv0, XT, w_attn, b_attn, QS0, KS0, V0),
            (experts_and_penalties, XT, X, w_red, wg, w1, b1, w2, b2, QS0, KS0, FFQ, FFK),
            (selective_attention, QS0, KS0, V0, FFQ, FFK, Y0),
            (project_out, "l0", Y0, X, w_proj, b_proj, True),
            (layernorm_transpose, "l1", X, XT1),
            (project_qkv1, XT1, W_qk, W_v, QA1, KA1, V1),
            (bias_operands, conv, QA1, KA1, EXT, BQ, BK),
            (lowrank_ffn, XT1, X, U1, V1w, fb1, U2, V2, fb2),
            (relative_attention, QA1, KA1, V1, BQ, BK, Y1),
            (project_out, "l1", Y1, X, W_out, b_out, False),
        )
        for c.stage, (stage, *operands) in enumerate(stages):
            stage(nc, c, *operands)
            nc.clear_and_free_semaphores(taken)
            taken.clear()
            nc.all_engine_barrier()
        with nc.Block() as block:
            @block.sync
            def _(sp):
                sp.dma_start(tokens(out), X[:]).then_inc(x_moved, 16)
                sp.wait_ge(x_moved, 32)


_INS = ['L0_attn_x', 'L0_attn_w_attn', 'L0_attn_b_attn', 'L0_attn_w_proj', 'L0_attn_b_proj', 'L0_ffn_w_red', 'L0_ffn_wg',
        'L0_ffn_w1', 'L0_ffn_b1', 'L0_ffn_w2', 'L0_ffn_b2', 'L1_attn_W_qk', 'L1_attn_W_v', 'L1_attn_W_out', 'L1_attn_b_out',
        'L1_attn_conv', 'L1_ffn_U1', 'L1_ffn_V1', 'L1_ffn_b1', 'L1_ffn_U2', 'L1_ffn_V2', 'L1_ffn_b2']


def kernel(**inputs):
    import numpy as np
    import concourse.bacc as bacc
    from concourse.bass_utils import run_bass_kernel_spmd

    nc = bacc.Bacc("TRN2", target_bir_lowering=False, num_devices=1)
    arrays, args = {}, []
    for name in _INS:
        a = np.ascontiguousarray(inputs[name])
        arrays[f"in_{name}_dram"] = a
        args.append(nc.dram_tensor(f"in_{name}_dram", a.shape, mybir.dt.from_np(a.dtype), kind="ExternalInput").ap())
    out = nc.dram_tensor("out_dram", (2, 2048, 256), F32, kind="ExternalOutput").ap()
    build(nc, *args, out)
    r = run_bass_kernel_spmd(nc, [arrays], core_ids=[0])
    return r.results[0]["out_dram"]
```
